# Optimizing a Trainium2 kernel written in Bass

```python
import numpy as np
import jax
import jax.numpy as jnp

def _softmax(x, axis=-1):
    return jax.nn.softmax(x, axis=axis)

def _gelu(x):
    return jax.nn.gelu(x, approximate=True)

def _silu(x):
    return jax.nn.silu(x)

def _sigmoid(x):
    return jax.nn.sigmoid(x)

def _layernorm(x, axis=-1, eps=1e-05):
    m = jnp.mean(x, axis=axis, keepdims=True)
    v = jnp.var(x, axis=axis, keepdims=True)
    return (x - m) / jnp.sqrt(v + eps)

def _scatter_add(tgt, idx, src, axis=0):
    return tgt.at[idx].add(src)

def _segment_sum(src, seg, n):
    return jax.ops.segment_sum(src, seg, n)
kernel_name = 'mk_xattn_ffn_d4_seqx_r8_a5e7b9'

def setup_inputs(seed: int=0):
    np.random.seed(seed)
    _w = jnp.asarray

    def _rec_inputs():
        import jax
        import jax.numpy as jnp
        _rk = jax.random.key(seed)
        x = -7.109e-05 + 0.9999 * jax.random.normal(jax.random.fold_in(_rk, 1), (4, 256, 256), jnp.float32)
        _lenS = 256 - jax.random.randint(jax.random.fold_in(_rk, 7), (4,), 0, max(1, 256 // 4) + 1, jnp.int32)
        _lenS2 = 256 - jax.random.randint(jax.random.fold_in(_rk, 8), (4,), 0, max(1, 256 // 4) + 1, jnp.int32)
        _ctx_512P = jax.random.normal(jax.random.fold_in(_rk, 11), (4, 16, 64), jnp.float32)
        _ctx_512c = jax.random.dirichlet(jax.random.fold_in(_rk, 511), 0.3 * jnp.ones((16,), jnp.float32), (4, 256))
        _ctx_512t = jnp.einsum('bsk,bkd->bsd', _ctx_512c, _ctx_512P)
        _ctx_512t = _ctx_512t * jax.lax.rsqrt(jnp.mean(jnp.square(_ctx_512t)) + 1e-12) * 0.953939
        ctx_512 = 2.81802e-05 + 1.00001 * (_ctx_512t + 0.3 * jax.random.normal(jax.random.fold_in(_rk, 611), (4, 256, 64), jnp.float32))
        return (x, ctx_512)
    x, ctx_512 = _rec_inputs()

    def _L0_xattn_setup():
        import jax, jax.numpy as jnp
        import numpy as np
        EPS = 1e-06
        IMAGE_DIMS = 256
        key = jax.random.key(seed)
        k1, k2, k3 = jax.random.split(key, 3)
        B, I, J, D = (16, 256, 256, 64)
        p = jax.random.normal(k1, (B, I, J), dtype=jnp.float32)
        k_v = jax.random.normal(k2, (B, J, D), dtype=jnp.float32)
        W_k = jax.random.normal(k3, (D, D), dtype=jnp.float32) * (1.0 / np.sqrt(D))
        b_k = jnp.zeros((D,), dtype=jnp.float32)
        ln_gamma = jnp.ones((J,), dtype=jnp.float32)
        ln_beta = jnp.zeros((J,), dtype=jnp.float32)
        return {'p': p, 'k_v': k_v, 'W_k': W_k, 'b_k': b_k, 'ln_gamma': ln_gamma, 'ln_beta': ln_beta}
    _L0_xattn_all = _L0_xattn_setup()
    _L0_xattn_in = {k: v for k, v in _L0_xattn_all.items() if k in ('W_k', 'b_k', 'ln_gamma', 'ln_beta')}
    del _L0_xattn_all

    def _L0_ffn_setup():
        import jax, jax.numpy as jnp
        import numpy as np
        TOP_K = 4
        NORM_TOPK_PROB = False
        key = jax.random.key(seed)
        B, S, D, E, F, FS = (4, 64, 256, 16, 176, 704)
        ks = jax.random.split(key, 9)
        w = lambda k, shape: jax.random.normal(k, shape, jnp.float32) * 0.02
        return {'hidden_states': jax.random.normal(ks[0], (B, S, D), jnp.float32), 'router_weight': w(ks[1], (E, D)), 'w_gate': w(ks[2], (E, F, D)), 'w_up': w(ks[3], (E, F, D)), 'w_down': w(ks[4], (E, D, F)), 'ws_gate': w(ks[5], (FS, D)), 'ws_up': w(ks[6], (FS, D)), 'ws_down': w(ks[7], (D, FS)), 'w_shared_gate': w(ks[8], (1, D))}
    _L0_ffn_all = _L0_ffn_setup()
    _L0_ffn_in = {k: v for k, v in _L0_ffn_all.items() if k in ('router_weight', 'w_gate', 'w_up', 'w_down', 'ws_gate', 'ws_up', 'ws_down', 'w_shared_gate')}
    del _L0_ffn_all

    def _L1_xattn_setup():
        import jax, jax.numpy as jnp
        import numpy as np
        B, S, L = (2, 128, 128)
        DIM_Q, H, K, D_C, D_CQ, R = (256, 16, 128, 64, 192, 64)

        def _rope_tables(length, dim):
            inv = 1.0 / 10000.0 ** (jnp.arange(0, dim, 2, dtype=jnp.float32) / dim)
            f = jnp.arange(length, dtype=jnp.float32)[:, None] * inv[None, :]
            sin = jnp.repeat(jnp.sin(f), 2, axis=-1)
            cos = jnp.repeat(jnp.cos(f), 2, axis=-1)
            return (sin, cos)

        def _rotate_half(x):
            half = x.shape[-1] // 2
            return jnp.concatenate([-x[..., half:], x[..., :half]], axis=-1)

        def _apply_rope(x, sin, cos):
            return x * cos + _rotate_half(x) * sin
        key = jax.random.key(seed)
        ks = jax.random.split(key, 8)
        return {'hidden_q': jax.random.normal(ks[0], (B, S, DIM_Q), jnp.float32), 'kv_c': jax.random.normal(ks[1], (B, L, D_C), jnp.float32), 'Wq': jax.random.normal(ks[2], (H * K, DIM_Q), jnp.float32) / np.sqrt(DIM_Q).astype(np.float32), 'w_kc_q': jax.random.normal(ks[3], (H, K, D_CQ), jnp.float32) / np.sqrt(K).astype(np.float32), 'w_kc_kv': jax.random.normal(ks[4], (H, K, D_C), jnp.float32) / np.sqrt(K).astype(np.float32), 'W_qr': jax.random.normal(ks[5], (H, D_CQ, R), jnp.float32) / np.float32(np.sqrt(D_CQ) * np.sqrt(R)), 'W_kr': jax.random.normal(ks[6], (H, D_C, R), jnp.float32) / np.sqrt(D_C).astype(np.float32), 'Wo': jax.random.normal(ks[7], (DIM_Q, H * K), jnp.float32) / np.sqrt(H * K).astype(np.float32)}
    _L1_xattn_all = _L1_xattn_setup()
    _L1_xattn_in = {k: v for k, v in _L1_xattn_all.items() if k in ('Wq', 'w_kc_q', 'w_kc_kv', 'W_qr', 'W_kr', 'Wo')}
    del _L1_xattn_all

    def _L1_ffn_setup():
        import jax, jax.numpy as jnp
        import numpy as np
        EPS = 1e-05

        def _quant_weight(w):
            scale = jnp.mean(jnp.abs(w)) + EPS
            wq = jnp.clip(jnp.round(w / scale), -1.0, 1.0)
            return (wq, scale)

        def _quant_act(x):
            s = jnp.max(jnp.abs(x), axis=-1, keepdims=True) / 127.0 + EPS
            xq = jnp.clip(jnp.round(x / s), -128.0, 127.0)
            return (xq, s)

        def _qlinear(x, w):
            wq, ws = _quant_weight(w)
            xq, xs = _quant_act(x)
            y = jnp.einsum('bsi,oi->bso', xq, wq)
            return y * xs * ws
        key = jax.random.key(seed)
        k1, k2, k3, k4 = jax.random.split(key, 4)
        H, I = (256, 1024)
        x = jax.random.normal(k1, (4, 512, H), dtype=jnp.float32)
        w_gate = jax.random.normal(k2, (I, H), dtype=jnp.float32) * (1.0 / np.sqrt(H))
        w_up = jax.random.normal(k3, (I, H), dtype=jnp.float32) * (1.0 / np.sqrt(H))
        w_down = jax.random.normal(k4, (H, I), dtype=jnp.float32) * (1.0 / np.sqrt(I))
        return {'x': x, 'w_gate': w_gate, 'w_up': w_up, 'w_down': w_down}
    _L1_ffn_all = _L1_ffn_setup()
    _L1_ffn_in = {k: v for k, v in _L1_ffn_all.items() if k in ('w_gate', 'w_up', 'w_down')}
    del _L1_ffn_all

    def _L2_xattn_setup():
        import jax, jax.numpy as jnp
        import numpy as np
        B, N, D = (16, 256, 64)
        H = 4
        TOP_K_RATIO = 0.3
        key = jax.random.key(seed)
        k1, k2, k3, k4 = jax.random.split(key, 4)
        h = jax.random.normal(k1, (B, N, D), dtype=jnp.float32)
        adj_raw = jax.random.uniform(k2, (B, N, N), dtype=jnp.float32)
        lim = 1.0 / np.sqrt(D)
        Wq = jax.random.uniform(k3, (D, D), minval=-lim, maxval=lim, dtype=jnp.float32)
        Wk = jax.random.uniform(k4, (D, D), minval=-lim, maxval=lim, dtype=jnp.float32)
        gamma_raw = jnp.float32(-0.85)
        return {'h': h, 'adj_raw': adj_raw, 'Wq': Wq, 'Wk': Wk, 'gamma_raw': gamma_raw}
    _L2_xattn_all = _L2_xattn_setup()
    _L2_xattn_in = {k: v for k, v in _L2_xattn_all.items() if k in ('Wq', 'Wk', 'gamma_raw')}
    del _L2_xattn_all

    def _L2_ffn_setup():
        import jax, jax.numpy as jnp
        import numpy as np
        H = 256
        E = 8
        K = 2
        I = 16
        key = jax.random.key(seed)
        k1, k2, k3, k4 = jax.random.split(key, 4)
        B, T = (2, 512)
        x = jax.random.normal(k1, (B, T, H), dtype=jnp.float32)
        router_w = jax.random.normal(k2, (E, H), dtype=jnp.float32) / np.sqrt(H)
        down_w = jax.random.normal(k3, (E, I, H), dtype=jnp.float32) / np.sqrt(H)
        up_w = jax.random.normal(k4, (E, H, I), dtype=jnp.float32) / np.sqrt(I)
        return {'x': x, 'router_w': router_w, 'down_w': down_w, 'up_w': up_w}
    _L2_ffn_all = _L2_ffn_setup()
    _L2_ffn_in = {k: v for k, v in _L2_ffn_all.items() if k in ('router_w', 'down_w', 'up_w')}
    del _L2_ffn_all

    def _L3_xattn_setup():
        import jax, jax.numpy as jnp
        import numpy as np
        B, S, L = (2, 128, 128)
        DIM_Q, H, K, D_C, D_CQ, R = (256, 16, 128, 64, 192, 64)

        def _rope_tables(seq_len, dim, dtype):
            inv_freq = 1.0 / 10000.0 ** (jnp.arange(0, dim, 2, dtype=dtype) / dim)
            t = jnp.arange(seq_len, dtype=dtype)
            freqs = t[:, None] * inv_freq[None, :]
            sin = jnp.repeat(jnp.sin(freqs), 2, axis=-1)
            cos = jnp.repeat(jnp.cos(freqs), 2, axis=-1)
            return (sin, cos)

        def _rotate_half(x):
            h = x.shape[-1] // 2
            return jnp.concatenate([-x[..., h:], x[..., :h]], axis=-1)
        key = jax.random.key(seed)
        ks = jax.random.split(key, 8)
        s_in = 1.0 / np.sqrt(DIM_Q)
        s_k = 1.0 / np.sqrt(K)
        s_cq = 1.0 / np.sqrt(D_CQ)
        s_c = 1.0 / np.sqrt(D_C)
        return {'hidden_q': jax.random.normal(ks[0], (B, S, DIM_Q), jnp.float32), 'kv_c': jax.random.normal(ks[1], (B, L, D_C), jnp.float32), 'Wq': jax.random.normal(ks[2], (H * K, DIM_Q), jnp.float32) * s_in, 'w_kc_q': jax.random.normal(ks[3], (H, K, D_CQ), jnp.float32) * s_k, 'w_kc_kv': jax.random.normal(ks[4], (H, K, D_C), jnp.float32) * s_k, 'W_qr': jax.random.normal(ks[5], (H, D_CQ, R), jnp.float32) * s_cq / np.sqrt(R), 'W_kr': jax.random.normal(ks[6], (H, D_C, R), jnp.float32) * s_c, 'Wo': jax.random.normal(ks[7], (DIM_Q, H * K), jnp.float32) * s_k}
    _L3_xattn_all = _L3_xattn_setup()
    _L3_xattn_in = {k: v for k, v in _L3_xattn_all.items() if k in ('Wq', 'w_kc_q', 'w_kc_kv', 'W_qr', 'W_kr', 'Wo')}
    del _L3_xattn_all

    def _L3_ffn_setup():
        import jax, jax.numpy as jnp
        import numpy as np
        B, S, H = (2, 256, 256)
        E, K = (16, 4)
        I_MOE, I_SH = (176, 704)
        key = jax.random.key(seed)
        ks = jax.random.split(key, 9)

        def w(k, shape, fan_in):
            return jax.random.normal(k, shape, jnp.float32) * fan_in ** (-0.5)
        return {'hidden_states': jax.random.normal(ks[0], (B, S, H), jnp.float32), 'router_w': w(ks[1], (E, H), H), 'w_gate': w(ks[2], (E, H, I_MOE), H), 'w_up': w(ks[3], (E, H, I_MOE), H), 'w_down': w(ks[4], (E, I_MOE, H), I_MOE), 'sh_gate': w(ks[5], (H, I_SH), H), 'sh_up': w(ks[6], (H, I_SH), H), 'sh_down': w(ks[7], (I_SH, H), I_SH), 'sh_gate_w': w(ks[8], (H, 1), H)}
    _L3_ffn_all = _L3_ffn_setup()
    _L3_ffn_in = {k: v for k, v in _L3_ffn_all.items() if k in ('router_w', 'w_gate', 'w_up', 'w_down', 'sh_gate', 'sh_up', 'sh_down', 'sh_gate_w')}
    del _L3_ffn_all
    return {'x': x, 'ctx_512': ctx_512, 'L0_xattn_W_k': _L0_xattn_in['W_k'], 'L0_xattn_b_k': _L0_xattn_in['b_k'], 'L0_xattn_ln_gamma': _L0_xattn_in['ln_gamma'], 'L0_xattn_ln_beta': _L0_xattn_in['ln_beta'], 'L0_ffn_router_weight': _L0_ffn_in['router_weight'], 'L0_ffn_w_gate': _L0_ffn_in['w_gate'], 'L0_ffn_w_up': _L0_ffn_in['w_up'], 'L0_ffn_w_down': _L0_ffn_in['w_down'], 'L0_ffn_ws_gate': _L0_ffn_in['ws_gate'], 'L0_ffn_ws_up': _L0_ffn_in['ws_up'], 'L0_ffn_ws_down': _L0_ffn_in['ws_down'], 'L0_ffn_w_shared_gate': _L0_ffn_in['w_shared_gate'], 'L1_xattn_Wq': _L1_xattn_in['Wq'], 'L1_xattn_w_kc_q': _L1_xattn_in['w_kc_q'], 'L1_xattn_w_kc_kv': _L1_xattn_in['w_kc_kv'], 'L1_xattn_W_qr': _L1_xattn_in['W_qr'], 'L1_xattn_W_kr': _L1_xattn_in['W_kr'], 'L1_xattn_Wo': _L1_xattn_in['Wo'], 'L1_ffn_w_gate': _L1_ffn_in['w_gate'], 'L1_ffn_w_up': _L1_ffn_in['w_up'], 'L1_ffn_w_down': _L1_ffn_in['w_down'], 'L2_xattn_Wq': _L2_xattn_in['Wq'], 'L2_xattn_Wk': _L2_xattn_in['Wk'], 'L2_xattn_gamma_raw': _L2_xattn_in['gamma_raw'], 'L2_ffn_router_w': _L2_ffn_in['router_w'], 'L2_ffn_down_w': _L2_ffn_in['down_w'], 'L2_ffn_up_w': _L2_ffn_in['up_w'], 'L3_xattn_Wq': _L3_xattn_in['Wq'], 'L3_xattn_w_kc_q': _L3_xattn_in['w_kc_q'], 'L3_xattn_w_kc_kv': _L3_xattn_in['w_kc_kv'], 'L3_xattn_W_qr': _L3_xattn_in['W_qr'], 'L3_xattn_W_kr': _L3_xattn_in['W_kr'], 'L3_xattn_Wo': _L3_xattn_in['Wo'], 'L3_ffn_router_w': _L3_ffn_in['router_w'], 'L3_ffn_w_gate': _L3_ffn_in['w_gate'], 'L3_ffn_w_up': _L3_ffn_in['w_up'], 'L3_ffn_w_down': _L3_ffn_in['w_down'], 'L3_ffn_sh_gate': _L3_ffn_in['sh_gate'], 'L3_ffn_sh_up': _L3_ffn_in['sh_up'], 'L3_ffn_sh_down': _L3_ffn_in['sh_down'], 'L3_ffn_sh_gate_w': _L3_ffn_in['sh_gate_w']}

def reference(x, ctx_512, L0_xattn_W_k, L0_xattn_b_k, L0_xattn_ln_gamma, L0_xattn_ln_beta, L0_ffn_router_weight, L0_ffn_w_gate, L0_ffn_w_up, L0_ffn_w_down, L0_ffn_ws_gate, L0_ffn_ws_up, L0_ffn_ws_down, L0_ffn_w_shared_gate, L1_xattn_Wq, L1_xattn_w_kc_q, L1_xattn_w_kc_kv, L1_xattn_W_qr, L1_xattn_W_kr, L1_xattn_Wo, L1_ffn_w_gate, L1_ffn_w_up, L1_ffn_w_down, L2_xattn_Wq, L2_xattn_Wk, L2_xattn_gamma_raw, L2_ffn_router_w, L2_ffn_down_w, L2_ffn_up_w, L3_xattn_Wq, L3_xattn_w_kc_q, L3_xattn_w_kc_kv, L3_xattn_W_qr, L3_xattn_W_kr, L3_xattn_Wo, L3_ffn_router_w, L3_ffn_w_gate, L3_ffn_w_up, L3_ffn_w_down, L3_ffn_sh_gate, L3_ffn_sh_up, L3_ffn_sh_down, L3_ffn_sh_gate_w):
    import jax
    import jax.numpy as jnp

    def _L0_xattn_ref(p, k_v, W_k, b_k, ln_gamma, ln_beta):
        import jax, jax.numpy as jnp
        import numpy as np
        EPS = 1e-06
        IMAGE_DIMS = 256
        kv = k_v @ W_k.T + b_k
        out = jnp.einsum('bij,bjd->bid', p, kv)
        scale = IMAGE_DIMS ** (-0.5)
        sim = jnp.einsum('bid,bjd->bij', out, kv) * scale
        mu = jnp.mean(sim, axis=-1, keepdims=True)
        var = jnp.var(sim, axis=-1, keepdims=True)
        sim = (sim - mu) * jax.lax.rsqrt(var + EPS) * ln_gamma + ln_beta
        attn = jax.nn.softmax(sim, axis=-1)
        return attn

    def _L0_ffn_ref(hidden_states, router_weight, w_gate, w_up, w_down, ws_gate, ws_up, ws_down, w_shared_gate):
        import jax, jax.numpy as jnp
        import numpy as np
        TOP_K = 4
        NORM_TOPK_PROB = False
        B, S, D = hidden_states.shape
        x = hidden_states.reshape(-1, D)
        T = x.shape[0]
        logits = x @ router_weight.T
        probs = jax.nn.softmax(logits.astype(jnp.float32), axis=-1)
        top_v, top_i = jax.lax.top_k(probs, TOP_K)
        if NORM_TOPK_PROB:
            top_v = top_v / jnp.sum(top_v, axis=-1, keepdims=True)
        scores = jnp.zeros_like(probs).at[jnp.arange(T)[:, None], top_i].set(top_v)
        hg = jnp.einsum('td,efd->tef', x, w_gate)
        hu = jnp.einsum('td,efd->tef', x, w_up)
        h = jax.nn.silu(hg) * hu
        expert_out = jnp.einsum('tef,te,edf->td', h, scores, w_down)
        sh = jax.nn.silu(x @ ws_gate.T) * (x @ ws_up.T) @ ws_down.T
        g = jax.nn.sigmoid(x @ w_shared_gate.T)
        out = expert_out + g * sh
        return out.reshape(B, S, D)

    def _L1_xattn_ref(hidden_q, kv_c, Wq, w_kc_q, w_kc_kv, W_qr, W_kr, Wo):
        import jax, jax.numpy as jnp
        import numpy as np
        B, S, L = (2, 128, 128)
        DIM_Q, H, K, D_C, D_CQ, R = (256, 16, 128, 64, 192, 64)

        def _rope_tables(length, dim):
            inv = 1.0 / 10000.0 ** (jnp.arange(0, dim, 2, dtype=jnp.float32) / dim)
            f = jnp.arange(length, dtype=jnp.float32)[:, None] * inv[None, :]
            sin = jnp.repeat(jnp.sin(f), 2, axis=-1)
            cos = jnp.repeat(jnp.cos(f), 2, axis=-1)
            return (sin, cos)

        def _rotate_half(x):
            half = x.shape[-1] // 2
            return jnp.concatenate([-x[..., half:], x[..., :half]], axis=-1)

        def _apply_rope(x, sin, cos):
            return x * cos + _rotate_half(x) * sin
        Bv, Sv, _ = hidden_q.shape
        _, Lv, _ = kv_c.shape
        q_hk = (hidden_q @ Wq.T).reshape(Bv, Sv, H, K)
        q_big = jnp.einsum('bshk,hkq->bshq', q_hk, w_kc_q)
        sin_q, cos_q = _rope_tables(Sv, D_CQ)
        q_big = _apply_rope(q_big, sin_q[None, :, None, :], cos_q[None, :, None, :])
        sin_k, cos_k = _rope_tables(Lv, D_C)
        kv_r = _apply_rope(kv_c, sin_k[None], cos_k[None])
        q_r = jnp.einsum('bshq,hqr->bhsr', q_big, W_qr)
        k_r = jnp.einsum('bld,hdr->bhlr', kv_r, W_kr)
        scores = jnp.einsum('bhsr,bhlr->bhsl', q_r, k_r)
        attn = jax.nn.softmax(scores, axis=-1)
        ctx_c = jnp.einsum('bhsl,bld->bhsd', attn, kv_r)
        ctx_lat = jnp.einsum('bhsd,hkd->bhsk', ctx_c, w_kc_kv)
        ctx = ctx_lat.transpose(0, 2, 1, 3).reshape(Bv, Sv, H * K)
        return ctx @ Wo.T

    def _L1_ffn_ref(x, w_gate, w_up, w_down):
        import jax, jax.numpy as jnp
        import numpy as np
        EPS = 1e-05

        def _quant_weight(w):
            scale = jnp.mean(jnp.abs(w)) + EPS
            wq = jnp.clip(jnp.round(w / scale), -1.0, 1.0)
            return (wq, scale)

        def _quant_act(x):
            s = jnp.max(jnp.abs(x), axis=-1, keepdims=True) / 127.0 + EPS
            xq = jnp.clip(jnp.round(x / s), -128.0, 127.0)
            return (xq, s)

        def _qlinear(x, w):
            wq, ws = _quant_weight(w)
            xq, xs = _quant_act(x)
            y = jnp.einsum('bsi,oi->bso', xq, wq)
            return y * xs * ws
        gate = jax.nn.silu(_qlinear(x, w_gate))
        up = _qlinear(x, w_up)
        return _qlinear(gate * up, w_down)

    def _L2_xattn_ref(h, adj_raw, Wq, Wk, gamma_raw):
        import jax, jax.numpy as jnp
        import numpy as np
        B, N, D = (16, 256, 64)
        H = 4
        TOP_K_RATIO = 0.3
        b, n, dm = h.shape
        d = dm // H
        Q = (h @ Wq.T).reshape(b, n, H, d).transpose(0, 2, 1, 3)
        K = (h @ Wk.T).reshape(b, n, H, d).transpose(0, 2, 1, 3)
        sim = jnp.einsum('bhnd,bhmd->bnm', Q, K) / (jnp.sqrt(jnp.float32(d)) * H)
        k = max(1, int(n * TOP_K_RATIO))
        topk_vals = jax.lax.top_k(sim, k)[0]
        threshold = topk_vals[:, :, -1:]
        sparse_mask = (sim >= threshold).astype(sim.dtype)
        A_learned = jax.nn.sigmoid(sim) * sparse_mask
        A_learned = (A_learned + jnp.swapaxes(A_learned, -1, -2)) * 0.5
        gamma = jax.nn.sigmoid(gamma_raw)
        return (1.0 - gamma) * adj_raw + gamma * A_learned

    def _L2_ffn_ref(x, router_w, down_w, up_w):
        import jax, jax.numpy as jnp
        import numpy as np
        H = 256
        E = 8
        K = 2
        I = 16
        logits = jnp.einsum('bth,eh->bte', x, router_w)
        weights = jax.nn.softmax(logits, axis=-1)
        top_w, top_idx = jax.lax.top_k(weights, K)
        topk_mask = jnp.sum(jax.nn.one_hot(top_idx, E, dtype=x.dtype), axis=-2)
        gate = weights * topk_mask
        h = jnp.einsum('bth,eih->beti', x, down_w)
        a = jax.nn.silu(h)
        expert_out = jnp.einsum('beti,ehi->beth', a, up_w)
        out = jnp.einsum('beth,bte->bth', expert_out, gate)
        return out

    def _L3_xattn_ref(hidden_q, kv_c, Wq, w_kc_q, w_kc_kv, W_qr, W_kr, Wo):
        import jax, jax.numpy as jnp
        import numpy as np
        B, S, L = (2, 128, 128)
        DIM_Q, H, K, D_C, D_CQ, R = (256, 16, 128, 64, 192, 64)

        def _rope_tables(seq_len, dim, dtype):
            inv_freq = 1.0 / 10000.0 ** (jnp.arange(0, dim, 2, dtype=dtype) / dim)
            t = jnp.arange(seq_len, dtype=dtype)
            freqs = t[:, None] * inv_freq[None, :]
            sin = jnp.repeat(jnp.sin(freqs), 2, axis=-1)
            cos = jnp.repeat(jnp.cos(freqs), 2, axis=-1)
            return (sin, cos)

        def _rotate_half(x):
            h = x.shape[-1] // 2
            return jnp.concatenate([-x[..., h:], x[..., :h]], axis=-1)
        b, s, _ = hidden_q.shape
        l = kv_c.shape[1]
        q_hk = (hidden_q @ Wq.T).reshape(b, s, H, K)
        q_big = jnp.einsum('bshk,hkq->bshq', q_hk, w_kc_q)
        sin, cos = _rope_tables(l, D_C, kv_c.dtype)
        kv_rope = kv_c * cos[None] + _rotate_half(kv_c) * sin[None]
        q_r = jnp.einsum('bshq,hqr->bhsr', q_big, W_qr)
        k_r = jnp.einsum('bld,hdr->bhlr', kv_rope, W_kr)
        scores = jnp.einsum('bhsr,bhlr->bhsl', q_r, k_r)
        attn = jax.nn.softmax(scores, axis=-1)
        ctx_c = jnp.einsum('bhsl,bld->bhsd', attn, kv_rope)
        ctx_lat = jnp.einsum('bhsd,hkd->bshk', ctx_c, w_kc_kv)
        out = ctx_lat.reshape(b, s, H * K) @ Wo.T
        return out

    def _L3_ffn_ref(hidden_states, router_w, w_gate, w_up, w_down, sh_gate, sh_up, sh_down, sh_gate_w):
        import jax, jax.numpy as jnp
        import numpy as np
        B, S, H = (2, 256, 256)
        E, K = (16, 4)
        I_MOE, I_SH = (176, 704)
        orig = hidden_states.shape
        h = hidden_states.reshape(-1, orig[-1])
        N = h.shape[0]
        logits = h @ router_w.T
        probs = jax.nn.softmax(logits.astype(jnp.float32), axis=-1)
        top_vals, top_idx = jax.lax.top_k(probs, K)
        top_vals = top_vals / jnp.maximum(top_vals.sum(-1, keepdims=True), 1e-09)
        top_vals = top_vals.astype(h.dtype)
        comb = jnp.zeros((N, E), h.dtype).at[jnp.arange(N)[:, None], top_idx].add(top_vals)
        g = jnp.einsum('nh,ehi->eni', h, w_gate)
        u = jnp.einsum('nh,ehi->eni', h, w_up)
        y = jnp.einsum('eni,eih->enh', jax.nn.silu(g) * u, w_down)
        routed = jnp.einsum('enh,ne->nh', y, comb)
        shared = jax.nn.silu(h @ sh_gate) * (h @ sh_up) @ sh_down
        sg = jax.nn.sigmoid(h @ sh_gate_w)
        return (routed + sg * shared).reshape(orig)
    x = x + _L0_xattn_ref(_layernorm(x, axis=-1), ctx_512, L0_xattn_W_k, L0_xattn_b_k, L0_xattn_ln_gamma, L0_xattn_ln_beta)
    x = x + _L0_ffn_ref(_layernorm(x, axis=-1), L0_ffn_router_weight, L0_ffn_w_gate, L0_ffn_w_up, L0_ffn_w_down, L0_ffn_ws_gate, L0_ffn_ws_up, L0_ffn_ws_down, L0_ffn_w_shared_gate)
    x = x + _L1_xattn_ref(_layernorm(x, axis=-1), ctx_512, L1_xattn_Wq, L1_xattn_w_kc_q, L1_xattn_w_kc_kv, L1_xattn_W_qr, L1_xattn_W_kr, L1_xattn_Wo)
    x = x + _L1_ffn_ref(_layernorm(x, axis=-1), L1_ffn_w_gate, L1_ffn_w_up, L1_ffn_w_down)
    x = x + _L2_xattn_ref(ctx_512, _layernorm(x, axis=-1), L2_xattn_Wq, L2_xattn_Wk, L2_xattn_gamma_raw)
    x = x + _L2_ffn_ref(_layernorm(x, axis=-1), L2_ffn_router_w, L2_ffn_down_w, L2_ffn_up_w)
    x = x + _L3_xattn_ref(_layernorm(x, axis=-1), ctx_512, L3_xattn_Wq, L3_xattn_w_kc_q, L3_xattn_w_kc_kv, L3_xattn_W_qr, L3_xattn_W_kr, L3_xattn_Wo)
    x = x + _L3_ffn_ref(_layernorm(x, axis=-1), L3_ffn_router_w, L3_ffn_w_gate, L3_ffn_w_up, L3_ffn_w_down, L3_ffn_sh_gate, L3_ffn_sh_up, L3_ffn_sh_down, L3_ffn_sh_gate_w)
    return x

_drawn_inputs = setup_inputs


def setup_inputs(seed=0):
    import zlib

    import numpy as np

    out = dict(_drawn_inputs(seed))
    spreads = {'L0_xattn_b_k': (0.0, 2.0),
     'L0_xattn_ln_gamma': (1.0, 0.6),
     'L0_xattn_ln_beta': (0.0, 0.8)}
    factors = {'L0_xattn_W_k': 7.502,
     'L0_ffn_router_weight': 7.931,
     'L0_ffn_w_gate': 7.497,
     'L0_ffn_w_up': 8.0,
     'L0_ffn_w_down': 6.79,
     'L0_ffn_ws_gate': 3.119,
     'L0_ffn_ws_up': 3.323,
     'L0_ffn_ws_down': 3.322,
     'L0_ffn_w_shared_gate': 8.0,
     'L2_xattn_Wq': 5.683,
     'L2_xattn_Wk': 5.716,
     'L3_ffn_sh_gate_w': 2.77}
    for name, (base, spread) in spreads.items():
        noise = np.random.default_rng([zlib.crc32(name.encode()), seed]).standard_normal(out[name].shape)
        drawn = base * np.exp(spread * noise) if base else spread * noise
        out[name] = jnp.asarray(drawn.astype(out[name].dtype))
    for name, factor in factors.items():
        out[name] = (out[name] * factor).astype(out[name].dtype)
    return out
```

```python
from contextlib import ExitStack

import numpy as np

import concourse.bass as bass
from concourse import mybir

F32 = mybir.dt.float32
BF16 = mybir.dt.bfloat16
U16 = mybir.dt.uint16
U32 = mybir.dt.uint32
ALU = mybir.AluOpType
ACT = mybir.ActivationFunctionType
AX = mybir.AxisListType

P = 128
B, S, D, C = 4, 256, 256, 64
T = B * S // P
TOK = B * S
KD = D // P
H, HK, CQ, R = 16, 128, 192, 64
CH = CQ // 2
E, FE, FS = 16, 176, 704
EX = E + 1
FT = (E * FE + FS + P - 1) // P
GRP = 2
NG = FT // GRP
LOOP = NG // 2
HALF = TOK // 2
TOPK = 4
I1 = 1024
KEEP = int(S * 0.3)
E2, IE2 = 8, 16
RNE = 1.5 * 2.0 ** 23
BIG = 3.0e38


class Chain:

    def __init__(self, eng, sem):
        self.eng, self.sem, self.base, self.at, self.trip = eng, sem, 0, 0, 0

    def __call__(self, ins):
        ins.then_inc(self.sem, 1)
        self.at += 1
        self.eng.wait_ge(self.sem, self.trip + self.base + self.at)

    def enter(self, i, first, per):
        self.base, self.at, self.first, self.per = self.base + self.at - first * per, 0, first, per
        self.trip = i * per

    def leave(self, trips):
        assert self.at == self.per, (self.at, self.per)
        self.base, self.at, self.trip = self.base + (self.first + trips) * self.per, 0, 0


def build(nc, a, out, stages=8):
    ctx = ExitStack()
    with ctx:
        def sb(name, shape, dt=F32):
            return ctx.enter_context(nc.sbuf_tensor(name, shape, dt))

        sems = {}

        def sem(name):
            if name not in sems:
                sems[name] = ctx.enter_context(nc.semaphore(name))
            return sems[name]

        PB = [ctx.enter_context(nc.psum_tensor(f"bank{i}", [P, 512], F32)) for i in range(8)]

        X = sb("X", [P, T, D])
        XN = sb("XN", [P, T, D])
        XT = sb("XT", [P, KD, TOK])
        A = sb("A", [P, T, S])
        ident = sb("ident", [P, P])
        identb = sb("identb", [P, P], BF16)
        ones = sb("ones", [P, P])
        ctok = sb("ctok", [P, T, C])
        kvdup = sb("kvdup", [P, T, 2, C])
        kvaug = sb("kvaug", [P, T, C + 1])
        kvrT = sb("kvrT", [P, TOK])
        st6 = sb("st6", [P, T, 6])
        mv = sb("mv", [P, T, 2])
        rstd = sb("rstd", [P, T])
        epsc = sb("epsc", [P, 2])
        sc8 = sb("sc8", [P, 3, T])
        small = sb("small", [P, 16])
        WB = sb("WB", [P, 3, 2048], BF16)
        WF = sb("WF", [P, 6144])
        RF = sb("RF", [P, 2048])
        PF = sb("PF", [P, 8, D])
        RAW = sb("RAW", [P, 17408])
        iote = sb("iote", [P, E])
        wr01 = sb("wr01", [P, 2, KD * EX])
        wr2 = sb("wr2", [P, KD * E2])
        PH = sb("PH", [P, 9984])

        ctxT = WF[0:C + 1, 0:TOK]
        wkaug = WF[0:C + 1, 1024:1024 + C]
        wq2 = WF[0:C, 1088:1088 + C]
        wk2 = WF[0:C, 1152:1152 + C]
        n2 = WF[0:C, 1216:1216 + C]
        uT = WF[0:C, 1280:1280 + TOK]
        SIM = WF[:, 2304:2304 + T * S].rearrange("p (t s) -> p t s", t=T)
        kvT0 = PH[0:C, 0:TOK]
        kv0 = PH[:, 1024:1024 + T * C].rearrange("p (t c) -> p t c", t=T)
        outT = PH[0:C, 1536:1536 + TOK]
        gam = PH[:, 2560:2816]
        bet = PH[:, 2816:3072]
        ropek = PH[:, 3072:3072 + 2 * 2 * C].rearrange("p (a s c) -> p a s c", a=2, s=2)
        kt1 = PH[:, 3328:3328 + T * C].rearrange("p (t c) -> p t c", t=T)
        kt2 = PH[:, 3840:3840 + T * C].rearrange("p (t c) -> p t c", t=T)

        ring = PH[:, 0:3072].rearrange("p (g w) -> p g w", g=2)
        selr = PH[0:3 * EX, 3072:3328].bitcast(BF16).rearrange("p (g w) -> p g w", g=2)
        HT = PH[:, 3328:5376].rearrange("p (q w) -> p q w", q=4)
        sil = PH[:, 5376:6400].rearrange("p (q w) -> p q w", q=2)
        tmu = PH[:, 6400:7424].rearrange("p (q w) -> p q w", q=2)
        SCT = PH[0:3 * EX, 7424:7936].bitcast(BF16)
        o = 7984
        pr = PH[:, o:o + T * EX].rearrange("p (t e) -> p t e", t=T); o += T * EX
        pm = PH[:, o:o + T * EX].rearrange("p (t e) -> p t e", t=T); o += T * EX
        pk = PH[:, o:o + T * E].rearrange("p (t e) -> p t e", t=T); o += T * E
        pq = PH[:, o:o + T * E].rearrange("p (t e) -> p t e", t=T); o += T * E
        top8 = PH[:, o:o + T * 8].rearrange("p (t e) -> p t e", t=T); o += T * 8
        idx8 = PH[:, o:o + T * 8].bitcast(U32).rearrange("p (t e) -> p t e", t=T); o += T * 8
        idf = PH[:, o:o + T * 8].rearrange("p (t e) -> p t e", t=T); o += T * 8
        scp = PH[:, o:o + T * 3 * EX // 2].bitcast(BF16).rearrange("p (t c e) -> p t c e", t=T, c=3); o += T * 3 * EX // 2
        twork = PH[:, o:o + S]; o += S
        tmax = PH[:, o:o + 8]; o += 8
        assert o <= 9984

        qcT = PH[:, 0:2048].rearrange("p (g s) -> p g s", g=8)
        Ex = PH[:, 2048:3072].rearrange("p (q s l) -> p q s l", q=2, s=2)
        PT = PH[:, 3072:4096].rearrange("p (q l s) -> p q l s", q=2, l=2)
        CC = PH[:, 4096:4608].rearrange("p (q s c) -> p q s c", q=2, s=2)
        CCT = PH[:, 4608:5120].rearrange("p (q s) -> p q s", q=2)
        kvb = PH[:, 5120:5376]
        kvab = PH[:, 5376:5506].rearrange("p (l c) -> p l c", l=2)
        nmx = PH[:, 5506:5514].rearrange("p (q s) -> p q s", q=4)
        rin = PH[:, 5514:5522].rearrange("p (q s) -> p q s", q=2)
        cosq = PH[0:CH, 5632:6144]
        sinq = PH[0:CH, 6144:6656]
        r1 = PH[0:CH, 6656:7680].rearrange("p (q s) -> p q s", q=2)
        r2 = PH[0:CH, 7680:8704].rearrange("p (q s) -> p q s", q=2)
        qr = PH[0:CH, 8704:9728].rearrange("p (q s) -> p q s", q=2)
        W1 = WF[:, :].rearrange("p (k h q) -> p k h q", k=KD, h=H)
        MF = WF[:, 0:2048].rearrange("p (k w) -> p k w", k=KD)
        GF = WF[:, 2048:3072].rearrange("p (h c) -> p h c", h=H)
        RFv = RF[0:CH, :].rearrange("p (h f c) -> p h f c", h=H, f=2)
        rWq = RAW[:, 0:4096].rearrange("p (h d) -> p h d", h=H)
        rWo = RAW[:, 4096:8192].rearrange("p (h d) -> p h d", h=H)
        rKv = RAW[:, 8192:9216].rearrange("p (h c) -> p h c", h=H)
        rKr = RAW[0:R, 9216:10240].rearrange("p (h c) -> p h c", h=H)
        rQr = RAW[0:R, 10240:13312 - 0].rearrange("p (h q) -> p h q", h=H)
        rKq = RAW[:, 13312:16384].rearrange("p (h q) -> p h q", h=H)
        rKqT = RAW[0:CH, 13312:17408].rearrange("p (f h k) -> p f h k", f=2, h=H)

        rF = RAW[:, 0:6144].rearrange("p (m w) -> p m w", m=3)
        XQ = PH[:, 0:1024].bitcast(BF16).rearrange("p (t d) -> p t d", t=T)
        XQT = PH[:, 1024:2048].bitcast(BF16).rearrange("p (k n) -> p k n", k=KD)
        qt = PH[:, 2048:4096]
        silq = PH[:, 4096:5120]
        hq = PH[:, 5120:6144]
        hqb = PH[:, 6144:6656].bitcast(BF16)
        hqT = PH[:, 6656:7168].bitcast(BF16)
        q8 = PH[:, 7168:7232].rearrange("p (c t) -> p c t", c=8)
        amax, xs8, xr8, sg8, su8, ys8 = (q8[:, n, :] for n in range(6))
        hs = PH[:, 7232:7240]
        sgc = PH[:, 7240:7241]
        wsum = sb("wsum", [P, 3])
        wtot = sb("wtot", [P, 3])
        winv = sb("winv", [P, 3])
        neg1 = sb("neg1", [P, 3])

        w2d = PH[:, 7296:7552].rearrange("p (k n) -> p k n", k=KD)
        w2u = PH[:, 7552:7808]
        a2 = PH[:, 8832:9856].rearrange("p (t n) -> p t n", t=T)
        a2T = PH[:, 0:1024]

        wg_ = lambda g, k, jj: ring[:, g, k * 256 + jj * P:k * 256 + jj * P + P]
        wu_ = lambda g, k, jj: ring[:, g, 512 + k * 256 + jj * P:512 + k * 256 + jj * P + P]
        wd_ = lambda g, jj: ring[:, g, 1024 + jj * D:1024 + jj * D + D]

        def fuse_copy(l, n, copy):
            src = PB[4 + n % 4]
            if n < 4:
                return copy(RF[0:CH, n * 512:(n + 1) * 512], src[0:CH, :])
            if n < 8:
                return copy(PF[:, 2 * (n - 4):2 * (n - 4) + 2, :], src[:, :].rearrange("p (g d) -> p g d", g=2))
            if l == 0:
                k, g = divmod(n - 8, 8)
                return copy(W1[:, k, 2 * g:2 * g + 2, :], src[:, 0:2 * CQ].rearrange("p (h q) -> p h q", h=2))
            if n < 10:
                return copy(GF[:, 8 * (n - 8):8 * (n - 7), :], src[:, :].rearrange("p (h c) -> p h c", h=8))
            k, g = divmod(n - 10, 2)
            return copy(MF[:, k, g * 512:(g + 1) * 512], src[:, :])

        block = ctx.enter_context(nc.Block())
        FFN_AT = {1: 0, 7: 1}

        @block.sync
        def _(sp):
            sp.dma_start(X[:, :, :], a["x"].rearrange("b (s p) d -> p (b s) d", p=P)).then_inc(sem("x_loaded"), 16)
            for dst, name in ((ident[:, :], "ident"), (ctxT[0:C, :], "ctxT"), (wkaug, "wkaug"), (wq2, "wq2"), (wk2, "wk2"),
                              (ctok[:, :, :], None), (ropek, "ropek"), (identb[:, :].bitcast(U16), "identb")):
                src = a[name] if name else a["ctx"].rearrange("b (s p) c -> p (b s) c", p=P)
                sp.dma_start(dst, src).then_inc(sem("consts_loaded"), 16)
            sp.dma_start(gam, a["gamma"].partition_broadcast(P)).then_inc(sem("consts_loaded"), 16)
            sp.dma_start(bet, a["beta"].partition_broadcast(P)).then_inc(sem("consts_loaded"), 16)
            sp.dma_start(small[:, 0:1], a["graw"].partition_broadcast(P)).then_inc(sem("consts_loaded"), 16)

            sp.dma_start(iote[:, :], a["iote"].partition_broadcast(P)).then_inc(sem("router_loaded"), 16)
            for dst, name in ((wr01[:, 0, :], "router0"), (wr01[:, 1, :], "router1"), (wr2[:, :], "router2")):
                sp.dma_start(dst, a[name]).then_inc(sem("router_loaded"), 16)

            def ffn_weights(f):
                w, sel = a[f"w{f}"], a["sel"]
                sp.wait_ge(sem("stage_done"), (1, 7)[f])
                for g in range(2):
                    sp.dma_start(ring[:, g, :], w[g]).then_inc(sem(f"w_full{g}"), 16)
                    sp.dma_start(selr[:, g, :].bitcast(U16), sel[:, g * 256:(g + 1) * 256]).then_inc(sem(f"w_full{g}"), 16)
                with sp.Fori(1, LOOP) as i:
                    for g in range(2):
                        sp.wait_ge(sem("down_done"), i * 8 + (8 * LOOP * f - 8 + 4 * (g + 1)))
                        sp.dma_start(ring[:, g, :], w[bass.ds(i * 2 + g, 1)].rearrange("g p w -> p (g w)")).then_inc(sem(f"w_full{g}"), 16)
                        sp.dma_start(selr[:, g, :].bitcast(U16), sel[:, bass.ds(i * 512 + g * 256, 256)]).then_inc(sem(f"w_full{g}"), 16)

            def attention_weights(l):
                for dst, name in ((rWq, "Wq"), (rWo, "Wo"), (rKv, "Kv"), (rKr, "Kr"), (rQr, "Qr"), (rKqT if l else rKq, "Kq")):
                    sp.dma_start(dst, a[f"{name}{l}"]).then_inc(sem("raw_loaded"), 16)

            attention_weights(0)
            if stages >= 2:
                ffn_weights(0)
            if stages >= 3:
                sp.wait_ge(sem("stage_done"), 2)
                sp.dma_start(cosq, a["cosq"]).then_inc(sem("rope_loaded"), 16)
                sp.dma_start(sinq, a["sinq"]).then_inc(sem("rope_loaded"), 16)
            if stages >= 4:
                sp.wait_ge(sem("fuse_done"), 24)
                sp.dma_start(rF, a["w1ffn"]).then_inc(sem("w1ffn_loaded"), 16)
            if stages >= 6:
                sp.wait_ge(sem("stage_done"), 3)
                sp.dma_start(w2d, a["w2d"]).then_inc(sem("w2_loaded"), 16)
                sp.dma_start(w2u, a["w2u"]).then_inc(sem("w2_loaded"), 16)
            if stages >= 7:
                sp.wait_ge(sem("wq_ready"), 3)
                attention_weights(1)
            if stages >= 8:
                ffn_weights(1)
            sp.wait_ge(sem("x_final"), 1)
            sp.dma_start(out.rearrange("b (s p) d -> p (b s) d", p=P), X[:, :, :]).then_inc(sem("stored"), 16)
            sp.wait_ge(sem("stored"), 16)

        @block.tensor
        def _(pe):
            mm = nc.tensor.matmul

            def ln_transposes(k):
                for tg in range(2):
                    for kk in range(KD):
                        for q in range(4):
                            t = tg * 4 + q
                            pe.wait_ge(sem("ln_x"), 8 * k + t + 1)
                            last = nc.tensor.transpose(PB[tg * 2 + kk][:, q * P:(q + 1) * P],
                                                       XN[:, t, kk * P:(kk + 1) * P], ident[:, :])
                        last.then_inc(sem("ln_T"), 1)
                pe.wait_ge(sem("xt_act"), 2 * (k + 1))
                pe.wait_ge(sem("xt_dve"), 2 * (k + 1))

            def context():
                pe.wait_ge(sem("consts_loaded"), 16 * 11)
                pe.wait_ge(sem("ctx_ones"), 1)
                for n in range(2):
                    mm(PB[n][0:C, :], wkaug, ctxT[:, n * 512:(n + 1) * 512], start=True, stop=True).then_inc(sem("kvT_done"), 1)
                for t in range(T):
                    last = mm(PB[2][:, t * C:(t + 1) * C], ctxT[:, t * P:(t + 1) * P], wkaug, start=True, stop=True)
                last.then_inc(sem("kv_done"), 1)
                mm(PB[3][0:C, 0:C], wq2, wk2, start=True, stop=True).then_inc(sem("n2_done"), 1)
                pe.wait_ge(sem("n2_copied"), 1)
                for n in range(2):
                    mm(PB[4 + n][0:C, :], n2, ctxT[0:C, n * 512:(n + 1) * 512], start=True, stop=True).then_inc(sem("uT_done"), 1)
                pe.wait_ge(sem("kvr_ready"), 1)
                for n in range(2):
                    for q in range(4):
                        t = 4 * n + q
                        last = nc.tensor.transpose(PB[6 + n][:, q * P:(q + 1) * P],
                                                   kvdup[:, t, :, :].rearrange("p a c -> p (a c)"), ident[:, :])
                    last.then_inc(sem("kvrT_done"), 1)
                pe.wait_ge(sem("uT_copied"), 2)
                pe.wait_ge(sem("kvT_copied"), 2)
                pe.wait_ge(sem("kv_copied"), 1)
                for t in range(T):
                    b = t // 2
                    last = mm(PB[b][:, (t % 2) * S:(t % 2 + 1) * S], uT[:, t * P:(t + 1) * P], ctxT[0:C, b * S:(b + 1) * S],
                              start=True, stop=True)
                    if t % 2:
                        last.then_inc(sem("sim_done"), 1)

            def l0_attention():
                ln_transposes(0)
                pe.wait_ge(sem("kvrT_copied"), 2)
                for b in range(B):
                    for k in range(KD):
                        last = mm(PB[4 + b // 2][0:C, (b % 2) * S:(b % 2 + 1) * S], kv0[:, 2 * b + k, :],
                                  XT[:, k, b * S:(b + 1) * S], start=(k == 0), stop=(k == KD - 1))
                    if b % 2:
                        last.then_inc(sem("l0_out"), 1)
                pe.wait_ge(sem("l0_out_copied"), 2)
                for t in range(T):
                    b = t // 2
                    last = mm(PB[b][:, (t % 2) * S:(t % 2 + 1) * S], outT[:, t * P:(t + 1) * P], kvT0[:, b * S:(b + 1) * S],
                              start=True, stop=True)
                    if t % 2:
                        last.then_inc(sem("l0_sim"), 1)

            def ffn(f, lnk):
                ln_transposes(lnk)
                pe.wait_ge(sem("router_loaded"), 64)
                wr = wr01[:, f, :].rearrange("p (k e) -> p k e", k=KD)
                for t in range(T):
                    for k in range(KD):
                        last = mm(PB[0][:, t * EX:(t + 1) * EX], XT[:, k, t * P:(t + 1) * P], wr[:, k, :],
                                  start=(k == 0), stop=(k == KD - 1))
                last.then_inc(sem("logits"), 1)
                pe.wait_ge(sem("scores_split"), f + 1)
                scT = PB[1][:, :].bitcast(BF16)
                for t in range(T):
                    last = nc.tensor.transpose(scT[0:3 * EX, t * P:(t + 1) * P], scp[:, t, :, :].rearrange("p c e -> p (c e)"), identb[:, :])
                last.then_inc(sem("scoresT"), 1)
                pe.wait_ge(sem("scoresT_copied"), f + 1)
                base = f * 8 * LOOP

                def gate_up(i, u):
                    g, jj, half = u // 4, u // 2 % 2, u % 2
                    n = i * 8 + (u + base)
                    first = isinstance(i, int) and u < 2
                    if u % 4 == 0:
                        pe.wait_ge(sem(f"w_full{g}"), i * 32 + (32 + 32 * LOOP * f))
                    if not first:
                        pe.wait_ge(sem("h_done"), n - 1)
                    for dst, w, done in ((PB[u % 2], wg_, "gate_done"), (PB[2 + u % 2], wu_, "up_done")):
                        for k in range(KD):
                            last = mm(dst[:, :], w(g, k, jj), XT[:, k, half * HALF:(half + 1) * HALF],
                                      start=(k == 0), stop=(k == KD - 1))
                        last.then_inc(sem(done), 1)

                def spread(i, u):
                    g, jj, half = u // 4, u // 2 % 2, u % 2
                    pe.wait_ge(sem("silu_done"), i * 8 + (u + base + 1))
                    mm(PB[u % 2][:, :], selr[:, g, jj * P:(jj + 1) * P], SCT[:, half * HALF:(half + 1) * HALF],
                       start=True, stop=True).then_inc(sem("spread_done"), 1)

                def down(i, u, first=False):
                    g, jj, half = u // 4, u // 2 % 2, u % 2
                    pe.wait_ge(sem("h_done"), i * 8 + (u + base + 1))
                    for q in range(4):
                        last = mm(PB[4 + half * 2 + q // 2][:, (q % 2) * D:(q % 2 + 1) * D], HT[:, u % 4, q * P:(q + 1) * P],
                                  wd_(g, jj), start=(first and q % 2 == 0), stop=False, skip_group_check=True)
                    last.then_inc(sem("down_done"), 1)

                def trip(i, first):
                    for u in range(8):
                        gate_up(i, u)
                        if not (first and u < 1):
                            spread(i if u else i - 1, (u - 1) % 8)
                        if not (first and u < 2):
                            down(i if u > 1 else i - 1, (u - 2) % 8, first=first and u - 2 < 2)

                trip(0, True)
                with pe.Fori(1, LOOP) as i:
                    trip(i, False)
                spread(LOOP - 1, 7)
                down(LOOP - 1, 6)
                down(LOOP - 1, 7)

            def fuse(l):
                pe.wait_ge(sem("raw_loaded"), 96 * (l + 1))
                pe.wait_ge(sem("stage_done"), (2, 6)[l])
                base, ab = (0, 24)[l], (0, 12)[l]
                n = [0]

                def bank():
                    if n[0] >= 4:
                        m = n[0] - 4
                        pe.wait_ge(sem(("fuse_act", "fuse_dve")[m % 2]), ab + m // 2 + 1)
                    n[0] += 1
                    return PB[4 + (n[0] - 1) % 4]

                for g in range(4):
                    dst = bank()
                    for q in range(4):
                        for half in range(2):
                            last = mm(dst[0:CH, (q * 2 + half) * C:(q * 2 + half + 1) * C], rQr[:, 4 * g + q, half * CH:(half + 1) * CH],
                                      rKr[:, 4 * g + q, :], start=True, stop=True)
                    last.then_inc(sem("fuse_done"), 1)
                for g in range(4):
                    dst = bank()
                    for q in range(4):
                        last = mm(dst[(q % 2) * C:(q % 2 + 1) * C, (q // 2) * D:(q // 2 + 1) * D], rKv[:, 4 * g + q, :], rWo[:, 4 * g + q, :],
                                  start=True, stop=True)
                    last.then_inc(sem("fuse_done"), 1)
                if l == 0:
                    for k in range(KD):
                        for g in range(8):
                            dst = bank()
                            for q in range(2):
                                last = mm(dst[:, q * CQ:(q + 1) * CQ], rWq[:, 2 * g + q, k * P:(k + 1) * P], rKq[:, 2 * g + q, :],
                                          start=True, stop=True)
                            last.then_inc(sem("fuse_done"), 1)
                else:
                    pe.wait_ge(sem("fuse_act"), ab + 2)
                    pe.wait_ge(sem("fuse_dve"), ab + 2)
                    for g in range(2):
                        dst = bank()
                        for q in range(8):
                            for half in range(2):
                                last = mm(dst[:, q * C:(q + 1) * C], rKqT[:, half, 8 * g + q, :], RFv[:, 8 * g + q, half, :],
                                          start=(half == 0), stop=(half == 1))
                        last.then_inc(sem("fuse_done"), 1)
                    pe.wait_ge(sem("fuse_act"), ab + 5)
                    pe.wait_ge(sem("fuse_dve"), ab + 5)
                    for k in range(KD):
                        for g in range(2):
                            dst = bank()
                            for q in range(8):
                                last = mm(dst[:, q * C:(q + 1) * C], rWq[:, 8 * g + q, k * P:(k + 1) * P], GF[:, 8 * g + q, :],
                                          start=True, stop=True)
                            last.then_inc(sem("fuse_done"), 1)
                pe.wait_ge(sem("fuse_act"), (12, 19)[l])
                pe.wait_ge(sem("fuse_dve"), (12, 19)[l])

            def attention(l, lnk):
                fuse(l)
                ln_transposes(lnk)

                def at(name, value):
                    if not isinstance(value, int) or value > 0:
                        pe.wait_ge(sem(name), value)

                def step(b, h):
                    hb, pb = b * H + l * B * H, b * 8 + l * B * 8
                    inside = lambda m: not isinstance(b, int) or 0 <= b * H + m < B * H

                    def cols(m):
                        bb = b + m // H
                        return slice(bb * S, bb * S + S) if isinstance(b, int) else bass.ds(bb * S, S)

                    m = h + 2
                    if l == 0 and inside(m):
                        at("rope_done", hb + (m + 1))
                        if m % 2 == 0:
                            at("qc_copied", pb + m // 2)
                        for half in range(2):
                            last = mm(PB[4][(m % 2) * C:(m % 2 + 1) * C, 0:S], RFv[:, m % H, half, :], qr[:, m % 2, half * S:(half + 1) * S],
                                      start=(half == 0), stop=(half == 1))
                        last.then_inc(sem("qc_done"), 1)
                    m = h + 4
                    if l == 0 and inside(m):
                        at("rope_read", hb + m)
                        for half in range(2):
                            for k in range(KD):
                                last = mm(PB[0][0:CH, half * S:(half + 1) * S], W1[:, k, m % H, half * CH:(half + 1) * CH], XT[:, k, cols(m)],
                                          start=(k == 0), stop=(k == KD - 1))
                        last.then_inc(sem("qbig_done"), 1)
                    if l == 1 and h % 2 and inside(h + 1):
                        m = (h + 1) // 2
                        at("qc_copied", pb + m)
                        for k in range(KD):
                            last = mm(PB[0][:, 0:S], MF[:, k, (m % 8) * P:(m % 8 + 1) * P], XT[:, k, cols(h + 1)], start=(k == 0), stop=(k == KD - 1))
                        last.then_inc(sem("qc_done"), 1)
                    if inside(h):
                        at("qc_copied", pb + (h // 2 + 1))
                        at("exp_done", hb + (h - 1))
                        if h % H == 0:
                            pe.wait_ge(sem("keys_ready"), b + (l * B + 1))
                        rows = slice((h % 2) * C, (h % 2 + 1) * C)
                        for s in range(2):
                            last = mm(PB[1 + h % 2][:, s * S:(s + 1) * S], qcT[rows, h // 2 % 8, s * P:(s + 1) * P], kvb[rows, :],
                                      start=True, stop=True)
                        last.then_inc(sem("score_done"), 1)
                    m = h - 1
                    if inside(m):
                        at("exp_done", hb + (m + 1))
                        at("pt_copied", hb + m)
                        for k in range(2):
                            for s in range(2):
                                last = nc.tensor.transpose(PB[3][:, k * S + s * P:k * S + (s + 1) * P], Ex[:, m % 2, s, k * P:(k + 1) * P],
                                                           ident[:, :])
                        last.then_inc(sem("pt_done"), 1)
                    m = h - 2
                    if inside(m):
                        at("pt_copied", hb + (m + 1))
                        if m % 2 == 0:
                            at("cc_done", pb + m // 2)
                        if m % H == 0:
                            pe.wait_ge(sem("values_ready"), b + (l * B + 1))
                        for s in range(2):
                            o = ((m % 2) * 2 + s) * (C + 1)
                            for k in range(2):
                                last = mm(PB[5][:, o:o + C + 1], PT[:, m % 2, k, s * P:(s + 1) * P], kvab[:, k, :],
                                          start=(k == 0), stop=(k == 1))
                        last.then_inc(sem("pv_done"), 1)
                    if h % 2 == 0 and inside(h - 4):
                        m = (h - 4) // 2
                        at("cc_done", pb + (m + 1))
                        at("cct_copied", pb + m)
                        for s in range(2):
                            last = nc.tensor.transpose(PB[6][:, s * P:(s + 1) * P], CC[:, m % 2, s, :], ident[:, :])
                        last.then_inc(sem("cct_done"), 1)
                    if h % 2 and inside(h - 5):
                        m = (h - 5) // 2
                        at("cct_copied", pb + (m + 1))
                        if m == 0:
                            at("y_added", b + l * B)
                        for s in range(2):
                            last = mm(PB[7][:, s * D:(s + 1) * D], CCT[:, m % 2, s * P:(s + 1) * P], PF[:, m % 8, :],
                                      start=(m % 8 == 0 and s == 0), stop=False, skip_group_check=True)
                        last.then_inc(sem("y_done"), 1)

                for h in range(-4, H):
                    step(0, h)
                with pe.Fori(1, B - 1) as b:
                    for h in range(H):
                        step(b, h)
                for h in range(H + 4):
                    step(B - 1, h)

            def quantized():
                xqT = [PB[k][:, :].bitcast(BF16) for k in range(KD)]
                pe.wait_ge(sem("xq_ready"), 1)
                for k in range(KD):
                    for t in range(T):
                        last = nc.tensor.transpose(xqT[k][:, t * P:(t + 1) * P], XQ[:, t, k * P:(k + 1) * P], identb[:, :])
                    last.then_inc(sem("xqT_done"), 1)
                pe.wait_ge(sem("xqT_copied"), 2)
                pe.wait_ge(sem("wq_ready"), 3)

                def gate_up(t):
                    if not isinstance(t, int):
                        pe.wait_ge(sem("q_silu"), t * 2)
                        pe.wait_ge(sem("q_h"), t * 2)
                    tok = slice(0, P) if isinstance(t, int) else bass.ds(t * P, P)
                    for m in range(2):
                        for c in range(2):
                            for k in range(KD):
                                last = mm(PB[2 * m + c][:, :], XQT[:, k, tok], WB[:, m, k * I1 + c * 512:k * I1 + c * 512 + 512],
                                          start=(k == 0), stop=(k == KD - 1))
                            last.then_inc(sem("q_gu"), 1)

                def down(t, one):
                    hT = PB[4][:, :].bitcast(BF16)
                    pe.wait_ge(sem("q_quant"), t + one)
                    for c in range(8):
                        last = nc.tensor.transpose(hT[:, c * P:(c + 1) * P], hqb[:, c * P:(c + 1) * P], identb[:, :])
                    last.then_inc(sem("q_T"), 1)
                    pe.wait_ge(sem("q_Tcopied"), t + one)
                    pe.wait_ge(sem("q_bank_free"), t)
                    for c in range(8):
                        last = mm(PB[5 + 0][:, 0:D], hqT[:, c * P:(c + 1) * P], WB[:, 2, c * D:(c + 1) * D], start=(c == 0), stop=(c == 7))
                    last.then_inc(sem("q_down"), 1)

                gate_up(0)
                with pe.Fori(1, T) as t:
                    gate_up(t)
                    down(t, 0)
                down(T, 0)

            def small_experts(lnk):
                ln_transposes(lnk)
                for t in range(T):
                    for k in range(KD):
                        last = mm(PB[4][:, t * E2:(t + 1) * E2], XT[:, k, t * P:(t + 1) * P], wr2[:, k * E2:(k + 1) * E2],
                                  start=(k == 0), stop=(k == KD - 1))
                last.then_inc(sem("logits2"), 1)
                pe.wait_ge(sem("w2_loaded"), 32)
                for t in range(T):
                    for k in range(KD):
                        last = mm(PB[5 + t // 4][:, (t % 4) * P:(t % 4 + 1) * P], XT[:, k, t * P:(t + 1) * P], w2d[:, k, :],
                                  start=(k == 0), stop=(k == KD - 1))
                    if t % 4 == 3:
                        last.then_inc(sem("h2_done"), 1)
                pe.wait_ge(sem("a2_ready"), 1)
                for t in range(T):
                    last = nc.tensor.transpose(PB[t // 4][:, (t % 4) * P:(t % 4 + 1) * P], a2[:, t, :], ident[:, :])
                    if t % 4 == 3:
                        last.then_inc(sem("a2T_done"), 1)
                pe.wait_ge(sem("a2T_copied"), 2)
                for t in range(T):
                    last = mm(PB[4 + t // 2][:, (t % 2) * D:(t % 2 + 1) * D], a2T[:, t * P:(t + 1) * P], w2u, start=True, stop=True)
                    if t % 2:
                        last.then_inc(sem("y2_done"), 1)

            def adjacency():
                pe.wait_ge(sem("a_kept"), 1)
                for b in range(B):
                    for r in range(2):
                        for c in range(2):
                            last = nc.tensor.transpose(PB[b][:, r * S + c * P:r * S + (c + 1) * P], A[:, 2 * b + c, r * P:(r + 1) * P], ident[:, :])
                    last.then_inc(sem("aT_done"), 1)

            context()
            l0_attention()
            if stages >= 2:
                ffn(0, 1)
            if stages >= 3:
                attention(0, 2)
            if stages >= 4:
                quantized()
            if stages >= 5:
                pe.wait_ge(sem("stage_done"), 4)
                adjacency()
            if stages >= 6:
                small_experts(3)
            if stages >= 7:
                attention(1, 4)
            if stages >= 8:
                ffn(1, 5)

        @block.vector
        def _(dve):
            v = nc.vector
            link = Chain(dve, sem("dve_chain"))
            stage = [0]

            def done(ins):
                stage[0] += 1
                ins.then_inc(sem("stage_done"), 1)
                dve.wait_ge(sem("stage_done"), stage[0])

            def normalize(k, lnk):
                for t in range(T):
                    v.bn_stats(st6[:, t, :], X[:, t, :]).then_inc(sem("dve_stats"), 1)
                for t in range(T):
                    dve.wait_ge(sem("dve_stats"), 8 * k + t + 1)
                    last = v.bn_aggr(mv[:, t, :], st6[:, t, :])
                last.then_inc(sem("ln_stat"), 1)
                dve.wait_ge(sem("ln_std"), k + 1)
                link(v.reciprocal(rstd[:, :], rstd[:, :]))
                for t in range(T):
                    last = v.tensor_scalar(XN[:, t, :], X[:, t, :], mv[:, t, 0:1], rstd[:, t:t + 1], ALU.subtract, ALU.mult)
                    if lnk is not None:
                        last.then_inc(sem("ln_x"), 1)
                if lnk is None:
                    return link(last)
                for kk in range(KD):
                    dve.wait_ge(sem("ln_T"), 4 * lnk + 3 + kk)
                    v.tensor_copy(XT[:, kk, 512:1024], PB[2 + kk][:, :]).then_inc(sem("xt_dve"), 1)

            def context():
                v.memset(ones[:, :], 1.0).then_inc(sem("dve_chain"), 1); link.at += 1
                v.memset(epsc[:, 0:1], 1e-5).then_inc(sem("eps_set"), 1)
                v.memset(epsc[:, 1:2], 1e-6).then_inc(sem("eps_set"), 1)
                v.memset(ctxT[C:C + 1, :], 1.0).then_inc(sem("ctx_ones"), 1)
                v.memset(kvaug[:, :, C:C + 1], 1.0)
                dve.wait_ge(sem("consts_loaded"), 16 * 11)
                bc = lambda ap: ap.unsqueeze(1).to_broadcast([P, B, 2, ap.shape[-1]])
                c4 = ctok[:, :, :].rearrange("p (b s) c -> p b s c", b=B)
                k1 = kt1.rearrange("p (b s) c -> p b s c", b=B)
                k2 = kt2.rearrange("p (b s) c -> p b s c", b=B)
                v.tensor_tensor(k1, c4, bc(ropek[:, 0, :, :]), ALU.mult)
                v.tensor_tensor(k2[:, :, :, 0:32], c4[:, :, :, 32:64], bc(ropek[:, 1, :, 0:32]), ALU.mult)
                link(v.tensor_tensor(k2[:, :, :, 32:64], c4[:, :, :, 0:32], bc(ropek[:, 1, :, 32:64]), ALU.mult))
                v.tensor_tensor(kvaug[:, :, 0:C], kt1, kt2, ALU.add)
                v.tensor_tensor(kvdup[:, :, 0, :], kt1, kt2, ALU.add)
                v.tensor_tensor(kvdup[:, :, 1, :], kt1, kt2, ALU.add).then_inc(sem("kvr_ready"), 1)
                dve.wait_ge(sem("n2_done"), 1)
                v.tensor_copy(n2, PB[3][0:C, 0:C]).then_inc(sem("n2_copied"), 1)
                dve.wait_ge(sem("kv_done"), 1)
                v.tensor_copy(kv0, PB[2][:, 0:T * C].rearrange("p (t c) -> p t c", t=T)).then_inc(sem("kv_copied"), 1)
                for n in range(2):
                    dve.wait_ge(sem("uT_done"), n + 1)
                    v.tensor_copy(uT[:, n * 512:(n + 1) * 512], PB[4 + n][0:C, :]).then_inc(sem("uT_copied"), 1)
                for b in range(B):
                    dve.wait_ge(sem("sim_done"), b + 1)
                    v.tensor_copy(SIM[:, 2 * b:2 * b + 2, :], PB[b][:, :].rearrange("p (s l) -> p s l", s=2)).then_inc(sem("sim_copied"), 1)

            def l0_attention():
                normalize(0, 0)
                for b in range(B):
                    dve.wait_ge(sem("l0_sim"), b + 1)
                    for s in range(2):
                        v.bn_stats(st6[:, 2 * b + s, :], PB[b][:, s * S:(s + 1) * S]).then_inc(sem("l0_stats"), 1)
                for t in range(T):
                    dve.wait_ge(sem("l0_stats"), t + 1)
                    last = v.bn_aggr(mv[:, t, :], st6[:, t, :])
                last.then_inc(sem("l0_stat"), 1)
                dve.wait_ge(sem("l0_std"), 1)
                link(v.reciprocal(rstd[:, :], rstd[:, :]))
                for t in range(T):
                    last = v.tensor_scalar(XN[:, t, :], PB[t // 2][:, (t % 2) * S:(t % 2 + 1) * S], mv[:, t, 0:1],
                                           rstd[:, t:t + 1], ALU.subtract, ALU.mult)
                link(last)
                g8 = gam.unsqueeze(1).to_broadcast([P, T, D])
                b8 = bet.unsqueeze(1).to_broadcast([P, T, D])
                link(v.tensor_tensor(XN[:, :, :], XN[:, :, :], g8, ALU.mult))
                link(v.tensor_tensor(XN[:, :, :], XN[:, :, :], b8, ALU.add))
                link(v.tensor_reduce(sc8[:, 0, :], XN[:, :, :], AX.X, ALU.max))
                v.tensor_tensor(XN[:, :, :], XN[:, :, :], sc8[:, 0, :].unsqueeze(2).to_broadcast([P, T, D]), ALU.subtract)\
                    .then_inc(sem("l0_shift"), 1)
                dve.wait_ge(sem("l0_exp"), 1)
                link(v.tensor_reduce(sc8[:, 1, :], XN[:, :, :], AX.X, ALU.add))
                link(v.reciprocal(sc8[:, 2, :], sc8[:, 1, :]))
                for t in range(T):
                    last = v.scalar_tensor_tensor(X[:, t, :], XN[:, t, :], sc8[:, 2, t:t + 1], X[:, t, :], ALU.mult, ALU.add)
                done(last)

            def scores(f):
                lg = PB[0][:, 0:T * EX].rearrange("p (t e) -> p t e", t=T)
                over = lambda col: col.unsqueeze(2).to_broadcast([P, T, E])
                dve.wait_ge(sem("logits"), f + 1)
                link(v.tensor_reduce(sc8[:, 0, :], lg[:, :, 0:E], AX.X, ALU.max))
                v.tensor_tensor(pm[:, :, 0:E], lg[:, :, 0:E], over(sc8[:, 0, :]), ALU.subtract)
                v.tensor_scalar(pm[:, :, E:EX], lg[:, :, E:EX], -1.0, None, ALU.mult).then_inc(sem("logits_shifted"), 1)
                dve.wait_ge(sem("logits_exp"), f + 1)
                v.tensor_scalar(pm[:, :, E:EX], pr[:, :, E:EX], 1.0, None, ALU.add)
                link(v.tensor_reduce(sc8[:, 0, :], pr[:, :, 0:E], AX.X, ALU.add))
                link(v.reciprocal(sc8[:, 1, :], sc8[:, 0, :]))
                link(v.tensor_tensor(pk[:, :, :], pr[:, :, 0:E], over(sc8[:, 1, :]), ALU.mult))
                for t in range(T):
                    last = v.max(top8[:, t, :], pk[:, t, :])
                link(last)
                for t in range(T):
                    last = v.max_index(idx8[:, t, :], top8[:, t, :], pk[:, t, :])
                link(last)
                link(v.tensor_copy(idf[:, :, :], idx8[:, :, :]))
                dve.wait_ge(sem("router_loaded"), 64)
                io = iote[:, :].unsqueeze(1).to_broadcast([P, T, E])
                link(v.tensor_tensor(pm[:, :, 0:E], io, over(idf[:, :, 0]), ALU.is_equal))
                for c in range(1, TOPK):
                    link(v.tensor_tensor(pq[:, :, :], io, over(idf[:, :, c]), ALU.is_equal))
                    link(v.tensor_tensor(pm[:, :, 0:E], pm[:, :, 0:E], pq[:, :, :], ALU.add))
                link(v.tensor_tensor(pr[:, :, 0:E], pm[:, :, 0:E], pk[:, :, :], ALU.mult))
                if f == 1:
                    link(v.tensor_reduce(sc8[:, 0, :], pr[:, :, 0:E], AX.X, ALU.add))
                    link(v.tensor_scalar(sc8[:, 0, :], sc8[:, 0, :], 1e-9, None, ALU.max))
                    link(v.reciprocal(sc8[:, 1, :], sc8[:, 0, :]))
                    link(v.tensor_tensor(pr[:, :, 0:E], pr[:, :, 0:E], over(sc8[:, 1, :]), ALU.mult))
                link(v.reciprocal(pr[:, :, E:EX], pm[:, :, E:EX]))
                link(v.tensor_copy(scp[:, :, 0, :], pr))
                link(v.tensor_tensor(pr, pr, scp[:, :, 0, :], ALU.subtract))
                link(v.tensor_copy(scp[:, :, 1, :], pr))
                link(v.tensor_tensor(pr, pr, scp[:, :, 1, :], ALU.subtract))
                v.tensor_copy(scp[:, :, 2, :], pr).then_inc(sem("scores_split"), 1)
                dve.wait_ge(sem("scoresT"), f + 1)
                v.tensor_copy(SCT, PB[1][0:3 * EX, :].bitcast(BF16)).then_inc(sem("scoresT_copied"), 1)

            PER_TILE = 2 * ((KEEP - 1) // 8) + 3

            def keep_neighbours(t, u):
                row = bass.ds(t, 1) if not isinstance(t, int) else slice(t, t + 1)
                spacer = lambda: v.tensor_copy(small[:, 9:10], small[:, 0:1])
                rounds = (KEEP - 1) // 8
                if u == 0:
                    link(v.tensor_copy(twork.unsqueeze(1), SIM[:, row, :]))
                for _ in range(2 if u < rounds // 2 else rounds % 2 if u == rounds // 2 else 0):
                    spacer()
                    link(v.max(tmax, twork))
                    spacer()
                    link(v.match_replace(twork, tmax, twork, -BIG))
                if u == 7:
                    spacer()
                    link(v.max(tmax, twork))
                    last_kept = (KEEP - 1) % 8
                    link(v.scalar_tensor_tensor(A[:, row, :], SIM[:, row, :], tmax[:, last_kept:last_kept + 1], A[:, row, :],
                                                ALU.is_ge, ALU.mult))

            def ffn(f, stage, lnk):
                normalize(stage, lnk)
                scores(f)
                base = f * 8 * LOOP
                if f == 0:
                    dve.wait_ge(sem("sim_sigmoid"), 1)

                def unit(i, u):
                    n = i * 8 + (u + base)
                    first = isinstance(i, int)
                    dve.wait_ge(sem("silu_done"), n + 1)
                    dve.wait_ge(sem("up_done"), n + 1)
                    v.tensor_tensor(tmu[:, u % 2, :], sil[:, u % 2, :], PB[2 + u % 2][:, :], ALU.mult).then_inc(sem("t_done"), 1)
                    dve.wait_ge(sem("t_done"), n + 1)
                    dve.wait_ge(sem("spread_done"), n + 1)
                    if not (first and u < 4):
                        dve.wait_ge(sem("down_done"), n - 3)
                    v.tensor_tensor(HT[:, u % 4, :], tmu[:, u % 2, :], PB[u % 2][:, :], ALU.mult).then_inc(sem("h_done"), 1)
                    if f == 0:
                        if first:
                            keep_neighbours(0, u)
                        else:
                            keep_neighbours(i, u)

                for u in range(8):
                    unit(0, u)
                with dve.Fori(1, LOOP) as i:
                    if f == 0:
                        link.enter(i, 1, PER_TILE)
                    for u in range(8):
                        unit(i, u)
                if f == 0:
                    link.leave(LOOP - 1)
                    for t in range(LOOP, T):
                        for u in range(8):
                            keep_neighbours(t, u)
                dve.wait_ge(sem("down_done"), 8 * LOOP * (f + 1))
                for q in range(4):
                    xs = X[:, 2 * q:2 * q + 2, :]
                    last = v.tensor_tensor(xs, xs, PB[4 + q][:, :].rearrange("p (s d) -> p s d", s=2), ALU.add)
                done(last)

            def fuse(l):
                base, ab = (0, 24)[l], 0
                for n in range(1, (24, 14)[l], 2):
                    dve.wait_ge(sem("fuse_done"), base + n + 1)
                    fuse_copy(l, n, v.tensor_copy).then_inc(sem("fuse_dve"), 1)

            def attention(l, stage_, lnk):
                fuse(l)
                normalize(stage_, lnk)
                if l == 0:
                    dve.wait_ge(sem("rope_loaded"), 32)

                def at(name, value):
                    if not isinstance(value, int) or value > 0:
                        dve.wait_ge(sem(name), value)

                def step(b, h):
                    hb, pb = b * H + l * B * H, b * 8 + l * B * 8
                    inside = lambda m: not isinstance(b, int) or 0 <= b * H + m < B * H
                    m = h + 4
                    if l == 0 and inside(m):
                        at("qbig_done", hb + (m + 1))
                        at("rope_done", hb + (m - 1))
                        v.tensor_tensor(r1[:, m % 2, :], PB[0][0:CH, :], cosq, ALU.mult)
                        v.tensor_tensor(r2[:, m % 2, :], PB[0][0:CH, :], sinq, ALU.mult).then_inc(sem("rope_read"), 1)
                    if inside(h):
                        at("score_done", hb + (h + 1))
                        at("exp_done", hb + (h - 3))
                        v.tensor_reduce(nmx[:, h % 4, :], PB[1 + h % 2][:, :].rearrange("p (s l) -> p s l", s=2), AX.X, ALU.max,
                                        negate=True).then_inc(sem("max_done"), 1)
                    m = h - 1
                    if inside(m):
                        at("pt_done", hb + (m + 1))
                        at("pv_done", hb + (m - 1))
                        v.tensor_copy(PT[:, m % 2, :, :], PB[3][:, :].rearrange("p (l s) -> p l s", l=2)).then_inc(sem("pt_copied"), 1)
                    if h % 2 and inside(h - 3):
                        m = (h - 3) // 2
                        at("pv_done", hb + (2 * m + 2))
                        at("cct_done", pb + (m - 1))
                        o4 = PB[5][:, 0:4 * (C + 1)].rearrange("p (q c) -> p q c", q=4)
                        v.reciprocal(rin[:, m % 2, :], o4[:, :, C]).then_inc(sem("rin_done"), 1)
                        dve.wait_ge(sem("rin_done"), pb + (m + 1))
                        v.tensor_tensor(CC[:, m % 2, :, :].rearrange("p s (h c) -> p h s c", h=2),
                                        o4[:, :, 0:C].rearrange("p (h s) c -> p h s c", h=2),
                                        rin[:, m % 2, :].rearrange("p (h s) -> p h s", h=2).unsqueeze(3).to_broadcast([P, 2, 2, C]),
                                        ALU.mult).then_inc(sem("cc_done"), 1)
                    if (h - 4) % H == 0 and inside(h - 5):
                        bb = b + (h - 5) // H
                        at("y_done", pb + 8 * ((h - 4) // H))
                        xs = X[:, 2 * bb:2 * bb + 2, :] if isinstance(b, int) else X[:, bass.ds(bb * 2, 2), :]
                        v.tensor_tensor(xs, xs, PB[7][:, :].rearrange("p (s d) -> p s d", s=2), ALU.add).then_inc(sem("y_added"), 1)

                for h in range(-4, H):
                    step(0, h)
                with dve.Fori(1, B - 1) as b:
                    for h in range(H):
                        step(b, h)
                for h in range(H + 5):
                    step(B - 1, h)
                    if l == 0 and stages >= 4 and 2 <= h < 11:
                        m, part = divmod(h - 2, 3)
                        w = rF[:, m, :]
                        if part == 0:
                            dve.wait_ge(sem("winv_ready"), 1)
                            v.tensor_scalar(w, w, winv[:, m:m + 1], -1.0, ALU.mult, ALU.max).then_inc(sem("wq_part"), 1)
                        elif part == 1:
                            dve.wait_ge(sem("wq_part"), 2 * m + 1)
                            v.tensor_scalar(w, w, 1.0, RNE, ALU.min, ALU.add).then_inc(sem("wq_part"), 1)
                        else:
                            dve.wait_ge(sem("wq_part"), 2 * m + 2)
                            v.tensor_scalar(WB[:, m, :], w, RNE, None, ALU.subtract).then_inc(sem("wq_ready"), 1)
                dve.wait_ge(sem("y_added"), B * (l + 1))
                done(v.tensor_copy(small[:, 8:9], small[:, 0:1]))

            def quantized():
                normalize(3, None)
                link(v.tensor_reduce(amax, XN[:, :, :], AX.X, ALU.max, apply_absolute_value=True))
                link(v.tensor_scalar(xs8, amax, 1.0 / 127.0, 1e-5, ALU.mult, ALU.add))
                link(v.reciprocal(xr8, xs8))
                for t in range(T):
                    last = v.tensor_scalar(qt[:, t * D:(t + 1) * D], XN[:, t, :], xr8[:, t:t + 1], -128.0, ALU.mult, ALU.max)
                link(last)
                link(v.tensor_scalar(qt, qt, 127.0, RNE, ALU.min, ALU.add))
                v.tensor_scalar(XQ.rearrange("p t d -> p (t d)"), qt, RNE, None, ALU.subtract).then_inc(sem("xq_ready"), 1)
                dve.wait_ge(sem("w_scales"), 1)
                v.tensor_scalar(sg8, xs8, wsum[:, 0:1], None, ALU.mult).then_inc(sem("q_bank_free"), 1)
                link(v.tensor_scalar(su8, xs8, wsum[:, 1:2], None, ALU.mult))
                dve.wait_ge(sem("xqT_done"), 2)
                v.tensor_copy(XQT[:, 1, :], PB[1][:, :].bitcast(BF16)).then_inc(sem("xqT_copied"), 1)

                def col(ap, t):
                    return ap[:, t:t + 1] if isinstance(t, int) else ap[:, bass.ds(t, 1)]

                def hidden(t):
                    v.tensor_scalar(sgc, col(sg8, t), 1.0, None, ALU.mult).then_inc(sem("q_scale"), 1)
                    for c in range(2):
                        dve.wait_ge(sem("q_silu"), t * 2 + (c + 1))
                        dve.wait_ge(sem("q_gu"), t * 4 + (3 + c))
                        last = v.scalar_tensor_tensor(hq[:, c * 512:(c + 1) * 512], PB[2 + c][:, :], col(su8, t), silq[:, c * 512:(c + 1) * 512],
                                                      ALU.mult, ALU.mult)
                        last.then_inc(sem("q_h"), 1)
                    dve.wait_ge(sem("q_h"), t * 2 + 2)
                    link(v.tensor_reduce(hs[:, 0:1], hq, AX.X, ALU.max, apply_absolute_value=True))
                    link(v.tensor_scalar(hs[:, 1:2], hs[:, 0:1], 1.0 / 127.0, 1e-5, ALU.mult, ALU.add))
                    v.tensor_scalar(col(ys8, t), hs[:, 1:2], wsum[:, 2:3], None, ALU.mult)
                    link(v.reciprocal(hs[:, 2:3], hs[:, 1:2]))
                    link(v.tensor_scalar(hq, hq, hs[:, 2:3], -128.0, ALU.mult, ALU.max))
                    link(v.tensor_scalar(hq, hq, 127.0, RNE, ALU.min, ALU.add))
                    if not isinstance(t, int):
                        dve.wait_ge(sem("q_T"), t)
                    v.tensor_scalar(hqb, hq, RNE, None, ALU.subtract).then_inc(sem("q_quant"), 1)

                def add(t, before):
                    dve.wait_ge(sem("q_down"), t + 1 - before)
                    xs = X[:, t:t + 1, :] if isinstance(t, int) else X[:, bass.ds(t - before, 1), :]
                    ysc = ys8[:, t:t + 1] if isinstance(t, int) else ys8[:, bass.ds(t - before, 1)]
                    last = v.scalar_tensor_tensor(xs, PB[5][:, 0:D].unsqueeze(1), ysc, xs, ALU.mult, ALU.add)
                    return last

                hidden(0)
                with dve.Fori(1, T) as t:
                    link.enter(t, 1, 5)
                    hidden(t)
                    add(t, 1).then_inc(sem("q_bank_free"), 1)
                link.leave(T - 1)
                done(add(T - 1, 0))

            def adjacency():
                normalize(4, None)
                v.tensor_scalar(small[:, 4:5], small[:, 3:4], -1.0, 1.0, ALU.mult, ALU.add)
                link(v.tensor_scalar(small[:, 5:6], small[:, 3:4], 0.5, None, ALU.mult))
                for b in range(B):
                    dve.wait_ge(sem("aT_done"), b + 1)
                    ab = A[:, 2 * b:2 * b + 2, :]
                    last = v.tensor_tensor(ab, ab, PB[b][:, :].rearrange("p (s l) -> p s l", s=2), ALU.add)
                link(last)
                link(v.scalar_tensor_tensor(X[:, :, :], XN[:, :, :], small[:, 4:5], X[:, :, :], ALU.mult, ALU.add))
                done(v.scalar_tensor_tensor(X[:, :, :], A[:, :, :], small[:, 5:6], X[:, :, :], ALU.mult, ALU.add))

            def small_experts(lnk):
                normalize(5, lnk)
                lg = PB[4][:, 0:T * E2].rearrange("p (t e) -> p t e", t=T)
                over = lambda col: col.unsqueeze(2).to_broadcast([P, T, E2])
                e8 = slice(0, E2)
                dve.wait_ge(sem("logits2"), 1)
                link(v.tensor_reduce(sc8[:, 0, :], lg, AX.X, ALU.max))
                v.tensor_tensor(pm[:, :, e8], lg, over(sc8[:, 0, :]), ALU.subtract).then_inc(sem("logits2_shifted"), 1)
                dve.wait_ge(sem("logits2_exp"), 1)
                link(v.tensor_reduce(sc8[:, 0, :], pr[:, :, e8], AX.X, ALU.add))
                link(v.reciprocal(sc8[:, 1, :], sc8[:, 0, :]))
                link(v.tensor_tensor(pk[:, :, e8], pr[:, :, e8], over(sc8[:, 1, :]), ALU.mult))
                for t in range(T):
                    last = v.max(top8[:, t, :], pk[:, t, e8])
                link(last)
                for t in range(T):
                    last = v.max_index(idx8[:, t, :], top8[:, t, :], pk[:, t, e8])
                link(last)
                link(v.tensor_copy(idf[:, :, :], idx8[:, :, :]))
                io = iote[:, e8].unsqueeze(1).to_broadcast([P, T, E2])
                link(v.tensor_tensor(pm[:, :, e8], io, over(idf[:, :, 0]), ALU.is_equal))
                link(v.tensor_tensor(pq[:, :, e8], io, over(idf[:, :, 1]), ALU.is_equal))
                link(v.tensor_tensor(pm[:, :, e8], pm[:, :, e8], pq[:, :, e8], ALU.add))
                link(v.tensor_tensor(pr[:, :, e8], pm[:, :, e8], pk[:, :, e8], ALU.mult))
                dve.wait_ge(sem("silu2_done"), 2)
                a4 = a2.rearrange("p t (e i) -> p t e i", e=E2)
                v.tensor_tensor(a4, a4, pr[:, :, e8].unsqueeze(3).to_broadcast([P, T, E2, IE2]), ALU.mult).then_inc(sem("a2_ready"), 1)
                dve.wait_ge(sem("a2T_done"), 2)
                v.tensor_copy(a2T[:, 512:1024], PB[1][:, :]).then_inc(sem("a2T_copied"), 1)
                for q in range(4):
                    dve.wait_ge(sem("y2_done"), q + 1)
                    xs = X[:, 2 * q:2 * q + 2, :]
                    last = v.tensor_tensor(xs, xs, PB[4 + q][:, :].rearrange("p (s d) -> p s d", s=2), ALU.add)
                done(last)

            context()
            dve.wait_ge(sem("x_loaded"), 16)
            l0_attention()
            if stages >= 2:
                ffn(0, 1, 1)
                v.tensor_copy(small[:, 2:3], small[:, 0:1]).then_inc(sem("a_kept"), 1)
            if stages >= 3:
                attention(0, 2, 2)
            if stages >= 4:
                quantized()
            if stages >= 5:
                adjacency()
            if stages >= 6:
                small_experts(3)
            if stages >= 7:
                attention(1, 6, 4)
            if stages >= 8:
                ffn(1, 7, 5)
            v.tensor_copy(small[:, 2:3], small[:, 0:1]).then_inc(sem("x_final"), 1)

        @block.scalar
        def _(act):
            sc = nc.scalar

            def normalize(k, lnk):
                act.wait_ge(sem("ln_stat"), k + 1)
                sc.activation(rstd[:, :], mv[:, :, 1], ACT.Sqrt, bias=epsc[:, 0:1]).then_inc(sem("ln_std"), 1)
                for kk in range(KD if lnk is not None else 0):
                    act.wait_ge(sem("ln_T"), 4 * lnk + 1 + kk)
                    sc.copy(XT[:, kk, 0:512], PB[kk][:, :]).then_inc(sem("xt_act"), 1)

            def context():
                for n in range(2):
                    act.wait_ge(sem("kvT_done"), n + 1)
                    sc.copy(kvT0[:, n * 512:(n + 1) * 512], PB[n][0:C, :]).then_inc(sem("kvT_copied"), 1)
                for n in range(2):
                    act.wait_ge(sem("kvrT_done"), n + 1)
                    sc.copy(kvrT[:, n * 512:(n + 1) * 512], PB[6 + n][:, :]).then_inc(sem("kvrT_copied"), 1)
                act.wait_ge(sem("sim_copied"), 4)
                sc.activation(A[:, :, :], SIM[:, :, :], ACT.Sigmoid, scale=1.0 / 16.0).then_inc(sem("sim_sigmoid"), 1)
                act.wait_ge(sem("consts_loaded"), 16 * 11)
                sc.activation(small[:, 3:4], small[:, 0:1], ACT.Sigmoid)

            def l0_attention():
                normalize(0, 0)
                for n in range(2):
                    act.wait_ge(sem("l0_out"), n + 1)
                    sc.activation(outT[:, n * 512:(n + 1) * 512], PB[4 + n][0:C, :], ACT.Copy, scale=D ** -0.5).then_inc(sem("l0_out_copied"), 1)
                act.wait_ge(sem("l0_stat"), 1)
                sc.activation(rstd[:, :], mv[:, :, 1], ACT.Sqrt, bias=epsc[:, 1:2]).then_inc(sem("l0_std"), 1)
                act.wait_ge(sem("l0_shift"), 1)
                sc.activation(XN[:, :, :], XN[:, :, :], ACT.Exp).then_inc(sem("l0_exp"), 1)

            def ffn(f, stage, lnk):
                normalize(stage, lnk)
                act.wait_ge(sem("logits_shifted"), f + 1)
                sc.activation(pr[:, :, :], pm[:, :, :], ACT.Exp).then_inc(sem("logits_exp"), 1)
                base = f * 8 * LOOP

                def unit(i, u):
                    n = i * 8 + (u + base)
                    act.wait_ge(sem("gate_done"), n + 1)
                    if not (isinstance(i, int) and u < 2):
                        act.wait_ge(sem("t_done"), n - 1)
                    sc.activation(sil[:, u % 2, :], PB[u % 2][:, :], ACT.Silu).then_inc(sem("silu_done"), 1)

                for u in range(8):
                    unit(0, u)
                with act.Fori(1, LOOP) as i:
                    for u in range(8):
                        unit(i, u)

            def fuse(l):
                base = (0, 24)[l]
                for n in range(0, (24, 14)[l], 2):
                    act.wait_ge(sem("fuse_done"), base + n + 1)
                    fuse_copy(l, n, sc.copy).then_inc(sem("fuse_act"), 1)

            def attention(l, stage, lnk):
                fuse(l)
                normalize(stage, lnk)

                def at(name, value):
                    if not isinstance(value, int) or value > 0:
                        act.wait_ge(sem(name), value)

                def step(b, h):
                    hb, pb = b * H + l * B * H, b * 8 + l * B * 8
                    inside = lambda m: not isinstance(b, int) or 0 <= b * H + m < B * H
                    if h % 2 and inside(h + 1):
                        m = (h + 1) // 2
                        at("qc_done", (hb + (2 * m + 2)) if l == 0 else (pb + (m + 1 + B * 8)))
                        src = PB[4] if l == 0 else PB[0]
                        sc.copy(qcT[:, m % 8, :], src[:, 0:S]).then_inc(sem("qc_copied"), 1)
                    if inside(h):
                        at("max_done", hb + (h + 1))
                        at("pt_done", hb + (h - 1))
                        for s in range(2):
                            last = sc.activation(Ex[:, h % 2, s, :], PB[1 + h % 2][:, s * S:(s + 1) * S], ACT.Exp, bias=nmx[:, h % 4, s:s + 1])
                        last.then_inc(sem("exp_done"), 1)
                    if h % 2 == 0 and inside(h - 4):
                        m = (h - 4) // 2
                        at("cct_done", pb + (m + 1))
                        at("y_done", pb + (m - 1))
                        sc.copy(CCT[:, m % 2, :], PB[6][:, 0:S]).then_inc(sem("cct_copied"), 1)

                for h in range(-4, H):
                    step(0, h)
                    if l == 0 and stages >= 4 and h in (9, 11, 13):
                        m = (h - 9) // 2
                        act.wait_ge(sem("w1ffn_loaded"), 16)
                        sc.activation(WB[:, m, :], rF[:, m, :], ACT.Abs, accum_out=wsum[:, m:m + 1]).then_inc(sem("w_abs"), 1)
                with act.Fori(1, B - 1) as b:
                    for h in range(H):
                        step(b, h)
                for h in range(H + 4):
                    step(B - 1, h)

            def quantized():
                normalize(3, None)
                act.wait_ge(sem("xqT_done"), 1)
                sc.copy(XQT[:, 0, :], PB[0][:, :].bitcast(BF16)).then_inc(sem("xqT_copied"), 1)

                def gate(t):
                    act.wait_ge(sem("q_scale"), t + 1)
                    if not isinstance(t, int):
                        act.wait_ge(sem("q_h"), t * 2)
                    for c in range(2):
                        act.wait_ge(sem("q_gu"), t * 4 + (c + 1))
                        sc.activation(silq[:, c * 512:(c + 1) * 512], PB[c][:, :], ACT.Silu, scale=sgc).then_inc(sem("q_silu"), 1)

                def copy(t):
                    act.wait_ge(sem("q_T"), t)
                    sc.copy(hqT, PB[4][:, :].bitcast(BF16)).then_inc(sem("q_Tcopied"), 1)

                gate(0)
                with act.Fori(1, T) as t:
                    gate(t)
                    copy(t)
                copy(T)

            def small_experts(lnk):
                normalize(5, lnk)
                act.wait_ge(sem("logits2_shifted"), 1)
                sc.activation(pr[:, :, 0:E2], pm[:, :, 0:E2], ACT.Exp).then_inc(sem("logits2_exp"), 1)
                for n in range(2):
                    act.wait_ge(sem("h2_done"), n + 1)
                    sc.activation(a2[:, 4 * n:4 * n + 4, :], PB[5 + n][:, :].rearrange("p (t n) -> p t n", t=4), ACT.Silu)\
                        .then_inc(sem("silu2_done"), 1)
                act.wait_ge(sem("a2T_done"), 1)
                sc.copy(a2T[:, 0:512], PB[0][:, :]).then_inc(sem("a2T_copied"), 1)

            context()
            act.wait_ge(sem("eps_set"), 2)
            l0_attention()
            if stages >= 2:
                ffn(0, 1, 1)
            if stages >= 3:
                attention(0, 2, 2)
            if stages >= 4:
                quantized()
            if stages >= 5:
                normalize(4, None)
            if stages >= 6:
                small_experts(3)
            if stages >= 7:
                attention(1, 6, 4)
            if stages >= 8:
                ffn(1, 7, 5)

        @block.gpsimd
        def _(pool):
            g = nc.gpsimd
            g.memset(neg1[:, :], -1.0).then_inc(sem("neg1_set"), 1)

            def attention(l):
                pool.wait_ge(sem("stage_done"), (2, 6)[l])

                def at(name, value):
                    if not isinstance(value, int) or value > 0:
                        pool.wait_ge(sem(name), value)

                def step(b, h):
                    hb, pb = b * H + l * B * H, b * 8 + l * B * 8
                    inside = lambda m: not isinstance(b, int) or 0 <= b * H + m < B * H
                    m = h + 4
                    if l == 0 and inside(m):
                        at("rope_read", hb + (m + 1))
                        at("qc_done", hb + (m - 1))
                        for half in range(2):
                            lo, hi = slice(half * S, half * S + S), slice((1 - half) * S, (1 - half) * S + S)
                            last = g.tensor_tensor(qr[:, m % 2, lo], r1[:, m % 2, lo], r2[:, m % 2, hi], ALU.add)
                        last.then_inc(sem("rope_done"), 1)
                    if h == -1 or h == H - 1 and inside(H):
                        bb = b + (h + 1) // H
                        at("score_done", hb + (h + 1))
                        g.tensor_copy(kvb, kvrT[:, bb * S:bb * S + S] if isinstance(b, int) else kvrT[:, bass.ds(bb * S, S)])\
                            .then_inc(sem("keys_ready"), 1)
                    if h == 1:
                        at("pv_done", hb)
                        g.tensor_copy(kvab, kvaug[:, 2 * b:2 * b + 2, :] if isinstance(b, int) else kvaug[:, bass.ds(b * 2, 2), :])\
                            .then_inc(sem("values_ready"), 1)

                for h in range(-4, H):
                    step(0, h)
                if l == 0 and stages >= 4:
                    weight_scales()
                with pool.Fori(1, B - 1) as b:
                    for h in range(H):
                        step(b, h)
                for h in range(H):
                    step(B - 1, h)

            def weight_scales():
                pool.wait_ge(sem("w_abs"), 3)
                pool.wait_ge(sem("neg1_set"), 1)
                g.partition_all_reduce(wtot[:, :], wsum[:, :], P, bass.bass_isa.ReduceOp.add).then_inc(sem("pool_chain"), 1)
                pool.wait_ge(sem("pool_chain"), 1)
                g.tensor_scalar(wsum[:, :], wtot[:, :], 1.0 / (D * I1), 1e-5, ALU.mult, ALU.add).then_inc(sem("w_scales"), 1)
                pool.wait_ge(sem("w_scales"), 1)
                g.tensor_tensor(winv[:, :], wsum[:, :], neg1[:, :], ALU.pow).then_inc(sem("winv_ready"), 1)

            if stages >= 3:
                attention(0)
            if stages >= 7:
                attention(1)


def bf16_of_01(ones):
    return np.where(ones > 0, 0x3F80, 0).astype(np.uint16)


def layouts(i):
    f = lambda n: np.asarray(i[n])
    c = np.ascontiguousarray
    two = lambda w: c(w.reshape(KD, P, w.shape[1]).transpose(1, 0, 2))
    flat2 = lambda w: two(w).reshape(P, -1)
    a = {"x": f("x"), "ctx": f("ctx_512"), "ctxT": c(f("ctx_512").reshape(TOK, C).T)}
    a["wkaug"] = c(np.concatenate([f("L0_xattn_W_k").T, f("L0_xattn_b_k")[None]], 0))
    a["gamma"], a["beta"] = f("L0_xattn_ln_gamma"), f("L0_xattn_ln_beta")
    a["graw"] = f("L2_xattn_gamma_raw").reshape(1)
    a["wq2"], a["wk2"] = f("L2_xattn_Wq"), f("L2_xattn_Wk")
    a["ident"] = np.eye(P, dtype=np.float32)
    a["identb"] = bf16_of_01(np.eye(P))
    a["iote"] = np.arange(E, dtype=np.float32)
    owner = np.concatenate([np.repeat(np.arange(E), FE), np.full(FS, E), np.full(FT * P - E * FE - FS, -1)])
    sel = (owner[None] == np.arange(EX)[:, None]).astype(np.float32)
    a["sel"] = bf16_of_01(np.concatenate([sel] * 3, 0))

    def groups(gate, up, down):
        pad = lambda w: np.concatenate([w, np.zeros((FT * P - w.shape[0], w.shape[1]), w.dtype)], 0)
        gu = [pad(w).reshape(NG, GRP * P, KD, P).transpose(0, 3, 2, 1).reshape(NG, P, KD * GRP * P) for w in (gate, up)]
        dn = pad(down).reshape(NG, GRP, P, D).transpose(0, 2, 1, 3).reshape(NG, P, GRP * D)
        return c(np.concatenate(gu + [dn], 2))

    e2 = lambda w: w.reshape(E * FE, D)
    a["w0"] = groups(np.concatenate([e2(f("L0_ffn_w_gate")), f("L0_ffn_ws_gate")]),
                     np.concatenate([e2(f("L0_ffn_w_up")), f("L0_ffn_ws_up")]),
                     np.concatenate([e2(f("L0_ffn_w_down").transpose(0, 2, 1)), f("L0_ffn_ws_down").T]))
    a["w1"] = groups(np.concatenate([e2(f("L3_ffn_w_gate").transpose(0, 2, 1)), f("L3_ffn_sh_gate").T]),
                     np.concatenate([e2(f("L3_ffn_w_up").transpose(0, 2, 1)), f("L3_ffn_sh_up").T]),
                     np.concatenate([e2(f("L3_ffn_w_down")), f("L3_ffn_sh_down")]))
    a["router0"] = flat2(np.concatenate([f("L0_ffn_router_weight"), f("L0_ffn_w_shared_gate")], 0).T)
    a["router1"] = flat2(np.concatenate([f("L3_ffn_router_w").T, f("L3_ffn_sh_gate_w")], 1))

    for l, n in ((0, "L1"), (1, "L3")):
        g = lambda w: f(f"{n}_xattn_{w}")
        a[f"Wq{l}"] = c(g("Wq").reshape(H, HK, D).transpose(1, 0, 2))
        a[f"Wo{l}"] = c(g("Wo").reshape(D, H, HK).transpose(2, 1, 0))
        a[f"Kv{l}"] = c(g("w_kc_kv").transpose(1, 0, 2))
        a[f"Kr{l}"] = c(g("W_kr").transpose(2, 0, 1))
        a[f"Qr{l}"] = c(g("W_qr").transpose(2, 0, 1))
    a["Kq0"] = c(f("L1_xattn_w_kc_q").transpose(1, 0, 2))
    a["Kq1"] = c(f("L3_xattn_w_kc_q").reshape(H, HK, 2, CH).transpose(3, 2, 0, 1))
    a["w1ffn"] = c(np.stack([two(f("L1_ffn_w_gate").T).reshape(P, 2048), two(f("L1_ffn_w_up").T).reshape(P, 2048),
                             f("L1_ffn_w_down").T.reshape(8, P, D).transpose(1, 0, 2).reshape(P, 2048)], 1))
    a["router2"] = two(f("L2_ffn_router_w").T).reshape(P, KD * E2)
    a["w2d"] = two(f("L2_ffn_down_w").reshape(E2 * IE2, D).T)
    a["w2u"] = c(f("L2_ffn_up_w").transpose(0, 2, 1).reshape(E2 * IE2, D))

    def rope(length, dim):
        inv = (np.float32(1.0) / np.power(np.float32(10000.0), np.arange(0, dim, 2, dtype=np.float32) / np.float32(dim))).astype(np.float32)
        ang = np.arange(length, dtype=np.float32)[:, None] * inv[None]
        return np.repeat(np.sin(ang), 2, -1), np.repeat(np.cos(ang), 2, -1)

    sk, ck = rope(S, C)
    sk = np.concatenate([-sk[:, :C // 2], sk[:, C // 2:]], 1)
    a["ropek"] = c(np.stack([ck, sk]).reshape(2, 2, P, C).transpose(2, 0, 1, 3))
    sq, cq = rope(S, CQ)
    a["cosq"] = c(np.concatenate([cq[:, :CH].T, cq[:, CH:].T], 1))
    a["sinq"] = c(np.concatenate([sq[:, CH:].T, -sq[:, :CH].T], 1))
    return a


STAGES = 8


def kernel(**inputs):
    import concourse.bacc as bacc
    from concourse.bass_utils import run_bass_kernel_spmd as run

    nc = bacc.Bacc("TRN2", target_bir_lowering=False, num_devices=1)
    arrays, aps = {}, {}
    for name, v in layouts(inputs).items():
        arrays[f"in_{name}"] = v
        aps[name] = nc.dram_tensor(f"in_{name}", v.shape, mybir.dt.from_np(v.dtype), kind="ExternalInput").ap()
    out = nc.dram_tensor("out", (B, S, D), F32, kind="ExternalOutput").ap()
    build(nc, aps, out, STAGES)
    r = run(nc, [arrays], core_ids=[0])
    return r.results[0]["out"]
```

```python
from contextlib import ExitStack

import numpy as np

import concourse.bass as bass
from concourse import mybir

F32 = mybir.dt.float32
F32R = mybir.dt.float32r
BF16 = mybir.dt.bfloat16
U16 = mybir.dt.uint16
U32 = mybir.dt.uint32
ALU = mybir.AluOpType
ACT = mybir.ActivationFunctionType
AX = mybir.AxisListType

P = 128
B, S, D, C = 4, 256, 256, 64
T = B * S // P
TOK = B * S
KD = D // P
H, HK, CQ, R = 16, 128, 192, 64
CH = CQ // 2
E, FE, FS = 16, 176, 704
EX = E + 1
FT = (E * FE + FS + P - 1) // P
GRP = 2
NG = FT // GRP
LOOP = NG // 2
HALF = TOK // 2
TOPK = 4
I1 = 1024
KEEP = int(S * 0.3)
E2, IE2 = 8, 16
RNE = 1.5 * 2.0 ** 23
BIG = 3.0e38


class Chain:

    def __init__(self, eng, sem):
        self.eng, self.sem, self.base, self.at, self.trip = eng, sem, 0, 0, 0

    def __call__(self, ins):
        ins.then_inc(self.sem, 1)
        self.at += 1
        self.eng.wait_ge(self.sem, self.trip + self.base + self.at)

    def enter(self, i, first, per):
        self.base, self.at, self.first, self.per = self.base + self.at - first * per, 0, first, per
        self.trip = i * per

    def leave(self, trips):
        assert self.at == self.per, (self.at, self.per)
        self.base, self.at, self.trip = self.base + (self.first + trips) * self.per, 0, 0


def build(nc, a, out, stages=8):
    ctx = ExitStack()
    with ctx:
        def sb(name, shape, dt=F32):
            return ctx.enter_context(nc.sbuf_tensor(name, shape, dt))

        sems = {}

        def sem(name):
            if name not in sems:
                sems[name] = ctx.enter_context(nc.semaphore(name))
            return sems[name]

        PB = [ctx.enter_context(nc.psum_tensor(f"bank{i}", [P, 512], F32)) for i in range(8)]

        X = sb("X", [P, T, D])
        XN = sb("XN", [P, T, D])
        XT = sb("XT", [P, KD, TOK])
        A = sb("A", [P, T, S])
        ident = sb("ident", [P, P])
        identb = sb("identb", [P, P], BF16)
        ones = sb("ones", [P, P])
        kvaug = sb("kvaug", [P, T, C + 1])
        kvrT = sb("kvrT", [P, TOK])
        st6 = sb("st6", [P, T, 6])
        mv = sb("mv", [P, T, 2])
        rstd = sb("rstd", [P, T])
        epsc = sb("epsc", [P, 2])
        sc8 = sb("sc8", [P, 3, T])
        small = sb("small", [P, 16])
        WB = sb("WB", [P, 3, 2048], BF16)
        WF = sb("WF", [P, 6144])
        RF = sb("RF", [P, 2048])
        PF = sb("PF", [P, 8, D])
        RAW = sb("RAW", [P, 2, 4352])
        iote = sb("iote", [P, E])
        wr01 = sb("wr01", [P, 2, KD * EX])
        wr2 = sb("wr2", [P, KD * E2])
        PH = sb("PH", [P, 10240])

        PR = sb("PR", [P, 9216], F32R)
        XTr = PR[:, 0:4096].rearrange("p (a k n) -> p a k n", a=2, k=KD)
        WGr = PR[:, 4096:6144].rearrange("p (a j w) -> p a j w", a=2, j=2)
        WDr = PR[:, 6144:7168].rearrange("p (a j w) -> p a j w", a=2, j=2)
        HTr = PR[:, 7168:9216].rearrange("p (a q w) -> p a q w", a=2, q=2)

        ctxT = PH[0:C + 1, 4352:4352 + TOK]
        wkaug = PH[0:C + 1, 5376:5376 + C]
        wq2 = PH[0:C, 5440:5440 + C]
        wk2 = PH[0:C, 5504:5504 + C]
        n2 = PH[0:C, 5568:5568 + C]
        uT = PH[0:C, 5632:5632 + TOK]
        ctok = PH[:, 6656:7168].rearrange("p (t c) -> p t c", t=T)
        kvdup = PH[:, 7168:8192].rearrange("p (t a c) -> p t a c", t=T, a=2)
        SIM = PH[:, 8192:8192 + T * S].rearrange("p (t s) -> p t s", t=T)
        kvT0 = PH[0:C, 0:TOK]
        kv0 = PH[:, 1024:1024 + T * C].rearrange("p (t c) -> p t c", t=T)
        outT = PH[0:C, 1536:1536 + TOK]
        gam = PH[:, 2560:2816]
        bet = PH[:, 2816:3072]
        ropek = PH[:, 3072:3072 + 2 * 2 * C].rearrange("p (a s c) -> p a s c", a=2, s=2)
        kt1 = PH[:, 3328:3328 + T * C].rearrange("p (t c) -> p t c", t=T)
        kt2 = PH[:, 3840:3840 + T * C].rearrange("p (t c) -> p t c", t=T)

        ring = PH[:, 0:3072].rearrange("p (g w) -> p g w", g=2)
        selr = PH[0:3 * EX, 3072:3328].bitcast(BF16).rearrange("p (g w) -> p g w", g=2)
        sil = PH[:, 3328:4352].rearrange("p (q w) -> p q w", q=2)
        tmu = PH[:, 4352:5376].rearrange("p (q w) -> p q w", q=2)
        SCT = PH[0:3 * EX, 5376:5888].bitcast(BF16)
        o = 5888
        pr = PH[:, o:o + T * EX].rearrange("p (t e) -> p t e", t=T); o += T * EX
        pm = PH[:, o:o + T * EX].rearrange("p (t e) -> p t e", t=T); o += T * EX
        pk = PH[:, o:o + T * E].rearrange("p (t e) -> p t e", t=T); o += T * E
        pq = PH[:, o:o + T * E].rearrange("p (t e) -> p t e", t=T); o += T * E
        top8 = PH[:, o:o + T * 8].rearrange("p (t e) -> p t e", t=T); o += T * 8
        idx8 = PH[:, o:o + T * 8].bitcast(U32).rearrange("p (t e) -> p t e", t=T); o += T * 8
        idf = PH[:, o:o + T * 8].rearrange("p (t e) -> p t e", t=T); o += T * 8
        scp = PH[:, o:o + T * 3 * EX // 2].bitcast(BF16).rearrange("p (t c e) -> p t c e", t=T, c=3); o += T * 3 * EX // 2
        twork = PH[:, o:o + S]; o += S
        tmax = PH[:, o:o + 8]; o += 8
        assert o <= 8192

        qcT = PH[:, 0:2048].rearrange("p (g s) -> p g s", g=8)
        Ex = PH[:, 2048:3072].rearrange("p (q s l) -> p q s l", q=2, s=2)
        PT = PH[:, 3072:4096].rearrange("p (q l s) -> p q l s", q=2, l=2)
        CC = PH[:, 4096:4608].rearrange("p (q s c) -> p q s c", q=2, s=2)
        CCT = PH[:, 4608:5120].rearrange("p (q s) -> p q s", q=2)
        kvb = PH[:, 5120:5376]
        kvab = PH[:, 5376:5506].rearrange("p (l c) -> p l c", l=2)
        nmx = PH[:, 5506:5514].rearrange("p (q s) -> p q s", q=4)
        rin = PH[:, 5514:5522].rearrange("p (q s) -> p q s", q=2)
        cosq = PH[0:CH, 5632:6144]
        sinq = PH[0:CH, 6144:6656]
        r1 = PH[0:CH, 6656:7680].rearrange("p (q s) -> p q s", q=2)
        r2 = PH[0:CH, 7680:8704].rearrange("p (q s) -> p q s", q=2)
        qr = PH[0:CH, 8704:9728].rearrange("p (q s) -> p q s", q=2)
        W1 = WF[:, :].rearrange("p (k h q) -> p k h q", k=KD, h=H)
        MF = WF[:, 0:2048].rearrange("p (k w) -> p k w", k=KD)
        GF = WF[:, 2048:3072].rearrange("p (h c) -> p h c", h=H)
        RFv = RF[0:CH, :].rearrange("p (h f c) -> p h f c", h=H, f=2)
        rWq = RAW[:, :, 0:1024].rearrange("p g (h d) -> p g h d", h=4)
        rWo = RAW[:, :, 1024:2048].rearrange("p g (h d) -> p g h d", h=4)
        rKv = RAW[:, :, 2048:2304].rearrange("p g (h c) -> p g h c", h=4)
        rKr = RAW[0:R, :, 2304:2560].rearrange("p g (h c) -> p g h c", h=4)
        rQr = RAW[0:R, :, 2560:3328].rearrange("p g (h q) -> p g h q", h=4)
        rKq = RAW[:, :, 3328:4096].rearrange("p g (h q) -> p g h q", h=4)
        rKqT = RAW[0:CH, :, 3328:4352].rearrange("p g (f h k) -> p g f h k", f=2, h=4)

        rF = RAW[:, :, :].rearrange("p g w -> p (g w)")[:, 0:6144].rearrange("p (m w) -> p m w", m=3)
        XQ = PH[:, 0:1024].bitcast(BF16).rearrange("p (t d) -> p t d", t=T)
        XQT = PH[:, 1024:2048].bitcast(BF16).rearrange("p (k n) -> p k n", k=KD)
        qt = PH[:, 2048:4096]
        silq = PH[:, 4096:5120]
        hq = PH[:, 5120:6144]
        hqb = PH[:, 6144:6656].bitcast(BF16)
        hqT = PH[:, 6656:7168].bitcast(BF16)
        q8 = PH[:, 7168:7232].rearrange("p (c t) -> p c t", c=8)
        amax, xs8, xr8, sg8, su8, ys8 = (q8[:, n, :] for n in range(6))
        hs = PH[:, 7232:7240]
        sgc = PH[:, 7240:7241]
        wsum = sb("wsum", [P, 3])
        wtot = sb("wtot", [P, 3])
        winv = sb("winv", [P, 3])
        neg1 = sb("neg1", [P, 3])

        w2d = PH[:, 7296:7552].rearrange("p (k n) -> p k n", k=KD)
        w2u = PH[:, 7552:7808]
        a2 = PH[:, 8832:9856].rearrange("p (t n) -> p t n", t=T)
        a2T = PH[:, 0:1024]

        FUSED = (6, 5)

        def fuse_copy(l, n, copy):
            src = PB[4 + n % 4]
            g, part = divmod(n, FUSED[l])
            if part == 0:
                return copy(RF[0:CH, g * 512:(g + 1) * 512], src[0:CH, :])
            if part == 1:
                return copy(PF[:, 2 * g:2 * g + 2, :], src[:, :].rearrange("p (g d) -> p g d", g=2))
            if l == 0:
                k, q = divmod(part - 2, 2)
                h = 4 * g + 2 * q
                return copy(W1[:, k, h:h + 2, :], src[:, 0:2 * CQ].rearrange("p (h q) -> p h q", h=2))
            if part == 2:
                return copy(GF[:, 4 * g:4 * g + 4, :], src[:, 0:256].rearrange("p (h c) -> p h c", h=4))
            return copy(MF[:, part - 3, g * 256:(g + 1) * 256], src[:, 0:256])

        block = ctx.enter_context(nc.Block())
        FFN_AT = {1: 0, 7: 1}

        @block.sync
        def _(sp):
            sp.dma_start(X[:, :, :], a["x"].rearrange("b (s p) d -> p (b s) d", p=P)).then_inc(sem("x_loaded"), 16)
            for dst, name in ((ident[:, :], "ident"), (ctxT[0:C, :], "ctxT"), (wkaug, "wkaug"), (wq2, "wq2"), (wk2, "wk2"),
                              (ctok, None), (ropek, "ropek"), (identb[:, :].bitcast(U16), "identb")):
                src = a[name] if name else a["ctx"].rearrange("b (s p) c -> p (b s) c", p=P)
                sp.dma_start(dst, src).then_inc(sem("consts_loaded"), 16)
            sp.dma_start(gam, a["gamma"].partition_broadcast(P)).then_inc(sem("consts_loaded"), 16)
            sp.dma_start(bet, a["beta"].partition_broadcast(P)).then_inc(sem("consts_loaded"), 16)
            sp.dma_start(small[:, 0:1], a["graw"].partition_broadcast(P)).then_inc(sem("consts_loaded"), 16)

            sp.dma_start(iote[:, :], a["iote"].partition_broadcast(P)).then_inc(sem("router_loaded"), 16)
            for dst, name in ((wr01[:, 0, :], "router0"), (wr01[:, 1, :], "router1"), (wr2[:, :], "router2")):
                sp.dma_start(dst, a[name]).then_inc(sem("router_loaded"), 16)

            def ffn_weights(f):
                w, sel = a[f"w{f}"], a["sel"]
                sp.wait_ge(sem("stage_done"), (1, 7)[f])
                for g in range(2):
                    sp.dma_start(ring[:, g, :], w[g]).then_inc(sem(f"w_full{g}"), 16)
                    sp.dma_start(selr[:, g, :].bitcast(U16), sel[:, g * 256:(g + 1) * 256]).then_inc(sem(f"sel_full{g}"), 16)
                with sp.Fori(1, LOOP) as i:
                    for g in range(2):
                        sp.wait_ge(sem("wd_low"), i * 4 + (4 * LOOP * f - 4 + 2 * (g + 1)))
                        sp.dma_start(ring[:, g, :], w[bass.ds(i * 2 + g, 1)].rearrange("g p w -> p (g w)")).then_inc(sem(f"w_full{g}"), 16)
                        sp.wait_ge(sem("spread_done"), i * 8 + (8 * LOOP * f - 8 + 4 * (g + 1)))
                        sp.dma_start(selr[:, g, :].bitcast(U16), sel[:, bass.ds(i * 512 + g * 256, 256)]).then_inc(sem(f"sel_full{g}"), 16)

            def attention_weights(l):
                for g in range(4):
                    if g >= 2:
                        sp.wait_ge(sem("fuse_done"), (0, 24)[l] + FUSED[l] * (g - 1))
                    for dst, name in ((rWq, "Wq"), (rWo, "Wo"), (rKv, "Kv"), (rKr, "Kr"), (rQr, "Qr")):
                        sp.dma_start(dst[:, g % 2], a[f"{name}{l}"][:, 4 * g:4 * g + 4, :]).then_inc(sem(f"raw_loaded{g % 2}"), 16)
                    if l == 0:
                        sp.dma_start(rKq[:, g % 2], a["Kq0"][:, 4 * g:4 * g + 4, :]).then_inc(sem(f"raw_loaded{g % 2}"), 16)
                    else:
                        sp.dma_start(rKqT[:, g % 2], a["Kq1"][:, :, 4 * g:4 * g + 4, :]).then_inc(sem(f"raw_loaded{g % 2}"), 16)

            attention_weights(0)
            sp.wait_ge(sem("fuse_done"), 24)
            sp.dma_start(rF, a["w1ffn"]).then_inc(sem("w1ffn_loaded"), 16)
            if stages >= 2:
                ffn_weights(0)
            if stages >= 3:
                sp.wait_ge(sem("stage_done"), 2)
                sp.dma_start(cosq, a["cosq"]).then_inc(sem("rope_loaded"), 16)
                sp.dma_start(sinq, a["sinq"]).then_inc(sem("rope_loaded"), 16)
            if stages >= 6:
                sp.wait_ge(sem("stage_done"), 3)
                sp.dma_start(w2d, a["w2d"]).then_inc(sem("w2_loaded"), 16)
                sp.dma_start(w2u, a["w2u"]).then_inc(sem("w2_loaded"), 16)
            if stages >= 7:
                sp.wait_ge(sem("wq_ready"), 3)
                attention_weights(1)
            if stages >= 8:
                ffn_weights(1)
            sp.wait_ge(sem("x_final"), 1)
            sp.dma_start(out.rearrange("b (s p) d -> p (b s) d", p=P), X[:, :, :]).then_inc(sem("stored"), 16)
            sp.wait_ge(sem("stored"), 16)

        @block.tensor
        def _(pe):
            mm = nc.tensor.matmul

            def ln_transposes(k):
                for tg in range(2):
                    for kk in range(KD):
                        for q in range(4):
                            t = tg * 4 + q
                            pe.wait_ge(sem("ln_x"), 8 * k + t + 1)
                            last = nc.tensor.transpose(PB[tg * 2 + kk][:, q * P:(q + 1) * P],
                                                       XN[:, t, kk * P:(kk + 1) * P], ident[:, :])
                        last.then_inc(sem("ln_T"), 1)
                pe.wait_ge(sem("xt_act"), 2 * (k + 1))
                pe.wait_ge(sem("xt_dve"), 2 * (k + 1))

            def context():
                pe.wait_ge(sem("consts_loaded"), 16 * 11)
                pe.wait_ge(sem("ctx_ones"), 1)
                for n in range(2):
                    mm(PB[n][0:C, :], wkaug, ctxT[:, n * 512:(n + 1) * 512], start=True, stop=True).then_inc(sem("kvT_done"), 1)
                for t in range(T):
                    last = mm(PB[2][:, t * C:(t + 1) * C], ctxT[:, t * P:(t + 1) * P], wkaug, start=True, stop=True)
                last.then_inc(sem("kv_done"), 1)
                mm(PB[3][0:C, 0:C], wq2, wk2, start=True, stop=True).then_inc(sem("n2_done"), 1)
                pe.wait_ge(sem("n2_copied"), 1)
                for n in range(2):
                    mm(PB[4 + n][0:C, :], n2, ctxT[0:C, n * 512:(n + 1) * 512], start=True, stop=True).then_inc(sem("uT_done"), 1)
                pe.wait_ge(sem("kvr_ready"), 1)
                for n in range(2):
                    for q in range(4):
                        t = 4 * n + q
                        last = nc.tensor.transpose(PB[6 + n][:, q * P:(q + 1) * P],
                                                   kvdup[:, t, :, :].rearrange("p a c -> p (a c)"), ident[:, :])
                    last.then_inc(sem("kvrT_done"), 1)
                pe.wait_ge(sem("uT_copied"), 2)
                pe.wait_ge(sem("kvT_copied"), 2)
                pe.wait_ge(sem("kv_copied"), 1)
                for t in range(T):
                    b = t // 2
                    last = mm(PB[b][:, (t % 2) * S:(t % 2 + 1) * S], uT[:, t * P:(t + 1) * P], ctxT[0:C, b * S:(b + 1) * S],
                              start=True, stop=True)
                    if t % 2:
                        last.then_inc(sem("sim_done"), 1)

            def l0_attention():
                ln_transposes(0)
                pe.wait_ge(sem("kvrT_copied"), 2)
                for b in range(B):
                    for k in range(KD):
                        last = mm(PB[4 + b // 2][0:C, (b % 2) * S:(b % 2 + 1) * S], kv0[:, 2 * b + k, :],
                                  XT[:, k, b * S:(b + 1) * S], start=(k == 0), stop=(k == KD - 1))
                    if b % 2:
                        last.then_inc(sem("l0_out"), 1)
                pe.wait_ge(sem("l0_out_copied"), 2)
                for t in range(T):
                    b = t // 2
                    last = mm(PB[b][:, (t % 2) * S:(t % 2 + 1) * S], outT[:, t * P:(t + 1) * P], kvT0[:, b * S:(b + 1) * S],
                              start=True, stop=True)
                    if t % 2:
                        last.then_inc(sem("l0_sim"), 1)

            def ffn(f, lnk):
                ln_transposes(lnk)
                pe.wait_ge(sem("router_loaded"), 64)
                wr = wr01[:, f, :].rearrange("p (k e) -> p k e", k=KD)
                for t in range(T):
                    for k in range(KD):
                        last = mm(PB[0][:, t * EX:(t + 1) * EX], XT[:, k, t * P:(t + 1) * P], wr[:, k, :],
                                  start=(k == 0), stop=(k == KD - 1))
                last.then_inc(sem("logits"), 1)
                pe.wait_ge(sem("scores_split"), f + 1)
                scT = PB[1][:, :].bitcast(BF16)
                for t in range(T):
                    last = nc.tensor.transpose(scT[0:3 * EX, t * P:(t + 1) * P], scp[:, t, :, :].rearrange("p c e -> p (c e)"), identb[:, :])
                last.then_inc(sem("scoresT"), 1)
                pe.wait_ge(sem("scoresT_copied"), f + 1)
                base = f * 8 * LOOP

                HI_LO = ((0, 0), (0, 1), (1, 0))
                pe.wait_ge(sem("xtr_done"), 4 * (f + 1))

                def gate_up(i, u):
                    jj, half = u // 2 % 2, u % 2
                    n = i * 8 + (u + base)
                    if half == 0:
                        pe.wait_ge(sem("wg_high"), i * 4 + (u // 2 + 1 + base // 2))
                        pe.wait_ge(sem("wg_low"), i * 4 + (u // 2 + 1 + base // 2))
                    if not (isinstance(i, int) and i == 0 and u < 2):
                        pe.wait_ge(sem("h_done"), n - 1)
                    for dst, w, done in ((PB[u % 2], 0, "gate_done"), (PB[2 + u % 2], 256, "up_done")):
                        for k in range(KD):
                            for x, y in HI_LO:
                                last = mm(dst[:, :], WGr[:, x, jj, w + k * P:w + (k + 1) * P], XTr[:, y, k, half * HALF:(half + 1) * HALF],
                                          start=(k == 0 and x + y == 0), stop=(k == KD - 1 and x == 1))
                        last.then_inc(sem(done), 1)

                def spread(i, u):
                    g, jj, half = u // 4, u // 2 % 2, u % 2
                    if u % 4 == 0:
                        pe.wait_ge(sem(f"sel_full{g}"), i * 16 + (16 + 16 * LOOP * f))
                    pe.wait_ge(sem("silu_done"), i * 8 + (u + base + 1))
                    mm(PB[u % 2][:, :], selr[:, g, jj * P:(jj + 1) * P], SCT[:, half * HALF:(half + 1) * HALF],
                       start=True, stop=True).then_inc(sem("spread_done"), 1)

                def down(i, u, first=False):
                    jj, half = u // 2 % 2, u % 2
                    if half == 0:
                        pe.wait_ge(sem("wd_high"), i * 4 + (u // 2 + 1 + base // 2))
                        pe.wait_ge(sem("wd_low"), i * 4 + (u // 2 + 1 + base // 2))
                    pe.wait_ge(sem("h_low"), i * 8 + (u + base + 1))
                    for q in range(4):
                        for x, y in HI_LO:
                            last = mm(PB[4 + half * 2 + q // 2][:, (q % 2) * D:(q % 2 + 1) * D], HTr[:, x, u % 2, q * P:(q + 1) * P],
                                      WDr[:, y, jj, :], start=(first and q % 2 == 0 and x + y == 0), stop=False, skip_group_check=True)
                    last.then_inc(sem("down_done"), 1)

                def trip(i, first):
                    for u in range(8):
                        gate_up(i, u)
                        if not (first and u < 1):
                            spread(i if u else i - 1, (u - 1) % 8)
                        if not (first and u < 2):
                            down(i if u > 1 else i - 1, (u - 2) % 8, first=first and u - 2 < 2)

                trip(0, True)
                with pe.Fori(1, LOOP) as i:
                    trip(i, False)
                spread(LOOP - 1, 7)
                down(LOOP - 1, 6)
                down(LOOP - 1, 7)

            def fuse(l):
                n = [0]
                base = (0, 24)[l]

                def bank():
                    if n[0] >= 4:
                        pe.wait_ge(sem("fuse_copied"), base + n[0] - 3)
                    n[0] += 1
                    return PB[4 + (n[0] - 1) % 4]

                for g in range(4):
                    pe.wait_ge(sem(f"raw_loaded{g % 2}"), 96 * (2 * l + g // 2 + 1))
                    e = g % 2
                    dst = bank()
                    for q in range(4):
                        for half in range(2):
                            last = mm(dst[0:CH, (q * 2 + half) * C:(q * 2 + half + 1) * C], rQr[:, e, q, half * CH:(half + 1) * CH],
                                      rKr[:, e, q, :], start=True, stop=True)
                    last.then_inc(sem("fuse_done"), 1)
                    dst = bank()
                    for q in range(4):
                        last = mm(dst[(q % 2) * C:(q % 2 + 1) * C, (q // 2) * D:(q // 2 + 1) * D], rKv[:, e, q, :], rWo[:, e, q, :],
                                  start=True, stop=True)
                    last.then_inc(sem("fuse_done"), 1)
                    if l == 0:
                        for k in range(KD):
                            for q2 in range(2):
                                dst = bank()
                                for q in range(2):
                                    last = mm(dst[:, q * CQ:(q + 1) * CQ], rWq[:, e, 2 * q2 + q, k * P:(k + 1) * P], rKq[:, e, 2 * q2 + q, :],
                                              start=True, stop=True)
                                last.then_inc(sem("fuse_done"), 1)
                    else:
                        pe.wait_ge(sem("fuse_copied"), base + 5 * g + 1)
                        dst = bank()
                        for q in range(4):
                            for half in range(2):
                                last = mm(dst[:, q * C:(q + 1) * C], rKqT[:, e, half, q, :], RFv[:, 4 * g + q, half, :],
                                          start=(half == 0), stop=(half == 1))
                        last.then_inc(sem("fuse_done"), 1)
                        pe.wait_ge(sem("fuse_copied"), base + 5 * g + 3)
                        for k in range(KD):
                            dst = bank()
                            for q in range(4):
                                last = mm(dst[:, q * C:(q + 1) * C], rWq[:, e, q, k * P:(k + 1) * P], GF[:, 4 * g + q, :],
                                          start=True, stop=True)
                            last.then_inc(sem("fuse_done"), 1)
                pe.wait_ge(sem("fuse_copied"), (24, 44)[l])

            def attention(l, lnk):
                ln_transposes(lnk)

                def at(name, value):
                    if not isinstance(value, int) or value > 0:
                        pe.wait_ge(sem(name), value)

                def step(b, h):
                    hb, pb = b * H + l * B * H, b * 8 + l * B * 8
                    inside = lambda m: not isinstance(b, int) or 0 <= b * H + m < B * H

                    def cols(m):
                        bb = b + m // H
                        return slice(bb * S, bb * S + S) if isinstance(b, int) else bass.ds(bb * S, S)

                    m = h + 2
                    if l == 0 and inside(m):
                        at("rope_done", hb + (m + 1))
                        if m % 2 == 0:
                            at("qc_copied", pb + m // 2)
                        for half in range(2):
                            last = mm(PB[4][(m % 2) * C:(m % 2 + 1) * C, 0:S], RFv[:, m % H, half, :], qr[:, m % 2, half * S:(half + 1) * S],
                                      start=(half == 0), stop=(half == 1))
                        last.then_inc(sem("qc_done"), 1)
                    m = h + 4
                    if l == 0 and inside(m):
                        at("rope_read", hb + m)
                        for half in range(2):
                            for k in range(KD):
                                last = mm(PB[0][0:CH, half * S:(half + 1) * S], W1[:, k, m % H, half * CH:(half + 1) * CH], XT[:, k, cols(m)],
                                          start=(k == 0), stop=(k == KD - 1))
                        last.then_inc(sem("qbig_done"), 1)
                    if l == 1 and h % 2 and inside(h + 1):
                        m = (h + 1) // 2
                        at("qc_copied", pb + m)
                        for k in range(KD):
                            last = mm(PB[0][:, 0:S], MF[:, k, (m % 8) * P:(m % 8 + 1) * P], XT[:, k, cols(h + 1)], start=(k == 0), stop=(k == KD - 1))
                        last.then_inc(sem("qc_done"), 1)
                    if inside(h):
                        at("qc_copied", pb + (h // 2 + 1))
                        at("exp_done", hb + (h - 1))
                        if h % H == 0:
                            pe.wait_ge(sem("keys_ready"), b + (l * B + 1))
                        rows = slice((h % 2) * C, (h % 2 + 1) * C)
                        for s in range(2):
                            last = mm(PB[1 + h % 2][:, s * S:(s + 1) * S], qcT[rows, h // 2 % 8, s * P:(s + 1) * P], kvb[rows, :],
                                      start=True, stop=True)
                        last.then_inc(sem("score_done"), 1)
                    m = h - 1
                    if inside(m):
                        at("exp_done", hb + (m + 1))
                        at("pt_copied", hb + m)
                        for k in range(2):
                            for s in range(2):
                                last = nc.tensor.transpose(PB[3][:, k * S + s * P:k * S + (s + 1) * P], Ex[:, m % 2, s, k * P:(k + 1) * P],
                                                           ident[:, :])
                        last.then_inc(sem("pt_done"), 1)
                    m = h - 2
                    if inside(m):
                        at("pt_copied", hb + (m + 1))
                        if m % 2 == 0:
                            at("cc_done", pb + m // 2)
                        if m % H == 0:
                            pe.wait_ge(sem("values_ready"), b + (l * B + 1))
                        for s in range(2):
                            o = ((m % 2) * 2 + s) * (C + 1)
                            for k in range(2):
                                last = mm(PB[5][:, o:o + C + 1], PT[:, m % 2, k, s * P:(s + 1) * P], kvab[:, k, :],
                                          start=(k == 0), stop=(k == 1))
                        last.then_inc(sem("pv_done"), 1)
                    if h % 2 == 0 and inside(h - 4):
                        m = (h - 4) // 2
                        at("cc_done", pb + (m + 1))
                        at("cct_copied", pb + m)
                        for s in range(2):
                            last = nc.tensor.transpose(PB[6][:, s * P:(s + 1) * P], CC[:, m % 2, s, :], ident[:, :])
                        last.then_inc(sem("cct_done"), 1)
                    if h % 2 and inside(h - 5):
                        m = (h - 5) // 2
                        at("cct_copied", pb + (m + 1))
                        if m == 0:
                            at("y_added", b + l * B)
                        for s in range(2):
                            last = mm(PB[7][:, s * D:(s + 1) * D], CCT[:, m % 2, s * P:(s + 1) * P], PF[:, m % 8, :],
                                      start=(m % 8 == 0 and s == 0), stop=False, skip_group_check=True)
                        last.then_inc(sem("y_done"), 1)

                for h in range(-4, H):
                    step(0, h)
                with pe.Fori(1, B - 1) as b:
                    for h in range(H):
                        step(b, h)
                for h in range(H + 4):
                    step(B - 1, h)

            def quantized():
                xqT = [PB[k][:, :].bitcast(BF16) for k in range(KD)]
                pe.wait_ge(sem("xq_ready"), 1)
                for k in range(KD):
                    for t in range(T):
                        last = nc.tensor.transpose(xqT[k][:, t * P:(t + 1) * P], XQ[:, t, k * P:(k + 1) * P], identb[:, :])
                    last.then_inc(sem("xqT_done"), 1)
                pe.wait_ge(sem("xqT_copied"), 2)
                pe.wait_ge(sem("wq_ready"), 3)

                def gate_up(t):
                    if not isinstance(t, int):
                        pe.wait_ge(sem("q_silu"), t * 2)
                        pe.wait_ge(sem("q_h"), t * 2)
                    tok = slice(0, P) if isinstance(t, int) else bass.ds(t * P, P)
                    for m in range(2):
                        for c in range(2):
                            for k in range(KD):
                                last = mm(PB[2 * m + c][:, :], XQT[:, k, tok], WB[:, m, k * I1 + c * 512:k * I1 + c * 512 + 512],
                                          start=(k == 0), stop=(k == KD - 1))
                            last.then_inc(sem("q_gu"), 1)

                def down(t, one):
                    hT = PB[4][:, :].bitcast(BF16)
                    pe.wait_ge(sem("q_quant"), t + one)
                    for c in range(8):
                        last = nc.tensor.transpose(hT[:, c * P:(c + 1) * P], hqb[:, c * P:(c + 1) * P], identb[:, :])
                    last.then_inc(sem("q_T"), 1)
                    pe.wait_ge(sem("q_Tcopied"), t + one)
                    pe.wait_ge(sem("q_bank_free"), t)
                    for c in range(8):
                        last = mm(PB[5 + 0][:, 0:D], hqT[:, c * P:(c + 1) * P], WB[:, 2, c * D:(c + 1) * D], start=(c == 0), stop=(c == 7))
                    last.then_inc(sem("q_down"), 1)

                gate_up(0)
                with pe.Fori(1, T) as t:
                    gate_up(t)
                    down(t, 0)
                down(T, 0)

            def small_experts(lnk):
                ln_transposes(lnk)
                for t in range(T):
                    for k in range(KD):
                        last = mm(PB[4][:, t * E2:(t + 1) * E2], XT[:, k, t * P:(t + 1) * P], wr2[:, k * E2:(k + 1) * E2],
                                  start=(k == 0), stop=(k == KD - 1))
                last.then_inc(sem("logits2"), 1)
                pe.wait_ge(sem("w2_loaded"), 32)
                for t in range(T):
                    for k in range(KD):
                        last = mm(PB[5 + t // 4][:, (t % 4) * P:(t % 4 + 1) * P], XT[:, k, t * P:(t + 1) * P], w2d[:, k, :],
                                  start=(k == 0), stop=(k == KD - 1))
                    if t % 4 == 3:
                        last.then_inc(sem("h2_done"), 1)
                pe.wait_ge(sem("a2_ready"), 1)
                for t in range(T):
                    last = nc.tensor.transpose(PB[t // 4][:, (t % 4) * P:(t % 4 + 1) * P], a2[:, t, :], ident[:, :])
                    if t % 4 == 3:
                        last.then_inc(sem("a2T_done"), 1)
                pe.wait_ge(sem("a2T_copied"), 2)
                for t in range(T):
                    last = mm(PB[4 + t // 2][:, (t % 2) * D:(t % 2 + 1) * D], a2T[:, t * P:(t + 1) * P], w2u, start=True, stop=True)
                    if t % 2:
                        last.then_inc(sem("y2_done"), 1)

            def adjacency():
                pe.wait_ge(sem("a_kept"), 1)
                for b in range(B):
                    for r in range(2):
                        for c in range(2):
                            last = nc.tensor.transpose(PB[b][:, r * S + c * P:r * S + (c + 1) * P], A[:, 2 * b + c, r * P:(r + 1) * P], ident[:, :])
                    last.then_inc(sem("aT_done"), 1)

            context()
            l0_attention()
            fuse(0)
            if stages >= 2:
                ffn(0, 1)
            if stages >= 3:
                attention(0, 2)
            if stages >= 4:
                quantized()
            if stages >= 5:
                pe.wait_ge(sem("stage_done"), 4)
                adjacency()
                fuse(1)
            if stages >= 6:
                small_experts(3)
            if stages >= 7:
                attention(1, 4)
            if stages >= 8:
                ffn(1, 5)

        @block.vector
        def _(dve):
            v = nc.vector
            link = Chain(dve, sem("dve_chain"))
            stage = [0]

            def done(ins):
                stage[0] += 1
                ins.then_inc(sem("stage_done"), 1)
                dve.wait_ge(sem("stage_done"), stage[0])

            def normalize(k, lnk):
                for t in range(T):
                    v.bn_stats(st6[:, t, :], X[:, t, :]).then_inc(sem("dve_stats"), 1)
                for t in range(T):
                    dve.wait_ge(sem("dve_stats"), 8 * k + t + 1)
                    last = v.bn_aggr(mv[:, t, :], st6[:, t, :])
                last.then_inc(sem("ln_stat"), 1)
                dve.wait_ge(sem("ln_std"), k + 1)
                link(v.reciprocal(rstd[:, :], rstd[:, :]))
                for t in range(T):
                    last = v.tensor_scalar(XN[:, t, :], X[:, t, :], mv[:, t, 0:1], rstd[:, t:t + 1], ALU.subtract, ALU.mult)
                    if lnk is not None:
                        last.then_inc(sem("ln_x"), 1)
                if lnk is None:
                    return link(last)
                for kk in range(KD):
                    dve.wait_ge(sem("ln_T"), 4 * lnk + 3 + kk)
                    v.tensor_copy(XT[:, kk, 512:1024], PB[2 + kk][:, :]).then_inc(sem("xt_dve"), 1)

            def context():
                v.memset(ones[:, :], 1.0).then_inc(sem("dve_chain"), 1); link.at += 1
                v.memset(epsc[:, 0:1], 1e-5).then_inc(sem("eps_set"), 1)
                v.memset(epsc[:, 1:2], 1e-6).then_inc(sem("eps_set"), 1)
                v.memset(ctxT[C:C + 1, :], 1.0).then_inc(sem("ctx_ones"), 1)
                v.memset(kvaug[:, :, C:C + 1], 1.0)
                dve.wait_ge(sem("consts_loaded"), 16 * 11)
                bc = lambda ap: ap.unsqueeze(1).to_broadcast([P, B, 2, ap.shape[-1]])
                c4 = ctok[:, :, :].rearrange("p (b s) c -> p b s c", b=B)
                k1 = kt1.rearrange("p (b s) c -> p b s c", b=B)
                k2 = kt2.rearrange("p (b s) c -> p b s c", b=B)
                v.tensor_tensor(k1, c4, bc(ropek[:, 0, :, :]), ALU.mult)
                v.tensor_tensor(k2[:, :, :, 0:32], c4[:, :, :, 32:64], bc(ropek[:, 1, :, 0:32]), ALU.mult)
                link(v.tensor_tensor(k2[:, :, :, 32:64], c4[:, :, :, 0:32], bc(ropek[:, 1, :, 32:64]), ALU.mult))
                v.tensor_tensor(kvaug[:, :, 0:C], kt1, kt2, ALU.add)
                v.tensor_tensor(kvdup[:, :, 0, :], kt1, kt2, ALU.add)
                v.tensor_tensor(kvdup[:, :, 1, :], kt1, kt2, ALU.add).then_inc(sem("kvr_ready"), 1)
                dve.wait_ge(sem("n2_done"), 1)
                v.tensor_copy(n2, PB[3][0:C, 0:C]).then_inc(sem("n2_copied"), 1)
                dve.wait_ge(sem("kv_done"), 1)
                v.tensor_copy(kv0, PB[2][:, 0:T * C].rearrange("p (t c) -> p t c", t=T)).then_inc(sem("kv_copied"), 1)
                for n in range(2):
                    dve.wait_ge(sem("uT_done"), n + 1)
                    v.tensor_copy(uT[:, n * 512:(n + 1) * 512], PB[4 + n][0:C, :]).then_inc(sem("uT_copied"), 1)
                for b in range(B):
                    dve.wait_ge(sem("sim_done"), b + 1)
                    v.tensor_copy(SIM[:, 2 * b:2 * b + 2, :], PB[b][:, :].rearrange("p (s l) -> p s l", s=2)).then_inc(sem("sim_copied"), 1)

            def l0_attention():
                normalize(0, 0)
                for b in range(B):
                    dve.wait_ge(sem("l0_sim"), b + 1)
                    for s in range(2):
                        v.bn_stats(st6[:, 2 * b + s, :], PB[b][:, s * S:(s + 1) * S]).then_inc(sem("l0_stats"), 1)
                for t in range(T):
                    dve.wait_ge(sem("l0_stats"), t + 1)
                    last = v.bn_aggr(mv[:, t, :], st6[:, t, :])
                last.then_inc(sem("l0_stat"), 1)
                dve.wait_ge(sem("l0_std"), 1)
                link(v.reciprocal(rstd[:, :], rstd[:, :]))
                for t in range(T):
                    last = v.tensor_scalar(XN[:, t, :], PB[t // 2][:, (t % 2) * S:(t % 2 + 1) * S], mv[:, t, 0:1],
                                           rstd[:, t:t + 1], ALU.subtract, ALU.mult)
                link(last)
                g8 = gam.unsqueeze(1).to_broadcast([P, T, D])
                b8 = bet.unsqueeze(1).to_broadcast([P, T, D])
                link(v.tensor_tensor(XN[:, :, :], XN[:, :, :], g8, ALU.mult))
                link(v.tensor_tensor(XN[:, :, :], XN[:, :, :], b8, ALU.add))
                link(v.tensor_reduce(sc8[:, 0, :], XN[:, :, :], AX.X, ALU.max))
                v.tensor_tensor(XN[:, :, :], XN[:, :, :], sc8[:, 0, :].unsqueeze(2).to_broadcast([P, T, D]), ALU.subtract)\
                    .then_inc(sem("l0_shift"), 1)
                dve.wait_ge(sem("l0_exp"), 1)
                link(v.tensor_reduce(sc8[:, 1, :], XN[:, :, :], AX.X, ALU.add))
                link(v.reciprocal(sc8[:, 2, :], sc8[:, 1, :]))
                for t in range(T):
                    last = v.scalar_tensor_tensor(X[:, t, :], XN[:, t, :], sc8[:, 2, t:t + 1], X[:, t, :], ALU.mult, ALU.add)
                done(last)

            def scores(f):
                lg = PB[0][:, 0:T * EX].rearrange("p (t e) -> p t e", t=T)
                over = lambda col: col.unsqueeze(2).to_broadcast([P, T, E])
                dve.wait_ge(sem("logits"), f + 1)
                link(v.tensor_reduce(sc8[:, 0, :], lg[:, :, 0:E], AX.X, ALU.max))
                v.tensor_tensor(pm[:, :, 0:E], lg[:, :, 0:E], over(sc8[:, 0, :]), ALU.subtract)
                v.tensor_scalar(pm[:, :, E:EX], lg[:, :, E:EX], -1.0, None, ALU.mult).then_inc(sem("logits_shifted"), 1)
                dve.wait_ge(sem("logits_exp"), f + 1)
                v.tensor_scalar(pm[:, :, E:EX], pr[:, :, E:EX], 1.0, None, ALU.add)
                link(v.tensor_reduce(sc8[:, 0, :], pr[:, :, 0:E], AX.X, ALU.add))
                link(v.reciprocal(sc8[:, 1, :], sc8[:, 0, :]))
                link(v.tensor_tensor(pk[:, :, :], pr[:, :, 0:E], over(sc8[:, 1, :]), ALU.mult))
                for t in range(T):
                    last = v.max(top8[:, t, :], pk[:, t, :])
                link(last)
                for t in range(T):
                    last = v.max_index(idx8[:, t, :], top8[:, t, :], pk[:, t, :])
                link(last)
                link(v.tensor_copy(idf[:, :, :], idx8[:, :, :]))
                dve.wait_ge(sem("router_loaded"), 64)
                io = iote[:, :].unsqueeze(1).to_broadcast([P, T, E])
                link(v.tensor_tensor(pm[:, :, 0:E], io, over(idf[:, :, 0]), ALU.is_equal))
                for c in range(1, TOPK):
                    link(v.tensor_tensor(pq[:, :, :], io, over(idf[:, :, c]), ALU.is_equal))
                    link(v.tensor_tensor(pm[:, :, 0:E], pm[:, :, 0:E], pq[:, :, :], ALU.add))
                link(v.tensor_tensor(pr[:, :, 0:E], pm[:, :, 0:E], pk[:, :, :], ALU.mult))
                if f == 1:
                    link(v.tensor_reduce(sc8[:, 0, :], pr[:, :, 0:E], AX.X, ALU.add))
                    link(v.tensor_scalar(sc8[:, 0, :], sc8[:, 0, :], 1e-9, None, ALU.max))
                    link(v.reciprocal(sc8[:, 1, :], sc8[:, 0, :]))
                    link(v.tensor_tensor(pr[:, :, 0:E], pr[:, :, 0:E], over(sc8[:, 1, :]), ALU.mult))
                link(v.reciprocal(pr[:, :, E:EX], pm[:, :, E:EX]))
                link(v.tensor_copy(scp[:, :, 0, :], pr))
                link(v.tensor_tensor(pr, pr, scp[:, :, 0, :], ALU.subtract))
                link(v.tensor_copy(scp[:, :, 1, :], pr))
                link(v.tensor_tensor(pr, pr, scp[:, :, 1, :], ALU.subtract))
                v.tensor_copy(scp[:, :, 2, :], pr).then_inc(sem("scores_split"), 1)
                dve.wait_ge(sem("scoresT"), f + 1)
                v.tensor_copy(SCT, PB[1][0:3 * EX, :].bitcast(BF16)).then_inc(sem("scoresT_copied"), 1)

            PER_TILE = 2 * ((KEEP - 1) // 8) + 3

            def keep_neighbours(t, u):
                row = bass.ds(t, 1) if not isinstance(t, int) else slice(t, t + 1)
                spacer = lambda: v.tensor_copy(small[:, 9:10], small[:, 0:1])
                rounds = (KEEP - 1) // 8
                if u == 0:
                    link(v.tensor_copy(twork.unsqueeze(1), SIM[:, row, :]))
                for _ in range(2 if u < rounds // 2 else rounds % 2 if u == rounds // 2 else 0):
                    spacer()
                    link(v.max(tmax, twork))
                    spacer()
                    link(v.match_replace(twork, tmax, twork, -BIG))
                if u == 7:
                    spacer()
                    link(v.max(tmax, twork))
                    last_kept = (KEEP - 1) % 8
                    link(v.scalar_tensor_tensor(A[:, row, :], SIM[:, row, :], tmax[:, last_kept:last_kept + 1], A[:, row, :],
                                                ALU.is_ge, ALU.mult))

            def ffn(f, stage, lnk):
                normalize(stage, lnk)
                scores(f)
                base = f * 8 * LOOP
                if f == 0:
                    dve.wait_ge(sem("sim_sigmoid"), 1)

                for kk in range(KD):
                    for tg in range(2):
                        dve.wait_ge(sem("xtr_high"), 4 * f + 2 * kk + tg + 1)
                        n5 = slice(tg * 512, tg * 512 + 512)
                        v.tensor_tensor(XTr[:, 1, kk, n5], XT[:, kk, n5], XTr[:, 0, kk, n5].bitcast(F32), ALU.subtract)\
                            .then_inc(sem("xtr_done"), 1)

                def low(n, u):
                    dve.wait_ge(sem("h_high"), n + 1)
                    v.tensor_tensor(HTr[:, 1, u % 2, :], tmu[:, u % 2, :], HTr[:, 0, u % 2, :].bitcast(F32), ALU.subtract)\
                        .then_inc(sem("h_low"), 1)

                def unit(i, u):
                    n = i * 8 + (u + base)
                    first = isinstance(i, int)
                    dve.wait_ge(sem("silu_done"), n + 1)
                    dve.wait_ge(sem("up_done"), n + 1)
                    v.tensor_tensor(tmu[:, u % 2, :], sil[:, u % 2, :], PB[2 + u % 2][:, :], ALU.mult).then_inc(sem("t_done"), 1)
                    dve.wait_ge(sem("t_done"), n + 1)
                    dve.wait_ge(sem("spread_done"), n + 1)
                    v.tensor_tensor(tmu[:, u % 2, :], tmu[:, u % 2, :], PB[u % 2][:, :], ALU.mult).then_inc(sem("h_done"), 1)
                    low(n, u)
                    if f == 0:
                        if first:
                            keep_neighbours(0, u)
                        else:
                            keep_neighbours(i, u)

                for u in range(8):
                    unit(0, u)
                with dve.Fori(1, LOOP) as i:
                    if f == 0:
                        link.enter(i, 1, PER_TILE)
                    for u in range(8):
                        unit(i, u)
                if f == 0:
                    link.leave(LOOP - 1)
                    for t in range(LOOP, T):
                        for u in range(8):
                            keep_neighbours(t, u)
                dve.wait_ge(sem("down_done"), 8 * LOOP * (f + 1))
                for q in range(4):
                    xs = X[:, 2 * q:2 * q + 2, :]
                    last = v.tensor_tensor(xs, xs, PB[4 + q][:, :].rearrange("p (s d) -> p s d", s=2), ALU.add)
                done(last)

            def attention(l, stage_, lnk):
                normalize(stage_, lnk)
                if l == 0:
                    dve.wait_ge(sem("rope_loaded"), 32)

                def at(name, value):
                    if not isinstance(value, int) or value > 0:
                        dve.wait_ge(sem(name), value)

                def step(b, h):
                    hb, pb = b * H + l * B * H, b * 8 + l * B * 8
                    inside = lambda m: not isinstance(b, int) or 0 <= b * H + m < B * H
                    m = h + 4
                    if l == 0 and inside(m):
                        at("qbig_done", hb + (m + 1))
                        at("rope_done", hb + (m - 1))
                        v.tensor_tensor(r1[:, m % 2, :], PB[0][0:CH, :], cosq, ALU.mult)
                        v.tensor_tensor(r2[:, m % 2, :], PB[0][0:CH, :], sinq, ALU.mult).then_inc(sem("rope_read"), 1)
                    if inside(h):
                        at("score_done", hb + (h + 1))
                        at("exp_done", hb + (h - 3))
                        v.tensor_reduce(nmx[:, h % 4, :], PB[1 + h % 2][:, :].rearrange("p (s l) -> p s l", s=2), AX.X, ALU.max,
                                        negate=True).then_inc(sem("max_done"), 1)
                    m = h - 1
                    if inside(m):
                        at("pt_done", hb + (m + 1))
                        at("pv_done", hb + (m - 1))
                        v.tensor_copy(PT[:, m % 2, :, :], PB[3][:, :].rearrange("p (l s) -> p l s", l=2)).then_inc(sem("pt_copied"), 1)
                    if h % 2 and inside(h - 3):
                        m = (h - 3) // 2
                        at("pv_done", hb + (2 * m + 2))
                        at("cct_done", pb + (m - 1))
                        o4 = PB[5][:, 0:4 * (C + 1)].rearrange("p (q c) -> p q c", q=4)
                        v.reciprocal(rin[:, m % 2, :], o4[:, :, C]).then_inc(sem("rin_done"), 1)
                        dve.wait_ge(sem("rin_done"), pb + (m + 1))
                        v.tensor_tensor(CC[:, m % 2, :, :].rearrange("p s (h c) -> p h s c", h=2),
                                        o4[:, :, 0:C].rearrange("p (h s) c -> p h s c", h=2),
                                        rin[:, m % 2, :].rearrange("p (h s) -> p h s", h=2).unsqueeze(3).to_broadcast([P, 2, 2, C]),
                                        ALU.mult).then_inc(sem("cc_done"), 1)
                    if (h - 4) % H == 0 and inside(h - 5):
                        bb = b + (h - 5) // H
                        at("y_done", pb + 8 * ((h - 4) // H))
                        xs = X[:, 2 * bb:2 * bb + 2, :] if isinstance(b, int) else X[:, bass.ds(bb * 2, 2), :]
                        v.tensor_tensor(xs, xs, PB[7][:, :].rearrange("p (s d) -> p s d", s=2), ALU.add).then_inc(sem("y_added"), 1)

                for h in range(-4, H):
                    step(0, h)
                with dve.Fori(1, B - 1) as b:
                    for h in range(H):
                        step(b, h)
                for h in range(H + 5):
                    step(B - 1, h)
                    if l == 0 and stages >= 4 and 2 <= h < 11:
                        m, part = divmod(h - 2, 3)
                        w = rF[:, m, :]
                        if part == 0:
                            dve.wait_ge(sem("winv_ready"), 1)
                            v.tensor_scalar(w, w, winv[:, m:m + 1], -1.0, ALU.mult, ALU.max).then_inc(sem("wq_part"), 1)
                        elif part == 1:
                            dve.wait_ge(sem("wq_part"), 2 * m + 1)
                            v.tensor_scalar(w, w, 1.0, RNE, ALU.min, ALU.add).then_inc(sem("wq_part"), 1)
                        else:
                            dve.wait_ge(sem("wq_part"), 2 * m + 2)
                            v.tensor_scalar(WB[:, m, :], w, RNE, None, ALU.subtract).then_inc(sem("wq_ready"), 1)
                dve.wait_ge(sem("y_added"), B * (l + 1))
                done(v.tensor_copy(small[:, 8:9], small[:, 0:1]))

            def quantized():
                normalize(3, None)
                link(v.tensor_reduce(amax, XN[:, :, :], AX.X, ALU.max, apply_absolute_value=True))
                link(v.tensor_scalar(xs8, amax, 1.0 / 127.0, 1e-5, ALU.mult, ALU.add))
                link(v.reciprocal(xr8, xs8))
                for t in range(T):
                    last = v.tensor_scalar(qt[:, t * D:(t + 1) * D], XN[:, t, :], xr8[:, t:t + 1], -128.0, ALU.mult, ALU.max)
                link(last)
                link(v.tensor_scalar(qt, qt, 127.0, RNE, ALU.min, ALU.add))
                v.tensor_scalar(XQ.rearrange("p t d -> p (t d)"), qt, RNE, None, ALU.subtract).then_inc(sem("xq_ready"), 1)
                dve.wait_ge(sem("w_scales"), 1)
                v.tensor_scalar(sg8, xs8, wsum[:, 0:1], None, ALU.mult).then_inc(sem("q_bank_free"), 1)
                link(v.tensor_scalar(su8, xs8, wsum[:, 1:2], None, ALU.mult))
                dve.wait_ge(sem("xqT_done"), 2)
                v.tensor_copy(XQT[:, 1, :], PB[1][:, :].bitcast(BF16)).then_inc(sem("xqT_copied"), 1)

                def col(ap, t):
                    return ap[:, t:t + 1] if isinstance(t, int) else ap[:, bass.ds(t, 1)]

                def hidden(t):
                    v.tensor_scalar(sgc, col(sg8, t), 1.0, None, ALU.mult).then_inc(sem("q_scale"), 1)
                    for c in range(2):
                        dve.wait_ge(sem("q_silu"), t * 2 + (c + 1))
                        dve.wait_ge(sem("q_gu"), t * 4 + (3 + c))
                        last = v.scalar_tensor_tensor(hq[:, c * 512:(c + 1) * 512], PB[2 + c][:, :], col(su8, t), silq[:, c * 512:(c + 1) * 512],
                                                      ALU.mult, ALU.mult)
                        last.then_inc(sem("q_h"), 1)
                    dve.wait_ge(sem("q_h"), t * 2 + 2)
                    link(v.tensor_reduce(hs[:, 0:1], hq, AX.X, ALU.max, apply_absolute_value=True))
                    link(v.tensor_scalar(hs[:, 1:2], hs[:, 0:1], 1.0 / 127.0, 1e-5, ALU.mult, ALU.add))
                    v.tensor_scalar(col(ys8, t), hs[:, 1:2], wsum[:, 2:3], None, ALU.mult)
                    link(v.reciprocal(hs[:, 2:3], hs[:, 1:2]))
                    link(v.tensor_scalar(hq, hq, hs[:, 2:3], -128.0, ALU.mult, ALU.max))
                    link(v.tensor_scalar(hq, hq, 127.0, RNE, ALU.min, ALU.add))
                    if not isinstance(t, int):
                        dve.wait_ge(sem("q_T"), t)
                    v.tensor_scalar(hqb, hq, RNE, None, ALU.subtract).then_inc(sem("q_quant"), 1)

                def add(t, before):
                    dve.wait_ge(sem("q_down"), t + 1 - before)
                    xs = X[:, t:t + 1, :] if isinstance(t, int) else X[:, bass.ds(t - before, 1), :]
                    ysc = ys8[:, t:t + 1] if isinstance(t, int) else ys8[:, bass.ds(t - before, 1)]
                    last = v.scalar_tensor_tensor(xs, PB[5][:, 0:D].unsqueeze(1), ysc, xs, ALU.mult, ALU.add)
                    return last

                hidden(0)
                with dve.Fori(1, T) as t:
                    link.enter(t, 1, 5)
                    hidden(t)
                    add(t, 1).then_inc(sem("q_bank_free"), 1)
                link.leave(T - 1)
                done(add(T - 1, 0))

            def adjacency():
                normalize(4, None)
                v.tensor_scalar(small[:, 4:5], small[:, 3:4], -1.0, 1.0, ALU.mult, ALU.add)
                link(v.tensor_scalar(small[:, 5:6], small[:, 3:4], 0.5, None, ALU.mult))
                for b in range(B):
                    dve.wait_ge(sem("aT_done"), b + 1)
                    ab = A[:, 2 * b:2 * b + 2, :]
                    last = v.tensor_tensor(ab, ab, PB[b][:, :].rearrange("p (s l) -> p s l", s=2), ALU.add)
                link(last)
                link(v.scalar_tensor_tensor(X[:, :, :], XN[:, :, :], small[:, 4:5], X[:, :, :], ALU.mult, ALU.add))
                done(v.scalar_tensor_tensor(X[:, :, :], A[:, :, :], small[:, 5:6], X[:, :, :], ALU.mult, ALU.add))

            def small_experts(lnk):
                normalize(5, lnk)
                lg = PB[4][:, 0:T * E2].rearrange("p (t e) -> p t e", t=T)
                over = lambda col: col.unsqueeze(2).to_broadcast([P, T, E2])
                e8 = slice(0, E2)
                dve.wait_ge(sem("logits2"), 1)
                link(v.tensor_reduce(sc8[:, 0, :], lg, AX.X, ALU.max))
                v.tensor_tensor(pm[:, :, e8], lg, over(sc8[:, 0, :]), ALU.subtract).then_inc(sem("logits2_shifted"), 1)
                dve.wait_ge(sem("logits2_exp"), 1)
                link(v.tensor_reduce(sc8[:, 0, :], pr[:, :, e8], AX.X, ALU.add))
                link(v.reciprocal(sc8[:, 1, :], sc8[:, 0, :]))
                link(v.tensor_tensor(pk[:, :, e8], pr[:, :, e8], over(sc8[:, 1, :]), ALU.mult))
                for t in range(T):
                    last = v.max(top8[:, t, :], pk[:, t, e8])
                link(last)
                for t in range(T):
                    last = v.max_index(idx8[:, t, :], top8[:, t, :], pk[:, t, e8])
                link(last)
                link(v.tensor_copy(idf[:, :, :], idx8[:, :, :]))
                io = iote[:, e8].unsqueeze(1).to_broadcast([P, T, E2])
                link(v.tensor_tensor(pm[:, :, e8], io, over(idf[:, :, 0]), ALU.is_equal))
                link(v.tensor_tensor(pq[:, :, e8], io, over(idf[:, :, 1]), ALU.is_equal))
                link(v.tensor_tensor(pm[:, :, e8], pm[:, :, e8], pq[:, :, e8], ALU.add))
                link(v.tensor_tensor(pr[:, :, e8], pm[:, :, e8], pk[:, :, e8], ALU.mult))
                dve.wait_ge(sem("silu2_done"), 2)
                a4 = a2.rearrange("p t (e i) -> p t e i", e=E2)
                v.tensor_tensor(a4, a4, pr[:, :, e8].unsqueeze(3).to_broadcast([P, T, E2, IE2]), ALU.mult).then_inc(sem("a2_ready"), 1)
                dve.wait_ge(sem("a2T_done"), 2)
                v.tensor_copy(a2T[:, 512:1024], PB[1][:, :]).then_inc(sem("a2T_copied"), 1)
                for q in range(4):
                    dve.wait_ge(sem("y2_done"), q + 1)
                    xs = X[:, 2 * q:2 * q + 2, :]
                    last = v.tensor_tensor(xs, xs, PB[4 + q][:, :].rearrange("p (s d) -> p s d", s=2), ALU.add)
                done(last)

            context()
            dve.wait_ge(sem("x_loaded"), 16)
            l0_attention()
            if stages >= 2:
                ffn(0, 1, 1)
                v.tensor_copy(small[:, 2:3], small[:, 0:1]).then_inc(sem("a_kept"), 1)
            if stages >= 3:
                attention(0, 2, 2)
            if stages >= 4:
                quantized()
            if stages >= 5:
                adjacency()
            if stages >= 6:
                small_experts(3)
            if stages >= 7:
                attention(1, 6, 4)
            if stages >= 8:
                ffn(1, 7, 5)
            v.tensor_copy(small[:, 2:3], small[:, 0:1]).then_inc(sem("x_final"), 1)

        @block.scalar
        def _(act):
            sc = nc.scalar

            def normalize(k, lnk):
                act.wait_ge(sem("ln_stat"), k + 1)
                sc.activation(rstd[:, :], mv[:, :, 1], ACT.Sqrt, bias=epsc[:, 0:1]).then_inc(sem("ln_std"), 1)
                for kk in range(KD if lnk is not None else 0):
                    act.wait_ge(sem("ln_T"), 4 * lnk + 1 + kk)
                    sc.copy(XT[:, kk, 0:512], PB[kk][:, :]).then_inc(sem("xt_act"), 1)

            def context():
                for n in range(2):
                    act.wait_ge(sem("kvT_done"), n + 1)
                    sc.copy(kvT0[:, n * 512:(n + 1) * 512], PB[n][0:C, :]).then_inc(sem("kvT_copied"), 1)
                for n in range(2):
                    act.wait_ge(sem("kvrT_done"), n + 1)
                    sc.copy(kvrT[:, n * 512:(n + 1) * 512], PB[6 + n][:, :]).then_inc(sem("kvrT_copied"), 1)
                act.wait_ge(sem("sim_copied"), 4)
                sc.activation(A[:, :, :], SIM[:, :, :], ACT.Sigmoid, scale=1.0 / 16.0).then_inc(sem("sim_sigmoid"), 1)
                act.wait_ge(sem("consts_loaded"), 16 * 11)
                sc.activation(small[:, 3:4], small[:, 0:1], ACT.Sigmoid)

            def fuse(l, first, end):
                for n in range(first, end):
                    act.wait_ge(sem("fuse_done"), (0, 24)[l] + n + 1)
                    fuse_copy(l, n, sc.copy).then_inc(sem("fuse_copied"), 1)

            def l0_attention():
                normalize(0, 0)
                for n in range(2):
                    act.wait_ge(sem("l0_out"), n + 1)
                    sc.activation(outT[:, n * 512:(n + 1) * 512], PB[4 + n][0:C, :], ACT.Copy, scale=D ** -0.5).then_inc(sem("l0_out_copied"), 1)
                act.wait_ge(sem("l0_stat"), 1)
                sc.activation(rstd[:, :], mv[:, :, 1], ACT.Sqrt, bias=epsc[:, 1:2]).then_inc(sem("l0_std"), 1)
                fuse(0, 0, 12)
                act.wait_ge(sem("l0_shift"), 1)
                sc.activation(XN[:, :, :], XN[:, :, :], ACT.Exp).then_inc(sem("l0_exp"), 1)
                fuse(0, 12, 24)

            def ffn(f, stage, lnk):
                normalize(stage, lnk)
                act.wait_ge(sem("logits_shifted"), f + 1)
                sc.activation(pr[:, :, :], pm[:, :, :], ACT.Exp).then_inc(sem("logits_exp"), 1)
                base = f * 8 * LOOP
                act.wait_ge(sem("xt_dve"), 2 * (lnk + 1))
                for kk in range(KD):
                    for tg in range(2):
                        n5 = slice(tg * 512, tg * 512 + 512)
                        sc.copy(XTr[:, 0, kk, n5], XT[:, kk, n5]).then_inc(sem("xtr_high"), 1)

                def split(i, j, down):
                    n = i * 4 + (j + base // 2)
                    ahead = isinstance(i, int) and i == 0 and j < 2
                    if down:
                        if not ahead:
                            act.wait_ge(sem("down_done"), i * 8 + (2 * j - 2 + base))
                        sc.copy(WDr[:, 0, j % 2, :], ring[:, j // 2 % 2, j % 2 * 768 + 512:j % 2 * 768 + 768]).then_inc(sem("wd_high"), 1)
                    else:
                        if j % 2 == 0:
                            act.wait_ge(sem(f"w_full{j // 2 % 2}"), (i + j // 4) * 16 + (16 + 16 * LOOP * f))
                        if not ahead:
                            act.wait_ge(sem("up_done"), i * 8 + (2 * j - 2 + base))
                        sc.copy(WGr[:, 0, j % 2, :], ring[:, j // 2 % 2, j % 2 * 768:j % 2 * 768 + 512]).then_inc(sem("wg_high"), 1)

                def high(i, u):
                    n = i * 8 + (u + base)
                    act.wait_ge(sem("h_done"), n + 1)
                    if not (isinstance(i, int) and i == 0 and u < 2):
                        act.wait_ge(sem("down_done"), n - 1)
                    sc.copy(HTr[:, 0, u % 2, :], tmu[:, u % 2, :]).then_inc(sem("h_high"), 1)

                def unit(i, u):
                    n = i * 8 + (u + base)
                    act.wait_ge(sem("gate_done"), n + 1)
                    if not (isinstance(i, int) and i == 0 and u < 2):
                        act.wait_ge(sem("t_done"), n - 1)
                    sc.activation(sil[:, u % 2, :], PB[u % 2][:, :], ACT.Silu).then_inc(sem("silu_done"), 1)
                    if u % 2 == 0 and not (isinstance(i, int) and i == LOOP - 1 and u == 6):
                        split(i, u // 2 + 1, False)
                    if u % 2 == 0:
                        split(i, u // 2, True)
                    high(i, u)

                split(0, 0, False)
                for u in range(8):
                    unit(0, u)
                with act.Fori(1, LOOP - 1) as i:
                    for u in range(8):
                        unit(i, u)
                for u in range(8):
                    unit(LOOP - 1, u)

            def attention(l, stage, lnk):
                normalize(stage, lnk)

                def at(name, value):
                    if not isinstance(value, int) or value > 0:
                        act.wait_ge(sem(name), value)

                def step(b, h):
                    hb, pb = b * H + l * B * H, b * 8 + l * B * 8
                    inside = lambda m: not isinstance(b, int) or 0 <= b * H + m < B * H
                    if h % 2 and inside(h + 1):
                        m = (h + 1) // 2
                        at("qc_done", (hb + (2 * m + 2)) if l == 0 else (pb + (m + 1 + B * 8)))
                        src = PB[4] if l == 0 else PB[0]
                        sc.copy(qcT[:, m % 8, :], src[:, 0:S]).then_inc(sem("qc_copied"), 1)
                    if inside(h):
                        at("max_done", hb + (h + 1))
                        at("pt_done", hb + (h - 1))
                        for s in range(2):
                            last = sc.activation(Ex[:, h % 2, s, :], PB[1 + h % 2][:, s * S:(s + 1) * S], ACT.Exp, bias=nmx[:, h % 4, s:s + 1])
                        last.then_inc(sem("exp_done"), 1)
                    if h % 2 == 0 and inside(h - 4):
                        m = (h - 4) // 2
                        at("cct_done", pb + (m + 1))
                        at("y_done", pb + (m - 1))
                        sc.copy(CCT[:, m % 2, :], PB[6][:, 0:S]).then_inc(sem("cct_copied"), 1)

                for h in range(-4, H):
                    step(0, h)
                    if l == 0 and stages >= 4 and h in (9, 11, 13):
                        m = (h - 9) // 2
                        act.wait_ge(sem("w1ffn_loaded"), 16)
                        sc.activation(WB[:, m, :], rF[:, m, :], ACT.Abs, accum_out=wsum[:, m:m + 1]).then_inc(sem("w_abs"), 1)
                with act.Fori(1, B - 1) as b:
                    for h in range(H):
                        step(b, h)
                for h in range(H + 4):
                    step(B - 1, h)

            def quantized():
                normalize(3, None)
                act.wait_ge(sem("xqT_done"), 1)
                sc.copy(XQT[:, 0, :], PB[0][:, :].bitcast(BF16)).then_inc(sem("xqT_copied"), 1)

                def gate(t):
                    act.wait_ge(sem("q_scale"), t + 1)
                    if not isinstance(t, int):
                        act.wait_ge(sem("q_h"), t * 2)
                    for c in range(2):
                        act.wait_ge(sem("q_gu"), t * 4 + (c + 1))
                        sc.activation(silq[:, c * 512:(c + 1) * 512], PB[c][:, :], ACT.Silu, scale=sgc).then_inc(sem("q_silu"), 1)

                def copy(t):
                    act.wait_ge(sem("q_T"), t)
                    sc.copy(hqT, PB[4][:, :].bitcast(BF16)).then_inc(sem("q_Tcopied"), 1)

                gate(0)
                with act.Fori(1, T) as t:
                    gate(t)
                    copy(t)
                copy(T)

            def small_experts(lnk):
                normalize(5, lnk)
                act.wait_ge(sem("logits2_shifted"), 1)
                sc.activation(pr[:, :, 0:E2], pm[:, :, 0:E2], ACT.Exp).then_inc(sem("logits2_exp"), 1)
                for n in range(2):
                    act.wait_ge(sem("h2_done"), n + 1)
                    sc.activation(a2[:, 4 * n:4 * n + 4, :], PB[5 + n][:, :].rearrange("p (t n) -> p t n", t=4), ACT.Silu)\
                        .then_inc(sem("silu2_done"), 1)
                act.wait_ge(sem("a2T_done"), 1)
                sc.copy(a2T[:, 0:512], PB[0][:, :]).then_inc(sem("a2T_copied"), 1)

            context()
            act.wait_ge(sem("eps_set"), 2)
            l0_attention()
            if stages >= 2:
                ffn(0, 1, 1)
            if stages >= 3:
                attention(0, 2, 2)
            if stages >= 4:
                quantized()
            if stages >= 5:
                normalize(4, None)
                fuse(1, 0, 20)
            if stages >= 6:
                small_experts(3)
            if stages >= 7:
                attention(1, 6, 4)
            if stages >= 8:
                ffn(1, 7, 5)

        @block.gpsimd
        def _(pool):
            g = nc.gpsimd
            g.memset(neg1[:, :], -1.0).then_inc(sem("neg1_set"), 1)

            def ffn(f):
                base = f * 8 * LOOP

                def split(i, j, down):
                    n = i * 4 + (j + base // 2)
                    lo, hi = (512, 768) if down else (0, 512)
                    dst, name = (WDr, "wd") if down else (WGr, "wg")
                    pool.wait_ge(sem(name + "_high"), n + 1)
                    g.tensor_tensor(dst[:, 1, j % 2, :], ring[:, j // 2 % 2, j % 2 * 768 + lo:j % 2 * 768 + hi], dst[:, 0, j % 2, :].bitcast(F32),
                                    ALU.subtract).then_inc(sem(name + "_low"), 1)

                def trip(i):
                    for j in range(4):
                        if not (isinstance(i, int) and i == LOOP - 1 and j == 3):
                            split(i, j + 1, False)
                        split(i, j, True)

                split(0, 0, False)
                trip(0)
                with pool.Fori(1, LOOP - 1) as i:
                    trip(i)
                trip(LOOP - 1)

            def attention(l):
                pool.wait_ge(sem("stage_done"), (2, 6)[l])

                def at(name, value):
                    if not isinstance(value, int) or value > 0:
                        pool.wait_ge(sem(name), value)

                def step(b, h):
                    hb, pb = b * H + l * B * H, b * 8 + l * B * 8
                    inside = lambda m: not isinstance(b, int) or 0 <= b * H + m < B * H
                    m = h + 4
                    if l == 0 and inside(m):
                        at("rope_read", hb + (m + 1))
                        at("qc_done", hb + (m - 1))
                        for half in range(2):
                            lo, hi = slice(half * S, half * S + S), slice((1 - half) * S, (1 - half) * S + S)
                            last = g.tensor_tensor(qr[:, m % 2, lo], r1[:, m % 2, lo], r2[:, m % 2, hi], ALU.add)
                        last.then_inc(sem("rope_done"), 1)
                    if h == -1 or h == H - 1 and inside(H):
                        bb = b + (h + 1) // H
                        at("score_done", hb + (h + 1))
                        g.tensor_copy(kvb, kvrT[:, bb * S:bb * S + S] if isinstance(b, int) else kvrT[:, bass.ds(bb * S, S)])\
                            .then_inc(sem("keys_ready"), 1)
                    if h == 1:
                        at("pv_done", hb)
                        g.tensor_copy(kvab, kvaug[:, 2 * b:2 * b + 2, :] if isinstance(b, int) else kvaug[:, bass.ds(b * 2, 2), :])\
                            .then_inc(sem("values_ready"), 1)

                for h in range(-4, H):
                    step(0, h)
                if l == 0 and stages >= 4:
                    weight_scales()
                with pool.Fori(1, B - 1) as b:
                    for h in range(H):
                        step(b, h)
                for h in range(H):
                    step(B - 1, h)

            def weight_scales():
                pool.wait_ge(sem("w_abs"), 3)
                pool.wait_ge(sem("neg1_set"), 1)
                g.partition_all_reduce(wtot[:, :], wsum[:, :], P, bass.bass_isa.ReduceOp.add).then_inc(sem("pool_chain"), 1)
                pool.wait_ge(sem("pool_chain"), 1)
                g.tensor_scalar(wsum[:, :], wtot[:, :], 1.0 / (D * I1), 1e-5, ALU.mult, ALU.add).then_inc(sem("w_scales"), 1)
                pool.wait_ge(sem("w_scales"), 1)
                g.tensor_tensor(winv[:, :], wsum[:, :], neg1[:, :], ALU.pow).then_inc(sem("winv_ready"), 1)

            if stages >= 2:
                ffn(0)
            if stages >= 3:
                attention(0)
            if stages >= 7:
                attention(1)
            if stages >= 8:
                ffn(1)


def bf16_of_01(ones):
    return np.where(ones > 0, 0x3F80, 0).astype(np.uint16)


def layouts(i):
    f = lambda n: np.asarray(i[n])
    c = np.ascontiguousarray
    two = lambda w: c(w.reshape(KD, P, w.shape[1]).transpose(1, 0, 2))
    flat2 = lambda w: two(w).reshape(P, -1)
    a = {"x": f("x"), "ctx": f("ctx_512"), "ctxT": c(f("ctx_512").reshape(TOK, C).T)}
    a["wkaug"] = c(np.concatenate([f("L0_xattn_W_k").T, f("L0_xattn_b_k")[None]], 0))
    a["gamma"], a["beta"] = f("L0_xattn_ln_gamma"), f("L0_xattn_ln_beta")
    a["graw"] = f("L2_xattn_gamma_raw").reshape(1)
    a["wq2"], a["wk2"] = f("L2_xattn_Wq"), f("L2_xattn_Wk")
    a["ident"] = np.eye(P, dtype=np.float32)
    a["identb"] = bf16_of_01(np.eye(P))
    a["iote"] = np.arange(E, dtype=np.float32)
    owner = np.concatenate([np.repeat(np.arange(E), FE), np.full(FS, E), np.full(FT * P - E * FE - FS, -1)])
    sel = (owner[None] == np.arange(EX)[:, None]).astype(np.float32)
    a["sel"] = bf16_of_01(np.concatenate([sel] * 3, 0))

    def groups(gate, up, down):
        pad = lambda w: np.concatenate([w, np.zeros((FT * P - w.shape[0], w.shape[1]), w.dtype)], 0)
        gu = [pad(w).reshape(NG, GRP, P, KD, P).transpose(0, 4, 1, 3, 2) for w in (gate, up)]
        dn = pad(down).reshape(NG, GRP, P, 1, D).transpose(0, 2, 1, 3, 4)
        flat = lambda w: w.reshape(NG, P, GRP, -1)
        return c(np.concatenate([flat(w) for w in gu + [dn]], 3).reshape(NG, P, -1))

    e2 = lambda w: w.reshape(E * FE, D)
    a["w0"] = groups(np.concatenate([e2(f("L0_ffn_w_gate")), f("L0_ffn_ws_gate")]),
                     np.concatenate([e2(f("L0_ffn_w_up")), f("L0_ffn_ws_up")]),
                     np.concatenate([e2(f("L0_ffn_w_down").transpose(0, 2, 1)), f("L0_ffn_ws_down").T]))
    a["w1"] = groups(np.concatenate([e2(f("L3_ffn_w_gate").transpose(0, 2, 1)), f("L3_ffn_sh_gate").T]),
                     np.concatenate([e2(f("L3_ffn_w_up").transpose(0, 2, 1)), f("L3_ffn_sh_up").T]),
                     np.concatenate([e2(f("L3_ffn_w_down")), f("L3_ffn_sh_down")]))
    a["router0"] = flat2(np.concatenate([f("L0_ffn_router_weight"), f("L0_ffn_w_shared_gate")], 0).T)
    a["router1"] = flat2(np.concatenate([f("L3_ffn_router_w").T, f("L3_ffn_sh_gate_w")], 1))

    for l, n in ((0, "L1"), (1, "L3")):
        g = lambda w: f(f"{n}_xattn_{w}")
        a[f"Wq{l}"] = c(g("Wq").reshape(H, HK, D).transpose(1, 0, 2))
        a[f"Wo{l}"] = c(g("Wo").reshape(D, H, HK).transpose(2, 1, 0))
        a[f"Kv{l}"] = c(g("w_kc_kv").transpose(1, 0, 2))
        a[f"Kr{l}"] = c(g("W_kr").transpose(2, 0, 1))
        a[f"Qr{l}"] = c(g("W_qr").transpose(2, 0, 1))
    a["Kq0"] = c(f("L1_xattn_w_kc_q").transpose(1, 0, 2))
    a["Kq1"] = c(f("L3_xattn_w_kc_q").reshape(H, HK, 2, CH).transpose(3, 2, 0, 1))
    a["w1ffn"] = c(np.stack([two(f("L1_ffn_w_gate").T).reshape(P, 2048), two(f("L1_ffn_w_up").T).reshape(P, 2048),
                             f("L1_ffn_w_down").T.reshape(8, P, D).transpose(1, 0, 2).reshape(P, 2048)], 1))
    a["router2"] = two(f("L2_ffn_router_w").T).reshape(P, KD * E2)
    a["w2d"] = two(f("L2_ffn_down_w").reshape(E2 * IE2, D).T)
    a["w2u"] = c(f("L2_ffn_up_w").transpose(0, 2, 1).reshape(E2 * IE2, D))

    def rope(length, dim):
        inv = (np.float32(1.0) / np.power(np.float32(10000.0), np.arange(0, dim, 2, dtype=np.float32) / np.float32(dim))).astype(np.float32)
        ang = np.arange(length, dtype=np.float32)[:, None] * inv[None]
        return np.repeat(np.sin(ang), 2, -1), np.repeat(np.cos(ang), 2, -1)

    sk, ck = rope(S, C)
    sk = np.concatenate([-sk[:, :C // 2], sk[:, C // 2:]], 1)
    a["ropek"] = c(np.stack([ck, sk]).reshape(2, 2, P, C).transpose(2, 0, 1, 3))
    sq, cq = rope(S, CQ)
    a["cosq"] = c(np.concatenate([cq[:, :CH].T, cq[:, CH:].T], 1))
    a["sinq"] = c(np.concatenate([sq[:, CH:].T, -sq[:, :CH].T], 1))
    return a


STAGES = 8


def kernel(**inputs):
    import concourse.bacc as bacc
    from concourse.bass_utils import run_bass_kernel_spmd as run

    nc = bacc.Bacc("TRN2", target_bir_lowering=False, num_devices=1)
    arrays, aps = {}, {}
    for name, v in layouts(inputs).items():
        arrays[f"in_{name}"] = v
        aps[name] = nc.dram_tensor(f"in_{name}", v.shape, mybir.dt.from_np(v.dtype), kind="ExternalInput").ap()
    out = nc.dram_tensor("out", (B, S, D), F32, kind="ExternalOutput").ap()
    build(nc, aps, out, STAGES)
    r = run(nc, [arrays], core_ids=[0])
    return r.results[0]["out"]
```

```python
from contextlib import ExitStack

import numpy as np

import concourse.bass as bass
from concourse import mybir

F32 = mybir.dt.float32
F32R = mybir.dt.float32r
BF16 = mybir.dt.bfloat16
U16 = mybir.dt.uint16
U32 = mybir.dt.uint32
ALU = mybir.AluOpType
ACT = mybir.ActivationFunctionType
AX = mybir.AxisListType

P = 128
B, S, D, C = 4, 256, 256, 64
T = B * S // P
TOK = B * S
KD = D // P
H, HK, CQ, R = 16, 128, 192, 64
CH = CQ // 2
E, FE, FS = 16, 176, 704
EX = E + 1
FT = (E * FE + FS + P - 1) // P
GRP = 2
NG = FT // GRP
LOOP = NG // 2
HALF = TOK // 2
TOPK = 4
I1 = 1024
KEEP = int(S * 0.3)
E2, IE2 = 8, 16
RNE = 1.5 * 2.0 ** 23
BIG = 3.0e38


class Chain:

    def __init__(self, eng, sem):
        self.eng, self.sem, self.base, self.at, self.trip = eng, sem, 0, 0, 0

    def __call__(self, ins):
        ins.then_inc(self.sem, 1)
        self.at += 1
        self.eng.wait_ge(self.sem, self.trip + self.base + self.at)

    def enter(self, i, first, per):
        self.base, self.at, self.first, self.per = self.base + self.at - first * per, 0, first, per
        self.trip = i * per

    def leave(self, trips):
        assert self.at == self.per, (self.at, self.per)
        self.base, self.at, self.trip = self.base + (self.first + trips) * self.per, 0, 0


def build(nc, a, out):
    ctx = ExitStack()
    with ctx:
        def sb(name, shape, dt=F32):
            return ctx.enter_context(nc.sbuf_tensor(name, shape, dt))

        sems = {}

        def sem(name):
            if name not in sems:
                sems[name] = ctx.enter_context(nc.semaphore(name))
            return sems[name]

        PB = [ctx.enter_context(nc.psum_tensor(f"bank{i}", [P, 512], F32)) for i in range(8)]

        X = sb("X", [P, T, D])
        XN = sb("XN", [P, T, D])
        XT = sb("XT", [P, KD, TOK])
        A = sb("A", [P, T, S])
        ident = sb("ident", [P, P])
        identb = sb("identb", [P, P], BF16)
        VW = C + 1
        keys = sb("keys", [P, 2, TOK], F32R)
        values = sb("values", [P, T, VW])
        st6 = sb("st6", [P, T, 6])
        mv = sb("mv", [P, T, 2])
        rstd = sb("rstd", [P, T])
        nmr = sb("nmr", [P, T])
        epsc = sb("epsc", [P, 2])
        sc8 = sb("sc8", [P, 3, T])
        small = sb("small", [P, 16])
        WB = sb("WB", [P, 3, 2048], BF16)
        WF = sb("WF", [P, 6144])
        RF = sb("RF", [P, 2048])
        PF = sb("PF", [P, 8, D])
        RAW = sb("RAW", [P, 2, 4352])
        iote = sb("iote", [P, E])
        wr01 = sb("wr01", [P, 2, KD * EX])
        wr2 = sb("wr2", [P, KD * E2])
        PH = sb("PH", [P, 10240])

        PR = sb("PR", [P, 9216], F32R)
        XTr = PR[:, 0:4096].rearrange("p (a k n) -> p a k n", a=2, k=KD)
        WGr = PR[:, 4096:6144].rearrange("p (a j w) -> p a j w", a=2, j=2)
        WDr = PR[:, 6144:7168].rearrange("p (a j w) -> p a j w", a=2, j=2)
        HTr = PR[:, 7168:9216].rearrange("p (a q w) -> p a q w", a=2, q=2)

        Q2 = PR[:, 0:1024].rearrange("p (g s) -> p g s", g=4)
        CCr = PR[:, 3072:4096].rearrange("p (q a s) -> p q a s", q=2, a=2)
        PFr = PR[:, 4096:8192].rearrange("p (a g d) -> p a g d", a=2, g=8)

        ctxT = PH[0:C + 1, 4352:4352 + TOK]
        wkaug = PH[0:C + 1, 5376:5376 + C]
        wq2 = PH[0:C, 5440:5440 + C]
        wk2 = PH[0:C, 5504:5504 + C]
        n2 = PH[0:C, 5568:5568 + C]
        uT = PH[0:C, 5632:5632 + TOK]
        ctok = PH[:, 6656:7168].rearrange("p (t c) -> p t c", t=T)
        kvdup = PH[:, 7168:8192].rearrange("p (t a c) -> p t a c", t=T, a=2)
        SIM = PH[:, 8192:8192 + T * S].rearrange("p (t s) -> p t s", t=T)
        kvT0 = PH[0:C, 0:TOK]
        kv0 = PH[:, 1024:1024 + T * C].rearrange("p (t c) -> p t c", t=T)
        outT = PH[0:C, 1536:1536 + TOK]
        gam = PH[:, 2560:2816]
        bet = PH[:, 2816:3072]
        ropek = PH[:, 3072:3072 + 2 * 2 * C].rearrange("p (a s c) -> p a s c", a=2, s=2)
        kt1 = PH[:, 3328:3328 + T * C].rearrange("p (t c) -> p t c", t=T)
        kt2 = PH[:, 3840:3840 + T * C].rearrange("p (t c) -> p t c", t=T)

        ring = PH[:, 0:3072].rearrange("p (g w) -> p g w", g=2)
        selr = PH[0:3 * EX, 3072:3328].bitcast(BF16).rearrange("p (g w) -> p g w", g=2)
        sil = PH[:, 3328:4352].rearrange("p (q w) -> p q w", q=2)
        tmu = PH[:, 4352:5376].rearrange("p (q w) -> p q w", q=2)
        SCT = PH[0:3 * EX, 5376:5888].bitcast(BF16)
        o = 5888
        pr = PH[:, o:o + T * EX].rearrange("p (t e) -> p t e", t=T); o += T * EX
        pm = PH[:, o:o + T * EX].rearrange("p (t e) -> p t e", t=T); o += T * EX
        pk = PH[:, o:o + T * E].rearrange("p (t e) -> p t e", t=T); o += T * E
        pq = PH[:, o:o + T * E].rearrange("p (t e) -> p t e", t=T); o += T * E
        top8 = PH[:, o:o + T * 8].rearrange("p (t e) -> p t e", t=T); o += T * 8
        idx8 = PH[:, o:o + T * 8].bitcast(U32).rearrange("p (t e) -> p t e", t=T); o += T * 8
        idf = PH[:, o:o + T * 8].rearrange("p (t e) -> p t e", t=T); o += T * 8
        scp = PH[:, o:o + T * 3 * EX // 2].bitcast(BF16).rearrange("p (t c e) -> p t c e", t=T, c=3); o += T * 3 * EX // 2
        twork = PH[:, o:o + S]; o += S
        tmax = PH[:, o:o + 8]; o += 8
        assert o <= 8192

        Ex = PH[:, 0:2048].rearrange("p (q s l) -> p q s l", q=4, s=2)
        PT = PH[:, 3072:4096].rearrange("p (q l s) -> p q l s", q=2, l=2)
        CC = PH[:, 4096:4608].rearrange("p (q s c) -> p q s c", q=2, s=2)
        CCT = PH[:, 4608:5120].rearrange("p (q s) -> p q s", q=2)
        nmx = PH[:, 5506:5514].rearrange("p (q s) -> p q s", q=4)
        rin = PH[:, 5514:5522].rearrange("p (q s) -> p q s", q=2)
        cosq = PH[0:CH, 5632:6144]
        sinq = PH[0:CH, 6144:6656]
        r1 = PH[0:CH, 6656:7680].rearrange("p (q s) -> p q s", q=2)
        r2 = PH[0:CH, 7680:8704].rearrange("p (q s) -> p q s", q=2)
        qr = PH[0:CH, 8704:9728].rearrange("p (q s) -> p q s", q=2)
        W1 = WF[:, :].rearrange("p (k h q) -> p k h q", k=KD, h=H)
        MF = WF[:, 0:2048].rearrange("p (k w) -> p k w", k=KD)
        GF = WF[:, 2048:3072].rearrange("p (h c) -> p h c", h=H)
        RFv = RF[0:CH, :].rearrange("p (h f c) -> p h f c", h=H, f=2)
        rWq = RAW[:, :, 0:1024].rearrange("p g (h d) -> p g h d", h=4)
        rWo = RAW[:, :, 1024:2048].rearrange("p g (h d) -> p g h d", h=4)
        rKv = RAW[:, :, 2048:2304].rearrange("p g (h c) -> p g h c", h=4)
        rKr = RAW[0:R, :, 2304:2560].rearrange("p g (h c) -> p g h c", h=4)
        rQr = RAW[0:R, :, 2560:3328].rearrange("p g (h q) -> p g h q", h=4)
        rKq = RAW[:, :, 3328:4096].rearrange("p g (h q) -> p g h q", h=4)
        rKqT = RAW[0:CH, :, 3328:4352].rearrange("p g (f h k) -> p g f h k", f=2, h=4)

        rF = RAW[:, :, :].rearrange("p g w -> p (g w)")[:, 0:6144].rearrange("p (m w) -> p m w", m=3)
        XQ = PH[:, 0:1024].bitcast(BF16).rearrange("p (t d) -> p t d", t=T)
        XQT = PH[:, 1024:2048].bitcast(BF16).rearrange("p (k n) -> p k n", k=KD)
        qt = PH[:, 2048:4096]
        silq = PH[:, 4096:5120]
        hq = PH[:, 5120:6144]
        hqb = PH[:, 6144:6656].bitcast(BF16)
        hqT = PH[:, 6656:7168].bitcast(BF16)
        q8 = PH[:, 7168:7232].rearrange("p (c t) -> p c t", c=8)
        amax, xs8, xr8, sg8, su8, ys8 = (q8[:, n, :] for n in range(6))
        hs = PH[:, 7232:7240]
        wstat = sb("wstat", [P, 12])
        wsum, wtot, winv, neg1 = (wstat[:, 3 * n:3 * n + 3] for n in range(4))

        w2d = PH[:, 7296:7552].rearrange("p (k n) -> p k n", k=KD)
        w2u = PH[:, 7552:7808]
        a2 = PH[:, 8832:9856].rearrange("p (t n) -> p t n", t=T)
        a2T = PH[:, 0:1024]

        FUSED = (6, 5)

        def fused_bank(l, n):
            return PB[4 + n % 4] if l == 0 else PB[6 + n % 2]

        def fuse_copy(l, n, copy):
            src = fused_bank(l, n)
            g, part = divmod(n, FUSED[l])
            if part == 0:
                return copy(RF[0:CH, g * 512:(g + 1) * 512], src[0:CH, :])
            if part == 1:
                return copy(PF[:, 2 * g:2 * g + 2, :], src[:, :].rearrange("p (g d) -> p g d", g=2))
            if l == 0:
                k, q = divmod(part - 2, 2)
                h = 4 * g + 2 * q
                return copy(W1[:, k, h:h + 2, :], src[:, 0:2 * CQ].rearrange("p (h q) -> p h q", h=2))
            if part == 2:
                return copy(GF[:, 4 * g:4 * g + 4, :], src[:, 0:256].rearrange("p (h c) -> p h c", h=4))
            return copy(MF[:, part - 3, g * 256:(g + 1) * 256], src[:, 0:256])

        EARLY = 12
        FUSE_SHARE = [range(4 * FUSED[1] * t // T, 4 * FUSED[1] * (t + 1) // T) for t in range(T)]

        block = ctx.enter_context(nc.Block())
        LOGITS = (PB[0], PB[4])

        @block.sync
        def _(sp):
            sp.dma_start(X[:, :, :], a["x"].rearrange("b (s p) d -> p (b s) d", p=P)).then_inc(sem("x_loaded"), 16)
            for dst, name in ((ident[:, :], "ident"), (ctxT[0:C, :], "ctxT"), (wkaug, "wkaug"), (wq2, "wq2"), (wk2, "wk2"),
                              (ctok, None), (ropek, "ropek"), (identb[:, :].bitcast(U16), "identb")):
                src = a[name] if name else a["ctx"].rearrange("b (s p) c -> p (b s) c", p=P)
                sp.dma_start(dst, src).then_inc(sem("consts_loaded"), 16)
            sp.dma_start(gam, a["gamma"].partition_broadcast(P)).then_inc(sem("consts_loaded"), 16)
            sp.dma_start(bet, a["beta"].partition_broadcast(P)).then_inc(sem("consts_loaded"), 16)
            sp.dma_start(small[:, 0:1], a["graw"].partition_broadcast(P)).then_inc(sem("consts_loaded"), 16)

            sp.dma_start(iote[:, :], a["iote"].partition_broadcast(P)).then_inc(sem("router_loaded"), 16)
            for dst, name in ((wr01[:, 0, :], "router0"), (wr01[:, 1, :], "router1"), (wr2[:, :], "router2")):
                sp.dma_start(dst, a[name]).then_inc(sem("router_loaded"), 16)

            def ffn_weights(f):
                w, sel = a[f"w{f}"], a["sel"]
                sp.wait_ge(sem("stage_done"), (1, 7)[f])
                for g in range(2):
                    sp.dma_start(ring[:, g, :], w[g]).then_inc(sem(f"w_full{g}"), 16)
                    sp.dma_start(selr[:, g, :].bitcast(U16), sel[:, g * 256:(g + 1) * 256]).then_inc(sem(f"sel_full{g}"), 16)
                with sp.Fori(1, LOOP) as i:
                    for g in range(2):
                        sp.wait_ge(sem("wd_low"), i * 4 + (4 * LOOP * f - 4 + 2 * (g + 1)))
                        sp.dma_start(ring[:, g, :], w[bass.ds(i * 2 + g, 1)].rearrange("g p w -> p (g w)")).then_inc(sem(f"w_full{g}"), 16)
                        sp.wait_ge(sem("spread_done"), i * 8 + (8 * LOOP * f - 8 + 4 * (g + 1)))
                        sp.dma_start(selr[:, g, :].bitcast(U16), sel[:, bass.ds(i * 512 + g * 256, 256)]).then_inc(sem(f"sel_full{g}"), 16)

            def attention_weights(l):
                for g in range(4):
                    if g >= 2:
                        sp.wait_ge(sem("fuse_done"), (0, 24)[l] + FUSED[l] * (g - 1))
                    for dst, name in ((rWq, "Wq"), (rWo, "Wo"), (rKv, "Kv"), (rKr, "Kr"), (rQr, "Qr")):
                        sp.dma_start(dst[:, g % 2], a[f"{name}{l}"][:, 4 * g:4 * g + 4, :]).then_inc(sem(f"raw_loaded{g % 2}"), 16)
                    if l == 0:
                        sp.dma_start(rKq[:, g % 2], a["Kq0"][:, 4 * g:4 * g + 4, :]).then_inc(sem(f"raw_loaded{g % 2}"), 16)
                    else:
                        sp.dma_start(rKqT[:, g % 2], a["Kq1"][:, :, 4 * g:4 * g + 4, :]).then_inc(sem(f"raw_loaded{g % 2}"), 16)

            attention_weights(0)
            ffn_weights(0)
            sp.wait_ge(sem("fuse_done"), 24)
            sp.dma_start(rF, a["w1ffn"]).then_inc(sem("w1ffn_loaded"), 16)
            sp.wait_ge(sem("stage_done"), 2)
            sp.dma_start(cosq, a["cosq"]).then_inc(sem("rope_loaded"), 16)
            sp.dma_start(sinq, a["sinq"]).then_inc(sem("rope_loaded"), 16)
            sp.wait_ge(sem("stage_done"), 3)
            sp.dma_start(w2d, a["w2d"]).then_inc(sem("w2_loaded"), 16)
            sp.dma_start(w2u, a["w2u"]).then_inc(sem("w2_loaded"), 16)
            sp.wait_ge(sem("wq_ready"), 3)
            attention_weights(1)
            ffn_weights(1)
            sp.wait_ge(sem("x_final"), 1)
            sp.dma_start(out.rearrange("b (s p) d -> p (b s) d", p=P), X[:, :, :]).then_inc(sem("stored"), 16)
            sp.wait_ge(sem("stored"), 16)

        @block.tensor
        def _(pe):
            mm = nc.tensor.matmul

            def ln_transposes(stage, k):
                for tg in range(2):
                    for kk in range(KD):
                        for q in range(4):
                            t = tg * 4 + q
                            pe.wait_ge(sem(("ln_x", "ln_x_act")[tg]), 4 * stage + q + 1)
                            last = nc.tensor.transpose(PB[tg * 2 + kk][:, q * P:(q + 1) * P],
                                                       XN[:, t, kk * P:(kk + 1) * P], ident[:, :])
                        last.then_inc(sem("ln_T"), 1)
                pe.wait_ge(sem("xt_act"), 2 * (k + 1))
                pe.wait_ge(sem("xt_dve"), 2 * (k + 1))

            def context():
                pe.wait_ge(sem("consts_loaded"), 16 * 11)
                pe.wait_ge(sem("ctx_ones"), 1)
                for n in range(2):
                    mm(PB[4 + n][0:C, :], wkaug, ctxT[:, n * 512:(n + 1) * 512], start=True, stop=True).then_inc(sem("kvT_done"), 1)
                for t in range(T):
                    last = mm(PB[6][:, t * C:(t + 1) * C], ctxT[:, t * P:(t + 1) * P], wkaug, start=True, stop=True)
                last.then_inc(sem("kv_done"), 1)
                mm(PB[7][0:C, 0:C], wq2, wk2, start=True, stop=True).then_inc(sem("n2_done"), 1)

            def l0_attention():
                ln_transposes(0, 0)
                pe.wait_ge(sem("kv_copied"), 1)
                pe.wait_ge(sem("kvT_copied"), 2)
                for b in range(B):
                    for k in range(KD):
                        last = mm(PB[4 + b // 2][0:C, (b % 2) * S:(b % 2 + 1) * S], kv0[:, 2 * b + k, :],
                                  XT[:, k, b * S:(b + 1) * S], start=(k == 0), stop=(k == KD - 1))
                    if b % 2:
                        last.then_inc(sem("l0_out"), 1)
                pe.wait_ge(sem("kvr_ready"), 1)
                pe.wait_ge(sem("n2_copied"), 1)
                for n in range(2):
                    for q in range(4):
                        t = 4 * n + q
                        last = nc.tensor.transpose(PB[6 + n][:, q * P:(q + 1) * P],
                                                   kvdup[:, t, :, :].rearrange("p a c -> p (a c)"), ident[:, :])
                    last.then_inc(sem("kvrT_done"), 1)
                pe.wait_ge(sem("l0_out_copied"), 2)
                for t in range(T):
                    b = t // 2
                    last = mm(PB[b][:, (t % 2) * S:(t % 2 + 1) * S], outT[:, t * P:(t + 1) * P], kvT0[:, b * S:(b + 1) * S],
                              start=True, stop=True)
                    if t % 2:
                        last.then_inc(sem("l0_sim"), 1)

            def similarity():
                for n in range(2):
                    mm(PB[4 + n][0:C, :], n2, ctxT[0:C, n * 512:(n + 1) * 512], start=True, stop=True).then_inc(sem("uT_done"), 1)
                pe.wait_ge(sem("keys_low"), 2)
                pe.wait_ge(sem("uT_copied"), 2)
                for t in range(T):
                    b = t // 2
                    last = mm(PB[4 + b][:, (t % 2) * S:(t % 2 + 1) * S], uT[:, t * P:(t + 1) * P], ctxT[0:C, b * S:(b + 1) * S],
                              start=True, stop=True)
                    if t % 2:
                        last.then_inc(sem("sim_done"), 1)
                pe.wait_ge(sem("sim_copied"), 4)

            def ffn(f, stage, lnk):
                ln_transposes(stage, lnk)
                pe.wait_ge(sem("router_loaded"), 64)
                wr = wr01[:, f, :].rearrange("p (k e) -> p k e", k=KD)
                for t in range(T):
                    for k in range(KD):
                        last = mm(LOGITS[f][:, t * EX:(t + 1) * EX], XT[:, k, t * P:(t + 1) * P], wr[:, k, :],
                                  start=(k == 0), stop=(k == KD - 1))
                last.then_inc(sem("logits"), 1)
                base = f * 8 * LOOP

                HI_LO = ((0, 0), (0, 1), (1, 0))
                pe.wait_ge(sem("xtr_done"), 4 * (f + 1))

                def gate_up(i, u):
                    jj, half = u // 2 % 2, u % 2
                    n = i * 8 + (u + base)
                    if half == 0:
                        pe.wait_ge(sem("wg_high"), i * 4 + (u // 2 + 1 + base // 2))
                        pe.wait_ge(sem("wg_low"), i * 4 + (u // 2 + 1 + base // 2))
                    if not (isinstance(i, int) and i == 0 and u < 2):
                        pe.wait_ge(sem("h_done"), n - 1)
                    for dst, w, done in ((PB[u % 2], 0, "gate_done"), (PB[2 + u % 2], 256, "up_done")):
                        for k in range(KD):
                            for x, y in HI_LO:
                                last = mm(dst[:, :], WGr[:, x, jj, w + k * P:w + (k + 1) * P], XTr[:, y, k, half * HALF:(half + 1) * HALF],
                                          start=(k == 0 and x + y == 0), stop=(k == KD - 1 and x == 1))
                        last.then_inc(sem(done), 1)

                def spread(i, u):
                    g, jj, half = u // 4, u // 2 % 2, u % 2
                    if u % 4 == 0:
                        pe.wait_ge(sem(f"sel_full{g}"), i * 16 + (16 + 16 * LOOP * f))
                    pe.wait_ge(sem("silu_done"), i * 8 + (u + base + 1))
                    mm(PB[u % 2][:, :], selr[:, g, jj * P:(jj + 1) * P], SCT[:, half * HALF:(half + 1) * HALF],
                       start=True, stop=True).then_inc(sem("spread_done"), 1)

                def down(i, u, first=False):
                    jj, half = u // 2 % 2, u % 2
                    if half == 0:
                        pe.wait_ge(sem("wd_high"), i * 4 + (u // 2 + 1 + base // 2))
                        pe.wait_ge(sem("wd_low"), i * 4 + (u // 2 + 1 + base // 2))
                    pe.wait_ge(sem("h_low"), i * 8 + (u + base + 1))
                    for q in range(4):
                        for x, y in HI_LO:
                            last = mm(PB[4 + half * 2 + q // 2][:, (q % 2) * D:(q % 2 + 1) * D], HTr[:, x, u % 2, q * P:(q + 1) * P],
                                      WDr[:, y, jj, :], start=(first and q % 2 == 0 and x + y == 0), stop=False, skip_group_check=True)
                    last.then_inc(sem("down_done"), 1)

                def scores_transposed():
                    pe.wait_ge(sem("scores_split"), f + 1)
                    scT = PB[5][:, :].bitcast(BF16)
                    for t in range(T):
                        last = nc.tensor.transpose(scT[0:3 * EX, t * P:(t + 1) * P], scp[:, t, :, :].rearrange("p c e -> p (c e)"), identb[:, :])
                    last.then_inc(sem("scoresT"), 1)
                    pe.wait_ge(sem("scoresT_copied"), f + 1)

                def trip(i, first):
                    for u in range(8):
                        if not (first and u < 2):
                            gate_up(i, u)
                        if not (first and u < 1):
                            spread(i if u else i - 1, (u - 1) % 8)
                        if not (first and u < 2):
                            down(i if u > 1 else i - 1, (u - 2) % 8, first=first and u - 2 < 2)

                if f == 0:
                    fuse(0, range(EARLY, 24))
                gate_up(0, 0)
                gate_up(0, 1)
                pe.wait_ge(sem("fuse_copied"), (24, 44)[f])
                scores_transposed()
                trip(0, True)
                with pe.Fori(1, LOOP) as i:
                    trip(i, False)
                spread(LOOP - 1, 7)
                down(LOOP - 1, 6)
                down(LOOP - 1, 7)

            def fuse(l, some):
                for n in some:
                    fuse_step(l, n)

            def fuse_step(l, n):
                base = (0, 24)[l]
                g, part = divmod(n, FUSED[l])
                e = g % 2
                dst = fused_bank(l, n)
                ring = (4, 2)[l]
                if n >= ring:
                    pe.wait_ge(sem("fuse_copied"), base + n - ring + 1)
                if part == 0:
                    pe.wait_ge(sem(f"raw_loaded{g % 2}"), 96 * (2 * l + g // 2 + 1))
                    for q in range(4):
                        for half in range(2):
                            last = mm(dst[0:CH, (q * 2 + half) * C:(q * 2 + half + 1) * C], rQr[:, e, q, half * CH:(half + 1) * CH],
                                      rKr[:, e, q, :], start=True, stop=True)
                elif part == 1:
                    for q in range(4):
                        last = mm(dst[(q % 2) * C:(q % 2 + 1) * C, (q // 2) * D:(q // 2 + 1) * D], rKv[:, e, q, :], rWo[:, e, q, :],
                                  start=True, stop=True)
                elif l == 0:
                    k, q2 = divmod(part - 2, 2)
                    for q in range(2):
                        last = mm(dst[:, q * CQ:(q + 1) * CQ], rWq[:, e, 2 * q2 + q, k * P:(k + 1) * P], rKq[:, e, 2 * q2 + q, :],
                                  start=True, stop=True)
                elif part == 2:
                    pe.wait_ge(sem("fuse_copied"), base + 5 * g + 1)
                    for q in range(4):
                        for half in range(2):
                            last = mm(dst[:, q * C:(q + 1) * C], rKqT[:, e, half, q, :], RFv[:, 4 * g + q, half, :],
                                      start=(half == 0), stop=(half == 1))
                else:
                    pe.wait_ge(sem("fuse_copied"), base + 5 * g + 3)
                    k = part - 3
                    for q in range(4):
                        last = mm(dst[:, q * C:(q + 1) * C], rWq[:, e, q, k * P:(k + 1) * P], GF[:, 4 * g + q, :],
                                  start=True, stop=True)
                last.then_inc(sem("fuse_done"), 1)

            def attention(l, stage, lnk):
                ln_transposes(stage, lnk)
                HI_LO = ((0, 0), (0, 1), (1, 0))

                def at(name, value):
                    if not isinstance(value, int) or value > 0:
                        pe.wait_ge(sem(name), value)

                def step(b, h):
                    hb, pb = b * H + l * B * H, b * 8 + l * B * 8
                    inside = lambda m: not isinstance(b, int) or 0 <= b * H + m < B * H

                    def cols(m):
                        bb = b + m // H
                        return slice(bb * S, bb * S + S) if isinstance(b, int) else bass.ds(bb * S, S)

                    m = h - 2
                    if inside(m):
                        at("exp_done", hb + (m + 1))
                        bank, ago = (PB[3], 1) if l == 0 else (PB[3 + m % 2], 2)
                        at("pt_copied", hb + (m + 1 - ago))
                        for k in range(2):
                            for s in range(2):
                                last = nc.tensor.transpose(bank[:, k * S + s * P:k * S + (s + 1) * P], Ex[:, m % 4, s, k * P:(k + 1) * P],
                                                           ident[:, :])
                        last.then_inc(sem("pt_done"), 1)
                    m = h + 2
                    if l == 0 and inside(m):
                        at("rope_done", hb + (m + 1))
                        if m % 2 == 0:
                            at("q_low", pb + m // 2)
                        for half in range(2):
                            last = mm(PB[4][(m % 2) * C:(m % 2 + 1) * C, 0:S], RFv[:, m % H, half, :], qr[:, m % 2, half * S:(half + 1) * S],
                                      start=(half == 0), stop=(half == 1))
                        last.then_inc(sem("qc_done"), 1)
                    m = h + 4
                    if l == 0 and inside(m):
                        at("rope_read", hb + m)
                        for half in range(2):
                            for k in range(KD):
                                last = mm(PB[0][0:CH, half * S:(half + 1) * S], W1[:, k, m % H, half * CH:(half + 1) * CH], XT[:, k, cols(m)],
                                          start=(k == 0), stop=(k == KD - 1))
                        last.then_inc(sem("qbig_done"), 1)
                    if l == 1 and h % 2 == 0 and inside(h + 2):
                        m = (h + 2) // 2
                        at("q_low", pb + m)
                        for k in range(KD):
                            last = mm(PB[0][:, 0:S], MF[:, k, (m % 8) * P:(m % 8 + 1) * P], XT[:, k, cols(h + 2)], start=(k == 0), stop=(k == KD - 1))
                        last.then_inc(sem("qc_done"), 1)
                    if inside(h):
                        at("q_low", pb + (h // 2 + 1))
                        at("exp_done", hb + (h - 1))
                        for s in range(2):
                            for y in range(2):
                                last = mm(PB[1 + h % 2][:, s * S:(s + 1) * S], Q2[:, h % 4, s * P:(s + 1) * P], keys[:, y, cols(h)],
                                          start=(y == 0), stop=(y == 1))
                        last.then_inc(sem("score_done"), 1)
                    m = h - 3
                    if inside(m):
                        at("pt_copied", hb + (m + 1))
                        if m % 2 == 0:
                            at("cc_done", pb + m // 2)
                        for s in range(2):
                            o = ((m % 2) * 2 + s) * VW
                            for k in range(2):
                                tile = (b + m // H) * 2 + k
                                tile = slice(tile, tile + 1) if isinstance(b, int) else bass.ds(tile, 1)
                                last = mm(PB[5][:, o:o + VW], PT[:, m % 2, k, s * P:(s + 1) * P],
                                          values[:, tile, :].rearrange("p t c -> p (t c)"), start=(k == 0), stop=(k == 1))
                        last.then_inc(sem("pv_done"), 1)
                    if h % 2 and inside(h - 5):
                        m = (h - 5) // 2
                        at("cc_done", pb + (m + 1))
                        at("cct_copied", pb + m)
                        for s in range(2):
                            last = nc.tensor.transpose(PB[6][:, s * P:(s + 1) * P], CC[:, m % 2, s, :], ident[:, :])
                        last.then_inc(sem("cct_done"), 1)
                    if h % 2 and inside(h - 7):
                        m = (h - 7) // 2
                        at("cct_low", pb + (m + 1))
                        if m == 0:
                            at("y_added", b + l * B)
                            at("pf_low", 4 * (l + 1))
                        for s in range(2):
                            for x, y in HI_LO:
                                last = mm(PB[7][:, s * D:(s + 1) * D], CCr[:, m % 2, x, s * P:(s + 1) * P], PFr[:, y, m % 8, :],
                                          start=(m % 8 == 0 and s == 0 and x + y == 0), stop=False, skip_group_check=True)
                        last.then_inc(sem("y_done"), 1)

                for h in range(-4, H):
                    step(0, h)
                with pe.Fori(1, B - 1) as b:
                    for h in range(H):
                        step(b, h)
                for h in range(H + 6):
                    step(B - 1, h)

            def adjacency():
                pe.wait_ge(sem("a_scaled"), 1)
                for b in range(B):
                    for r in range(2):
                        for c in range(2):
                            last = nc.tensor.transpose(PB[b][:, r * S + c * P:r * S + (c + 1) * P], A[:, 2 * b + c, r * P:(r + 1) * P], ident[:, :])
                    last.then_inc(sem("aT_done"), 1)

            def quantized():
                xqT = [PB[k][:, :].bitcast(BF16) for k in range(KD)]
                pe.wait_ge(sem("xq_ready"), 1)
                for k in range(KD):
                    for t in range(T):
                        last = nc.tensor.transpose(xqT[k][:, t * P:(t + 1) * P], XQ[:, t, k * P:(k + 1) * P], identb[:, :])
                    last.then_inc(sem("xqT_done"), 1)
                pe.wait_ge(sem("xqT_copied"), 2)
                pe.wait_ge(sem("wq_ready"), 3)

                def gate_up(t):
                    if t:
                        pe.wait_ge(sem("q_silu"), t * 2)
                        pe.wait_ge(sem("q_h"), t * 2)
                    for m in range(2):
                        for c in range(2):
                            for k in range(KD):
                                last = mm(PB[2 * m + c][:, :], XQT[:, k, t * P:(t + 1) * P], WB[:, m, k * I1 + c * 512:k * I1 + c * 512 + 512],
                                          start=(k == 0), stop=(k == KD - 1))
                            last.then_inc(sem("q_gu"), 1)

                def transposes(t):
                    hT = PB[4][:, :].bitcast(BF16)
                    pe.wait_ge(sem("q_quant"), t + 1)
                    for c in range(8):
                        last = nc.tensor.transpose(hT[:, c * P:(c + 1) * P], hqb[:, c * P:(c + 1) * P], identb[:, :])
                    last.then_inc(sem("q_T"), 1)

                def down(t):
                    pe.wait_ge(sem("q_Tcopied"), t + 1)
                    pe.wait_ge(sem("q_bank_free"), t + 1)
                    for c in range(8):
                        last = mm(PB[5][:, 0:D], hqT[:, c * P:(c + 1) * P], WB[:, 2, c * D:(c + 1) * D], start=(c == 0), stop=(c == 7))
                    last.then_inc(sem("q_down"), 1)

                for t in range(T):
                    gate_up(t)
                    fuse(1, FUSE_SHARE[t][:-1])
                    if t:
                        transposes(t - 1)
                    fuse(1, FUSE_SHARE[t][-1:])
                    if t:
                        down(t - 1)
                pe.wait_ge(sem("q_silu"), 2 * T)
                pe.wait_ge(sem("q_h"), 2 * T)
                adjacency()
                transposes(T - 1)
                down(T - 1)

            def small_experts(stage, lnk):
                ln_transposes(stage, lnk)
                for t in range(T):
                    for k in range(KD):
                        last = mm(PB[4][:, t * E2:(t + 1) * E2], XT[:, k, t * P:(t + 1) * P], wr2[:, k * E2:(k + 1) * E2],
                                  start=(k == 0), stop=(k == KD - 1))
                last.then_inc(sem("logits2"), 1)
                pe.wait_ge(sem("w2_loaded"), 32)
                for t in range(T):
                    for k in range(KD):
                        last = mm(PB[5 + t // 4][:, (t % 4) * P:(t % 4 + 1) * P], XT[:, k, t * P:(t + 1) * P], w2d[:, k, :],
                                  start=(k == 0), stop=(k == KD - 1))
                    if t % 4 == 3:
                        last.then_inc(sem("h2_done"), 1)
                pe.wait_ge(sem("a2_ready"), 1)
                for t in range(T):
                    last = nc.tensor.transpose(PB[t // 4][:, (t % 4) * P:(t % 4 + 1) * P], a2[:, t, :], ident[:, :])
                    if t % 4 == 3:
                        last.then_inc(sem("a2T_done"), 1)
                pe.wait_ge(sem("a2T_copied"), 2)
                for t in range(T):
                    last = mm(PB[4 + t // 2][:, (t % 2) * D:(t % 2 + 1) * D], a2T[:, t * P:(t + 1) * P], w2u, start=True, stop=True)
                    if t % 2:
                        last.then_inc(sem("y2_done"), 1)

            context()
            l0_attention()
            similarity()
            fuse(0, range(EARLY))
            ffn(0, 1, 1)
            attention(0, 2, 2)
            quantized()
            small_experts(5, 3)
            attention(1, 6, 4)
            ffn(1, 7, 5)

        @block.vector
        def _(dve):
            v = nc.vector
            link = Chain(dve, sem("dve_chain"))
            stage = [0]

            def done(ins):
                stage[0] += 1
                ins.then_inc(sem("stage_done"), 1)
                dve.wait_ge(sem("stage_done"), stage[0])

            def normalize(k, lnk, meanwhile=None):
                for t in range(T):
                    v.bn_stats(st6[:, t, :], X[:, t, :]).then_inc(sem("dve_stats"), 1)
                for t in range(T):
                    dve.wait_ge(sem("dve_stats"), 8 * k + t + 1)
                    last = v.bn_aggr(mv[:, t, :], st6[:, t, :])
                last.then_inc(sem("ln_stat"), 1)
                dve.wait_ge(sem("ln_std"), k + 1)
                link(v.reciprocal(rstd[:, :], rstd[:, :]))
                v.scalar_tensor_tensor(nmr[:, :], mv[:, :, 0], -1.0, rstd[:, :], ALU.mult, ALU.mult).then_inc(sem("ln_shift"), 1)
                for t in range(T // 2):
                    v.tensor_scalar(XN[:, t, :], X[:, t, :], mv[:, t, 0:1], rstd[:, t:t + 1], ALU.subtract, ALU.mult)\
                        .then_inc(sem("ln_x"), 1)
                if lnk is None:
                    dve.wait_ge(sem("ln_x"), 4 * (k + 1))
                    dve.wait_ge(sem("ln_x_act"), 4 * (k + 1))
                    return
                if meanwhile:
                    meanwhile()
                for kk in range(KD):
                    dve.wait_ge(sem("ln_T"), 4 * lnk + 3 + kk)
                    v.tensor_copy(XT[:, kk, 512:1024], PB[2 + kk][:, :]).then_inc(sem("xt_dve"), 1)

            def context():
                dve.wait_ge(sem("consts_loaded"), 16 * 11)
                bc = lambda ap: ap.unsqueeze(1).to_broadcast([P, B, 2, ap.shape[-1]])
                c4 = ctok[:, :, :].rearrange("p (b s) c -> p b s c", b=B)
                k1 = kt1.rearrange("p (b s) c -> p b s c", b=B)
                k2 = kt2.rearrange("p (b s) c -> p b s c", b=B)
                v.tensor_tensor(k1, c4, bc(ropek[:, 0, :, :]), ALU.mult)
                v.tensor_tensor(k2[:, :, :, 0:32], c4[:, :, :, 32:64], bc(ropek[:, 1, :, 0:32]), ALU.mult)
                link(v.tensor_tensor(k2[:, :, :, 32:64], c4[:, :, :, 0:32], bc(ropek[:, 1, :, 32:64]), ALU.mult))
                v.tensor_tensor(kvdup[:, :, 0, :], kt1, kt2, ALU.add)
                v.tensor_tensor(kvdup[:, :, 1, :], kt1, kt2, ALU.add).then_inc(sem("kvr_ready"), 1)
                dve.wait_ge(sem("kv_done"), 1)
                v.tensor_copy(kv0, PB[6][:, 0:T * C].rearrange("p (t c) -> p t c", t=T)).then_inc(sem("kv_copied"), 1)
                dve.wait_ge(sem("n2_done"), 1)
                v.tensor_copy(n2, PB[7][0:C, 0:C]).then_inc(sem("n2_copied"), 1)

            def l0_attention():
                dve.wait_ge(sem("x_loaded"), 16)
                normalize(0, 0, context)
                v.tensor_tensor(values[:, :, 0:C], kt1, kt2, ALU.add)
                for n in range(2):
                    n5 = slice(n * 512, n * 512 + 512)
                    dve.wait_ge(sem("keys_high"), n + 1)
                    v.tensor_tensor(keys[:, 1, n5], PB[6 + n][:, :], keys[:, 0, n5].bitcast(F32), ALU.subtract).then_inc(sem("keys_low"), 1)
                for b in range(B):
                    dve.wait_ge(sem("l0_sim"), b + 1)
                    for s in range(2):
                        v.bn_stats(st6[:, 2 * b + s, :], PB[b][:, s * S:(s + 1) * S]).then_inc(sem("l0_stats"), 1)
                for t in range(T):
                    dve.wait_ge(sem("l0_stats"), t + 1)
                    last = v.bn_aggr(mv[:, t, :], st6[:, t, :])
                last.then_inc(sem("l0_stat"), 1)
                dve.wait_ge(sem("l0_std"), 1)
                link(v.reciprocal(rstd[:, :], rstd[:, :]))
                for t in range(T):
                    last = v.tensor_scalar(XN[:, t, :], PB[t // 2][:, (t % 2) * S:(t % 2 + 1) * S], mv[:, t, 0:1],
                                           rstd[:, t:t + 1], ALU.subtract, ALU.mult)
                link(last)
                g4 = gam.unsqueeze(1).to_broadcast([P, 4, D])
                b4 = bet.unsqueeze(1).to_broadcast([P, 4, D])
                for n in range(2):
                    some = slice(4 * n, 4 * n + 4)
                    link(v.tensor_tensor(XN[:, some, :], XN[:, some, :], g4, ALU.mult))
                    link(v.tensor_tensor(XN[:, some, :], XN[:, some, :], b4, ALU.add))
                    v.tensor_reduce(sc8[:, 0, some], XN[:, some, :], AX.X, ALU.max, negate=True).then_inc(sem("l0_max"), 1)
                for t in range(T):
                    if t % 4 == 0:
                        dve.wait_ge(sem("l0_exp"), t // 4 + 1)
                        link(v.reciprocal(sc8[:, 2, t:t + 4], sc8[:, 1, t:t + 4]))
                    last = v.scalar_tensor_tensor(X[:, t, :], XN[:, t, :], sc8[:, 2, t:t + 1], X[:, t, :], ALU.mult, ALU.add)
                done(last)

            def scores(f):
                lg = LOGITS[f][:, 0:T * EX].rearrange("p (t e) -> p t e", t=T)
                over = lambda col: col.unsqueeze(2).to_broadcast([P, T, E])
                dve.wait_ge(sem("logits"), f + 1)
                link(v.tensor_reduce(sc8[:, 0, :], lg[:, :, 0:E], AX.X, ALU.max))
                v.tensor_tensor(pm[:, :, 0:E], lg[:, :, 0:E], over(sc8[:, 0, :]), ALU.subtract)
                v.tensor_scalar(pm[:, :, E:EX], lg[:, :, E:EX], -1.0, None, ALU.mult).then_inc(sem("logits_shifted"), 1)
                dve.wait_ge(sem("logits_exp"), f + 1)
                v.tensor_scalar(pm[:, :, E:EX], pr[:, :, E:EX], 1.0, None, ALU.add)
                link(v.tensor_reduce(sc8[:, 0, :], pr[:, :, 0:E], AX.X, ALU.add))
                link(v.reciprocal(sc8[:, 1, :], sc8[:, 0, :]))
                link(v.tensor_tensor(pk[:, :, :], pr[:, :, 0:E], over(sc8[:, 1, :]), ALU.mult))
                for t in range(T):
                    last = v.max(top8[:, t, :], pk[:, t, :])
                link(last)
                for t in range(T):
                    last = v.max_index(idx8[:, t, :], top8[:, t, :], pk[:, t, :])
                link(last)
                link(v.tensor_copy(idf[:, :, :], idx8[:, :, :]))
                dve.wait_ge(sem("router_loaded"), 64)
                io = iote[:, :].unsqueeze(1).to_broadcast([P, T, E])
                link(v.tensor_tensor(pm[:, :, 0:E], io, over(idf[:, :, 0]), ALU.is_equal))
                for c in range(1, TOPK):
                    link(v.tensor_tensor(pq[:, :, :], io, over(idf[:, :, c]), ALU.is_equal))
                    link(v.tensor_tensor(pm[:, :, 0:E], pm[:, :, 0:E], pq[:, :, :], ALU.add))
                link(v.tensor_tensor(pr[:, :, 0:E], pm[:, :, 0:E], pk[:, :, :], ALU.mult))
                if f == 1:
                    link(v.tensor_reduce(sc8[:, 0, :], pr[:, :, 0:E], AX.X, ALU.add))
                    link(v.tensor_scalar(sc8[:, 0, :], sc8[:, 0, :], 1e-9, None, ALU.max))
                    link(v.reciprocal(sc8[:, 1, :], sc8[:, 0, :]))
                    link(v.tensor_tensor(pr[:, :, 0:E], pr[:, :, 0:E], over(sc8[:, 1, :]), ALU.mult))
                link(v.reciprocal(pr[:, :, E:EX], pm[:, :, E:EX]))
                link(v.tensor_copy(scp[:, :, 0, :], pr))
                link(v.tensor_tensor(pr, pr, scp[:, :, 0, :], ALU.subtract))
                link(v.tensor_copy(scp[:, :, 1, :], pr))
                link(v.tensor_tensor(pr, pr, scp[:, :, 1, :], ALU.subtract))
                v.tensor_copy(scp[:, :, 2, :], pr).then_inc(sem("scores_split"), 1)
                dve.wait_ge(sem("scoresT"), f + 1)
                v.tensor_copy(SCT, PB[5][0:3 * EX, :].bitcast(BF16)).then_inc(sem("scoresT_copied"), 1)

            KEEP_WORK = ["load"] + ["eight"] * ((KEEP - 1) // 8) + ["keep"]
            PER_TILE = 1 + 2 * ((KEEP - 1) // 8) + 2

            def keep_neighbours(t, slot, slots, work, best):
                row = bass.ds(t, 1) if not isinstance(t, int) else slice(t, t + 1)
                spacer = lambda: None if isinstance(t, int) else v.tensor_copy(small[:, 9:10], small[:, 0:1])
                n = len(KEEP_WORK)
                for item in KEEP_WORK[n * slot // slots:n * (slot + 1) // slots]:
                    if item == "load":
                        link(v.tensor_copy(work.unsqueeze(1), SIM[:, row, :]))
                        continue
                    spacer()
                    link(v.max(best, work))
                    if item == "eight":
                        spacer()
                        link(v.match_replace(work, best, work, -BIG))
                    else:
                        last_kept = (KEEP - 1) % 8
                        link(v.scalar_tensor_tensor(A[:, row, :], SIM[:, row, :], best[:, last_kept:last_kept + 1], A[:, row, :],
                                                    ALU.is_ge, ALU.mult))

            def ffn(f, stage, lnk):
                normalize(stage, lnk)
                scores(f)
                base = f * 8 * LOOP
                if f == 0:
                    dve.wait_ge(sem("sim_sigmoid"), 1)

                def low(n, u):
                    dve.wait_ge(sem("h_high"), n + 1)
                    v.tensor_tensor(HTr[:, 1, u % 2, :], tmu[:, u % 2, :], HTr[:, 0, u % 2, :].bitcast(F32), ALU.subtract)\
                        .then_inc(sem("h_low"), 1)

                def unit(i, u):
                    n = i * 8 + (u + base)
                    dve.wait_ge(sem("silu_done"), n + 1)
                    dve.wait_ge(sem("up_done"), n + 1)
                    v.tensor_tensor(tmu[:, u % 2, :], sil[:, u % 2, :], PB[2 + u % 2][:, :], ALU.mult).then_inc(sem("t_done"), 1)
                    if f == 0:
                        keep_neighbours(i, 2 * u, 16, twork, tmax)
                    dve.wait_ge(sem("t_done"), n + 1)
                    dve.wait_ge(sem("spread_done"), n + 1)
                    v.tensor_tensor(tmu[:, u % 2, :], tmu[:, u % 2, :], PB[u % 2][:, :], ALU.mult).then_inc(sem("h_done"), 1)
                    if f == 0:
                        keep_neighbours(i, 2 * u + 1, 16, twork, tmax)
                    low(n, u)

                for u in range(8):
                    unit(0, u)
                with dve.Fori(1, LOOP) as i:
                    if f == 0:
                        link.enter(i, 1, PER_TILE)
                    for u in range(8):
                        unit(i, u)
                if f == 0:
                    link.leave(LOOP - 1)
                dve.wait_ge(sem("down_done"), 8 * LOOP * (f + 1))
                for q in range(4):
                    xs = X[:, 2 * q:2 * q + 2, :]
                    last = v.tensor_tensor(xs, xs, PB[4 + q][:, :].rearrange("p (s d) -> p s d", s=2), ALU.add)
                done(last)

            def attention(l, stage_, lnk):
                normalize(stage_, lnk)
                if l == 0:
                    dve.wait_ge(sem("rope_loaded"), 32)

                def at(name, value):
                    if not isinstance(value, int) or value > 0:
                        dve.wait_ge(sem(name), value)

                def step(b, h):
                    hb, pb = b * H + l * B * H, b * 8 + l * B * 8
                    inside = lambda m: not isinstance(b, int) or 0 <= b * H + m < B * H
                    m = h - 2
                    if l == 1 and inside(m):
                        at("pt_done", hb + (m + 1))
                        at("pv_done", hb + (m - 1))
                        v.tensor_copy(PT[:, m % 2, :, :], PB[3 + m % 2][:, :].rearrange("p (l s) -> p l s", l=2)).then_inc(sem("pt_copied"), 1)
                    m = h + 4
                    if l == 0 and inside(m):
                        at("qbig_done", hb + (m + 1))
                        at("rope_done", hb + (m - 1))
                        v.tensor_tensor(r1[:, m % 2, :], PB[0][0:CH, :], cosq, ALU.mult)
                        v.tensor_tensor(r2[:, m % 2, :], PB[0][0:CH, :], sinq, ALU.mult).then_inc(sem("rope_read"), 1)
                    if inside(h):
                        at("score_done", hb + (h + 1))
                        at("exp_done", hb + (h - 3))
                        v.tensor_reduce(nmx[:, h % 4, :], PB[1 + h % 2][:, :].rearrange("p (s l) -> p s l", s=2), AX.X, ALU.max,
                                        negate=True).then_inc(sem("max_done"), 1)
                    if h % 2 == 0 and inside(h - 4):
                        m = (h - 4) // 2
                        at("pv_done", hb + (2 * m + 2))
                        at("cct_done", pb + (m - 1))
                        o4 = PB[5][:, 0:4 * VW].rearrange("p (q c) -> p q c", q=4)
                        v.reciprocal(rin[:, m % 2, :], o4[:, :, C]).then_inc(sem("rin_done"), 1)
                        dve.wait_ge(sem("rin_done"), pb + (m + 1))
                        v.tensor_tensor(CC[:, m % 2, :, :].rearrange("p s (h c) -> p h s c", h=2),
                                        o4[:, :, 0:C].rearrange("p (h s) c -> p h s c", h=2),
                                        rin[:, m % 2, :].rearrange("p (h s) -> p h s", h=2).unsqueeze(3).to_broadcast([P, 2, 2, C]),
                                        ALU.mult).then_inc(sem("cc_done"), 1)
                    ahead = 1 + l
                    if (h + ahead) % 2 == 0 and inside(h + ahead):
                        m = (h + ahead) // 2
                        at("q_high", pb + (m + 1))
                        src = PB[4] if l == 0 else PB[0]
                        for e in range(2):
                            own, other = slice(e * C, e * C + C), slice((1 - e) * C, (1 - e) * C + C)
                            last = v.tensor_tensor(Q2[other, 2 * m % 4 + e, :], src[own, 0:S], Q2[own, 2 * m % 4 + e, :].bitcast(F32), ALU.subtract)
                        last.then_inc(sem("q_low"), 1)
                    if (h - 6) % H == 0 and inside(h - 7):
                        bb = b + (h - 7) // H
                        at("y_done", pb + 8 * ((h - 6) // H))
                        xs = X[:, 2 * bb:2 * bb + 2, :] if isinstance(b, int) else X[:, bass.ds(bb * 2, 2), :]
                        v.tensor_tensor(xs, xs, PB[7][:, :].rearrange("p (s d) -> p s d", s=2), ALU.add).then_inc(sem("y_added"), 1)

                for h in range(-4, H):
                    step(0, h)
                    if l == 0 and h >= 0:
                        keep_neighbours(T - 1, h, H, SIM[:, T - 2, :], sc8[:, 0, :])
                if l == 0:
                    v.tensor_copy(small[:, 2:3], small[:, 0:1]).then_inc(sem("a_kept"), 1)
                with dve.Fori(1, B - 1) as b:
                    for h in range(H):
                        step(b, h)
                for h in range(H + 7):
                    step(B - 1, h)
                    if l == 0 and 2 <= h < 11:
                        m, part = divmod(h - 2, 3)
                        w = rF[:, m, :]
                        if part == 0:
                            dve.wait_ge(sem("winv_ready"), 1)
                            v.tensor_scalar(w, w, winv[:, m:m + 1], -1.0, ALU.mult, ALU.max).then_inc(sem("wq_part"), 1)
                        elif part == 1:
                            dve.wait_ge(sem("wq_part"), 2 * m + 1)
                            v.tensor_scalar(w, w, 1.0, RNE, ALU.min, ALU.add).then_inc(sem("wq_part"), 1)
                        else:
                            dve.wait_ge(sem("wq_part"), 2 * m + 2)
                            v.tensor_scalar(WB[:, m, :], w, RNE, None, ALU.subtract).then_inc(sem("wq_ready"), 1)
                dve.wait_ge(sem("y_added"), B * (l + 1))
                done(v.tensor_copy(small[:, 8:9], small[:, 0:1]))

            def quantized():
                normalize(3, None)
                link(v.tensor_reduce(amax, XN[:, :, :], AX.X, ALU.max, apply_absolute_value=True))
                link(v.tensor_scalar(xs8, amax, 1.0 / 127.0, 1e-5, ALU.mult, ALU.add))
                link(v.reciprocal(xr8, xs8))
                for t in range(T):
                    last = v.tensor_scalar(qt[:, t * D:(t + 1) * D], XN[:, t, :], xr8[:, t:t + 1], -128.0, ALU.mult, ALU.max)
                link(last)
                link(v.tensor_scalar(qt, qt, 127.0, RNE, ALU.min, ALU.add))
                v.tensor_scalar(XQ.rearrange("p t d -> p (t d)"), qt, RNE, None, ALU.subtract).then_inc(sem("xq_ready"), 1)
                dve.wait_ge(sem("w_scales"), 1)
                v.tensor_copy(hs[:, 0:1], amax[:, 0:1]).then_inc(sem("q_bank_free"), 1)
                v.tensor_scalar(sg8, xs8, wsum[:, 0:1], None, ALU.mult).then_inc(sem("q_scale"), 1)
                link(v.tensor_scalar(su8, xs8, wsum[:, 1:2], None, ALU.mult))
                dve.wait_ge(sem("xqT_done"), 2)
                v.tensor_copy(XQT[:, 1, :], PB[1][:, :].bitcast(BF16)).then_inc(sem("xqT_copied"), 1)

                def col(ap, t):
                    return ap[:, t:t + 1] if isinstance(t, int) else ap[:, bass.ds(t, 1)]

                def hidden(t):
                    first = isinstance(t, int) and t == 0
                    if not first:
                        dve.wait_ge(sem("q_quant"), t)
                    for c in range(2):
                        dve.wait_ge(sem("q_silu"), t * 2 + (c + 1))
                        dve.wait_ge(sem("q_gu"), t * 4 + (3 + c))
                        last = v.scalar_tensor_tensor(hq[:, c * 512:(c + 1) * 512], PB[2 + c][:, :], col(su8, t), silq[:, c * 512:(c + 1) * 512],
                                                      ALU.mult, ALU.mult)
                        last.then_inc(sem("q_h"), 1)
                    dve.wait_ge(sem("q_h"), t * 2 + 2)
                    link(v.tensor_reduce(hs[:, 0:1], hq, AX.X, ALU.max, apply_absolute_value=True))
                    if not isinstance(t, int):
                        add(t, 2).then_inc(sem("q_bank_free"), 1)
                    link(v.tensor_scalar(hs[:, 1:2], hs[:, 0:1], 1.0 / 127.0, 1e-5, ALU.mult, ALU.add))
                    v.tensor_scalar(col(ys8, t), hs[:, 1:2], wsum[:, 2:3], None, ALU.mult)
                    link(v.reciprocal(hs[:, 2:3], hs[:, 1:2]))
                    link(v.tensor_scalar(hq, hq, hs[:, 2:3], -128.0, ALU.mult, ALU.max))
                    link(v.tensor_scalar(hq, hq, 127.0, RNE, ALU.min, ALU.add))
                    if not first:
                        dve.wait_ge(sem("q_T"), t)
                    v.tensor_scalar(hqb, hq, RNE, None, ALU.subtract).then_inc(sem("q_quant"), 1)

                def add(t, before):
                    dve.wait_ge(sem("q_down"), t + 1 - before)
                    xs = X[:, t - before:t - before + 1, :] if isinstance(t, int) else X[:, bass.ds(t - before, 1), :]
                    return v.scalar_tensor_tensor(xs, PB[5][:, 0:D].unsqueeze(1), col(ys8, t - before), xs, ALU.mult, ALU.add)

                hidden(0)
                hidden(1)
                with dve.Fori(2, T) as t:
                    link.enter(t, 2, 5)
                    hidden(t)
                link.leave(T - 2)
                add(T, 2).then_inc(sem("q_bank_free"), 1)
                for b in range(B):
                    dve.wait_ge(sem("aT_done"), b + 1)
                    ab = A[:, 2 * b:2 * b + 2, :]
                    v.tensor_tensor(ab, ab, PB[b][:, :].rearrange("p (s l) -> p s l", s=2), ALU.add).then_inc(sem("a_summed"), 1)
                done(add(T, 1))

            def adjacency():
                dve.wait_ge(sem("g_ready"), 1)
                v.tensor_scalar(small[:, 4:5], small[:, 3:4], -1.0, 1.0, ALU.mult, ALU.add)
                normalize(4, None)
                dve.wait_ge(sem("ax_summed"), 1)
                done(v.scalar_tensor_tensor(X[:, :, :], XN[:, :, :], small[:, 4:5], A[:, :, :], ALU.mult, ALU.add))

            def small_experts(lnk):
                normalize(5, lnk)
                lg = PB[4][:, 0:T * E2].rearrange("p (t e) -> p t e", t=T)
                over = lambda col: col.unsqueeze(2).to_broadcast([P, T, E2])
                e8 = slice(0, E2)
                dve.wait_ge(sem("logits2"), 1)
                link(v.tensor_reduce(sc8[:, 0, :], lg, AX.X, ALU.max))
                v.tensor_tensor(pm[:, :, e8], lg, over(sc8[:, 0, :]), ALU.subtract).then_inc(sem("logits2_shifted"), 1)
                dve.wait_ge(sem("logits2_exp"), 1)
                link(v.tensor_reduce(sc8[:, 0, :], pr[:, :, e8], AX.X, ALU.add))
                link(v.reciprocal(sc8[:, 1, :], sc8[:, 0, :]))
                link(v.tensor_tensor(pk[:, :, e8], pr[:, :, e8], over(sc8[:, 1, :]), ALU.mult))
                for t in range(T):
                    last = v.max(top8[:, t, :], pk[:, t, e8])
                link(last)
                for t in range(T):
                    last = v.max_index(idx8[:, t, :], top8[:, t, :], pk[:, t, e8])
                link(last)
                link(v.tensor_copy(idf[:, :, :], idx8[:, :, :]))
                io = iote[:, e8].unsqueeze(1).to_broadcast([P, T, E2])
                link(v.tensor_tensor(pm[:, :, e8], io, over(idf[:, :, 0]), ALU.is_equal))
                link(v.tensor_tensor(pq[:, :, e8], io, over(idf[:, :, 1]), ALU.is_equal))
                link(v.tensor_tensor(pm[:, :, e8], pm[:, :, e8], pq[:, :, e8], ALU.add))
                link(v.tensor_tensor(pr[:, :, e8], pm[:, :, e8], pk[:, :, e8], ALU.mult))
                dve.wait_ge(sem("silu2_done"), 2)
                a4 = a2.rearrange("p t (e i) -> p t e i", e=E2)
                v.tensor_tensor(a4, a4, pr[:, :, e8].unsqueeze(3).to_broadcast([P, T, E2, IE2]), ALU.mult).then_inc(sem("a2_ready"), 1)
                dve.wait_ge(sem("a2T_done"), 2)
                v.tensor_copy(a2T[:, 512:1024], PB[1][:, :]).then_inc(sem("a2T_copied"), 1)
                for q in range(4):
                    dve.wait_ge(sem("y2_done"), q + 1)
                    xs = X[:, 2 * q:2 * q + 2, :]
                    last = v.tensor_tensor(xs, xs, PB[4 + q][:, :].rearrange("p (s d) -> p s d", s=2), ALU.add)
                done(last)

            v.memset(epsc[:, 0:1], 1e-5).then_inc(sem("eps_set"), 1)
            v.memset(epsc[:, 1:2], 1e-6).then_inc(sem("eps_set"), 1)
            v.memset(ctxT[C:C + 1, :], 1.0).then_inc(sem("ctx_ones"), 1)
            v.memset(values[:, :, C:VW], 1.0)
            l0_attention()
            ffn(0, 1, 1)
            attention(0, 2, 2)
            quantized()
            adjacency()
            small_experts(3)
            attention(1, 6, 4)
            ffn(1, 7, 5)
            v.tensor_copy(small[:, 2:3], small[:, 0:1]).then_inc(sem("x_final"), 1)

        @block.scalar
        def _(act):
            sc = nc.scalar

            def context():
                for n in range(2):
                    act.wait_ge(sem("kvT_done"), n + 1)
                    sc.copy(kvT0[:, n * 512:(n + 1) * 512], PB[4 + n][0:C, :]).then_inc(sem("kvT_copied"), 1)

            def normalize(k, lnk, meanwhile=None):
                act.wait_ge(sem("ln_stat"), k + 1)
                sc.activation(rstd[:, :], mv[:, :, 1], ACT.Sqrt, bias=epsc[:, 0:1]).then_inc(sem("ln_std"), 1)
                act.wait_ge(sem("ln_shift"), k + 1)
                for t in range(T // 2, T):
                    sc.activation(XN[:, t, :], X[:, t, :], ACT.Identity, scale=rstd[:, t:t + 1], bias=nmr[:, t:t + 1])\
                        .then_inc(sem("ln_x_act"), 1)
                if meanwhile:
                    meanwhile()
                for kk in range(KD if lnk is not None else 0):
                    act.wait_ge(sem("ln_T"), 4 * lnk + 1 + kk)
                    sc.copy(XT[:, kk, 0:512], PB[kk][:, :]).then_inc(sem("xt_act"), 1)

            def fuse(l, some):
                for n in some:
                    act.wait_ge(sem("fuse_done"), (0, 24)[l] + n + 1)
                    fuse_copy(l, n, sc.copy).then_inc(sem("fuse_copied"), 1)

            def l0_attention():
                normalize(0, 0, context)
                for n in range(2):
                    act.wait_ge(sem("l0_out"), n + 1)
                    sc.activation(outT[:, n * 512:(n + 1) * 512], PB[4 + n][0:C, :], ACT.Copy, scale=D ** -0.5).then_inc(sem("l0_out_copied"), 1)
                for n in range(2):
                    act.wait_ge(sem("kvrT_done"), n + 1)
                    sc.copy(keys[:, 0, n * 512:(n + 1) * 512], PB[6 + n][:, :]).then_inc(sem("keys_high"), 1)
                for n in range(2):
                    act.wait_ge(sem("uT_done"), n + 1)
                    sc.copy(uT[:, n * 512:(n + 1) * 512], PB[4 + n][0:C, :]).then_inc(sem("uT_copied"), 1)
                act.wait_ge(sem("l0_stat"), 1)
                sc.activation(rstd[:, :], mv[:, :, 1], ACT.Sqrt, bias=epsc[:, 1:2]).then_inc(sem("l0_std"), 1)
                for b in range(B):
                    act.wait_ge(sem("sim_done"), b + 1)
                    sc.copy(SIM[:, 2 * b:2 * b + 2, :], PB[4 + b][:, :].rearrange("p (s l) -> p s l", s=2)).then_inc(sem("sim_copied"), 1)
                act.wait_ge(sem("sim_copied"), 4)
                sc.activation(A[:, :, :], SIM[:, :, :], ACT.Sigmoid, scale=1.0 / 16.0).then_inc(sem("sim_sigmoid"), 1)
                act.wait_ge(sem("consts_loaded"), 16 * 11)
                sc.activation(small[:, 3:4], small[:, 0:1], ACT.Sigmoid).then_inc(sem("g_ready"), 1)
                for t in range(T):
                    if t % 4 == 0:
                        fuse(0, range(t // 4 * 3, t // 4 * 3 + 3))
                        act.wait_ge(sem("l0_max"), t // 4 + 1)
                    last = sc.activation(XN[:, t, :], XN[:, t, :], ACT.Exp, bias=sc8[:, 0, t:t + 1], accum_out=sc8[:, 1, t:t + 1])
                    if t % 4 == 3:
                        last.then_inc(sem("l0_exp"), 1)
                fuse(0, range(6, EARLY))

            def ffn(f, stage, lnk):
                normalize(stage, lnk)
                base = f * 8 * LOOP
                act.wait_ge(sem("xt_dve"), 2 * (lnk + 1))
                act.wait_ge(sem("xt_act"), 2 * (lnk + 1))
                for kk in range(KD):
                    for tg in range(2):
                        n5 = slice(tg * 512, tg * 512 + 512)
                        sc.copy(XTr[:, 0, kk, n5], XT[:, kk, n5]).then_inc(sem("xtr_high"), 1)

                def split(i, j, down):
                    n = i * 4 + (j + base // 2)
                    ahead = isinstance(i, int) and i == 0 and j < 2
                    if down:
                        if not ahead:
                            act.wait_ge(sem("down_done"), i * 8 + (2 * j - 2 + base))
                        sc.copy(WDr[:, 0, j % 2, :], ring[:, j // 2 % 2, j % 2 * 768 + 512:j % 2 * 768 + 768]).then_inc(sem("wd_high"), 1)
                    else:
                        if j % 2 == 0:
                            act.wait_ge(sem(f"w_full{j // 2 % 2}"), (i + j // 4) * 16 + (16 + 16 * LOOP * f))
                        if not ahead:
                            act.wait_ge(sem("up_done"), i * 8 + (2 * j - 2 + base))
                        sc.copy(WGr[:, 0, j % 2, :], ring[:, j // 2 % 2, j % 2 * 768:j % 2 * 768 + 512]).then_inc(sem("wg_high"), 1)

                def high(i, u):
                    n = i * 8 + (u + base)
                    act.wait_ge(sem("h_done"), n + 1)
                    if not (isinstance(i, int) and i == 0 and u < 2):
                        act.wait_ge(sem("down_done"), n - 1)
                    sc.copy(HTr[:, 0, u % 2, :], tmu[:, u % 2, :]).then_inc(sem("h_high"), 1)

                def unit(i, u):
                    n = i * 8 + (u + base)
                    act.wait_ge(sem("gate_done"), n + 1)
                    if not (isinstance(i, int) and i == 0 and u < 2):
                        act.wait_ge(sem("t_done"), n - 1)
                    sc.activation(sil[:, u % 2, :], PB[u % 2][:, :], ACT.Silu).then_inc(sem("silu_done"), 1)
                    if u % 2 == 0 and not (isinstance(i, int) and i == LOOP - 1 and u == 6):
                        split(i, u // 2 + 1, False)
                    if u % 2 == 0:
                        split(i, u // 2, True)
                    high(i, u)

                split(0, 0, False)
                act.wait_ge(sem("logits_shifted"), f + 1)
                sc.activation(pr[:, :, :], pm[:, :, :], ACT.Exp).then_inc(sem("logits_exp"), 1)
                if f == 0:
                    fuse(0, range(EARLY, 24))
                for u in range(8):
                    unit(0, u)
                with act.Fori(1, LOOP - 1) as i:
                    for u in range(8):
                        unit(i, u)
                for u in range(8):
                    unit(LOOP - 1, u)

            def attention(l, stage, lnk):
                normalize(stage, lnk)

                def at(name, value):
                    if not isinstance(value, int) or value > 0:
                        act.wait_ge(sem(name), value)

                def step(b, h):
                    hb, pb = b * H + l * B * H, b * 8 + l * B * 8
                    inside = lambda m: not isinstance(b, int) or 0 <= b * H + m < B * H
                    m = h - 2
                    if l == 0 and inside(m):
                        at("pt_done", hb + (m + 1))
                        at("pv_done", hb + (m - 1))
                        sc.copy(PT[:, m % 2, :, :], PB[3][:, :].rearrange("p (l s) -> p l s", l=2)).then_inc(sem("pt_copied"), 1)
                    ahead = 1 + l
                    if (h + ahead) % 2 == 0 and inside(h + ahead):
                        m = (h + ahead) // 2
                        at("qc_done", (hb + (2 * m + 2)) if l == 0 else (pb + (m + 1 + B * 8)))
                        at("score_done", hb + (2 * m - 2))
                        src = PB[4] if l == 0 else PB[0]
                        for e in range(2):
                            own = slice(e * C, e * C + C)
                            last = sc.copy(Q2[own, 2 * m % 4 + e, :], src[own, 0:S])
                        last.then_inc(sem("q_high"), 1)
                    if inside(h):
                        at("max_done", hb + (h + 1))
                        at("pt_done", hb + (h - 3))
                        for s in range(2):
                            last = sc.activation(Ex[:, h % 4, s, :], PB[1 + h % 2][:, s * S:(s + 1) * S], ACT.Exp, bias=nmx[:, h % 4, s:s + 1])
                        last.then_inc(sem("exp_done"), 1)
                    if h % 2 and inside(h - 5):
                        m = (h - 5) // 2
                        at("cct_done", pb + (m + 1))
                        at("cct_low", pb + (m - 1))
                        at("y_done", pb + (m - 1))
                        sc.copy(CCT[:, m % 2, :], PB[6][:, 0:S])
                        sc.copy(CCr[:, m % 2, 0, :], PB[6][:, 0:S]).then_inc(sem("cct_copied"), 1)

                for n in range(2):
                    sc.copy(PFr[:, 0, 4 * n:4 * n + 4, :], PF[:, 4 * n:4 * n + 4, :]).then_inc(sem("pf_high"), 1)
                for h in range(-4, H):
                    step(0, h)
                    if l == 0 and h in (9, 11, 13):
                        m = (h - 9) // 2
                        act.wait_ge(sem("w1ffn_loaded"), 16)
                        sc.activation(WB[:, m, :], rF[:, m, :], ACT.Abs, accum_out=wsum[:, m:m + 1]).then_inc(sem("w_abs"), 1)
                with act.Fori(1, B - 1) as b:
                    for h in range(H):
                        step(b, h)
                for h in range(H + 5):
                    step(B - 1, h)
                    if l == 0 and h == 2:
                        act.wait_ge(sem("g_ready"), 1)
                        sc.activation(small[:, 5:6], small[:, 3:4], ACT.Copy, scale=0.5).then_inc(sem("half_g"), 1)
                        act.wait_ge(sem("half_g"), 1)
                        act.wait_ge(sem("a_kept"), 1)
                        sc.activation(A[:, :, :], A[:, :, :], ACT.Copy, scale=small[:, 5:6]).then_inc(sem("a_scaled"), 1)

            def quantized():
                normalize(3, None)
                act.wait_ge(sem("xqT_done"), 1)
                sc.copy(XQT[:, 0, :], PB[0][:, :].bitcast(BF16)).then_inc(sem("xqT_copied"), 1)

                act.wait_ge(sem("q_scale"), 1)
                for t in range(T):
                    if t:
                        act.wait_ge(sem("q_h"), t * 2)
                    for c in range(2):
                        act.wait_ge(sem("q_gu"), t * 4 + (c + 1))
                        sc.activation(silq[:, c * 512:(c + 1) * 512], PB[c][:, :], ACT.Silu, scale=sg8[:, t:t + 1]).then_inc(sem("q_silu"), 1)
                    fuse(1, FUSE_SHARE[t][:-1])
                    if t:
                        act.wait_ge(sem("q_T"), t)
                        sc.copy(hqT, PB[4][:, :].bitcast(BF16)).then_inc(sem("q_Tcopied"), 1)
                    fuse(1, FUSE_SHARE[t][-1:])
                act.wait_ge(sem("q_T"), T)
                sc.copy(hqT, PB[4][:, :].bitcast(BF16)).then_inc(sem("q_Tcopied"), 1)

            def small_experts(lnk):
                normalize(5, lnk)
                act.wait_ge(sem("logits2_shifted"), 1)
                sc.activation(pr[:, :, 0:E2], pm[:, :, 0:E2], ACT.Exp).then_inc(sem("logits2_exp"), 1)
                for n in range(2):
                    act.wait_ge(sem("h2_done"), n + 1)
                    sc.activation(a2[:, 4 * n:4 * n + 4, :], PB[5 + n][:, :].rearrange("p (t n) -> p t n", t=4), ACT.Silu)\
                        .then_inc(sem("silu2_done"), 1)
                act.wait_ge(sem("a2T_done"), 1)
                sc.copy(a2T[:, 0:512], PB[0][:, :]).then_inc(sem("a2T_copied"), 1)

            act.wait_ge(sem("eps_set"), 2)
            l0_attention()
            ffn(0, 1, 1)
            attention(0, 2, 2)
            quantized()
            normalize(4, None)
            small_experts(3)
            attention(1, 6, 4)
            ffn(1, 7, 5)

        @block.gpsimd
        def _(pool):
            g = nc.gpsimd
            g.memset(neg1[:, :], -1.0).then_inc(sem("neg1_set"), 1)

            def ffn(f):
                base = f * 8 * LOOP
                for n in range(4):
                    kk, n5 = n // 2, slice(n % 2 * 512, n % 2 * 512 + 512)
                    pool.wait_ge(sem("xtr_high"), 4 * f + n + 1)
                    g.tensor_tensor(XTr[:, 1, kk, n5], XT[:, kk, n5], XTr[:, 0, kk, n5].bitcast(F32), ALU.subtract)\
                        .then_inc(sem("xtr_done"), 1)

                def split(i, j, down):
                    n = i * 4 + (j + base // 2)
                    lo, hi = (512, 768) if down else (0, 512)
                    dst, name = (WDr, "wd") if down else (WGr, "wg")
                    pool.wait_ge(sem(name + "_high"), n + 1)
                    g.tensor_tensor(dst[:, 1, j % 2, :], ring[:, j // 2 % 2, j % 2 * 768 + lo:j % 2 * 768 + hi], dst[:, 0, j % 2, :].bitcast(F32),
                                    ALU.subtract).then_inc(sem(name + "_low"), 1)

                def trip(i):
                    for j in range(4):
                        if not (isinstance(i, int) and i == LOOP - 1 and j == 3):
                            split(i, j + 1, False)
                        split(i, j, True)

                split(0, 0, False)
                trip(0)
                with pool.Fori(1, LOOP - 1) as i:
                    trip(i)
                trip(LOOP - 1)

            def attention(l):
                pool.wait_ge(sem("stage_done"), (2, 6)[l])

                def at(name, value):
                    if not isinstance(value, int) or value > 0:
                        pool.wait_ge(sem(name), value)

                def step(b, h):
                    hb, pb = b * H + l * B * H, b * 8 + l * B * 8
                    inside = lambda m: not isinstance(b, int) or 0 <= b * H + m < B * H
                    m = h + 4
                    if l == 0 and inside(m):
                        at("rope_read", hb + (m + 1))
                        at("qc_done", hb + (m - 1))
                        for half in range(2):
                            lo, hi = slice(half * S, half * S + S), slice((1 - half) * S, (1 - half) * S + S)
                            last = g.tensor_tensor(qr[:, m % 2, lo], r1[:, m % 2, lo], r2[:, m % 2, hi], ALU.add)
                        last.then_inc(sem("rope_done"), 1)
                    if h % 2 and inside(h - 5):
                        m = (h - 5) // 2
                        at("cct_copied", pb + (m + 1))
                        g.tensor_tensor(CCr[:, m % 2, 1, :], CCT[:, m % 2, :], CCr[:, m % 2, 0, :].bitcast(F32), ALU.subtract)\
                            .then_inc(sem("cct_low"), 1)

                for h in range(-4, H):
                    step(0, h)
                    if 0 <= h < 4:
                        n2 = slice(2 * h, 2 * h + 2)
                        pool.wait_ge(sem("pf_high"), 2 * l + h // 2 + 1)
                        g.tensor_tensor(PFr[:, 1, n2, :], PF[:, n2, :], PFr[:, 0, n2, :].bitcast(F32), ALU.subtract).then_inc(sem("pf_low"), 1)
                if l == 0:
                    weight_scales()
                with pool.Fori(1, B - 1) as b:
                    for h in range(H):
                        step(b, h)
                for h in range(H + 5):
                    step(B - 1, h)

            def weight_scales():
                pool.wait_ge(sem("w_abs"), 3)
                pool.wait_ge(sem("neg1_set"), 1)
                g.partition_all_reduce(wtot[:, :], wsum[:, :], P, bass.bass_isa.ReduceOp.add).then_inc(sem("pool_chain"), 1)
                pool.wait_ge(sem("pool_chain"), 1)
                g.tensor_scalar(wsum[:, :], wtot[:, :], 1.0 / (D * I1), 1e-5, ALU.mult, ALU.add).then_inc(sem("w_scales"), 1)
                pool.wait_ge(sem("w_scales"), 1)
                g.tensor_tensor(winv[:, :], wsum[:, :], neg1[:, :], ALU.pow).then_inc(sem("winv_ready"), 1)

            ffn(0)
            attention(0)
            pool.wait_ge(sem("a_summed"), B)
            pool.wait_ge(sem("stage_done"), 4)
            g.tensor_tensor(A[:, :, :], A[:, :, :], X[:, :, :], ALU.add).then_inc(sem("ax_summed"), 1)
            attention(1)
            ffn(1)


def bf16_of_01(ones):
    return np.where(ones > 0, 0x3F80, 0).astype(np.uint16)


def layouts(i):
    f = lambda n: np.asarray(i[n])
    c = np.ascontiguousarray
    two = lambda w: c(w.reshape(KD, P, w.shape[1]).transpose(1, 0, 2))
    flat2 = lambda w: two(w).reshape(P, -1)
    a = {"x": f("x"), "ctx": f("ctx_512"), "ctxT": c(f("ctx_512").reshape(TOK, C).T)}
    a["wkaug"] = c(np.concatenate([f("L0_xattn_W_k").T, f("L0_xattn_b_k")[None]], 0))
    a["gamma"], a["beta"] = f("L0_xattn_ln_gamma"), f("L0_xattn_ln_beta")
    a["graw"] = f("L2_xattn_gamma_raw").reshape(1)
    a["wq2"], a["wk2"] = f("L2_xattn_Wq"), f("L2_xattn_Wk")
    a["ident"] = np.eye(P, dtype=np.float32)
    a["identb"] = bf16_of_01(np.eye(P))
    a["iote"] = np.arange(E, dtype=np.float32)
    owner = np.concatenate([np.repeat(np.arange(E), FE), np.full(FS, E), np.full(FT * P - E * FE - FS, -1)])
    sel = (owner[None] == np.arange(EX)[:, None]).astype(np.float32)
    a["sel"] = bf16_of_01(np.concatenate([sel] * 3, 0))

    def groups(gate, up, down):
        pad = lambda w: np.concatenate([w, np.zeros((FT * P - w.shape[0], w.shape[1]), w.dtype)], 0)
        gu = [pad(w).reshape(NG, GRP, P, KD, P).transpose(0, 4, 1, 3, 2) for w in (gate, up)]
        dn = pad(down).reshape(NG, GRP, P, 1, D).transpose(0, 2, 1, 3, 4)
        flat = lambda w: w.reshape(NG, P, GRP, -1)
        return c(np.concatenate([flat(w) for w in gu + [dn]], 3).reshape(NG, P, -1))

    e2 = lambda w: w.reshape(E * FE, D)
    a["w0"] = groups(np.concatenate([e2(f("L0_ffn_w_gate")), f("L0_ffn_ws_gate")]),
                     np.concatenate([e2(f("L0_ffn_w_up")), f("L0_ffn_ws_up")]),
                     np.concatenate([e2(f("L0_ffn_w_down").transpose(0, 2, 1)), f("L0_ffn_ws_down").T]))
    a["w1"] = groups(np.concatenate([e2(f("L3_ffn_w_gate").transpose(0, 2, 1)), f("L3_ffn_sh_gate").T]),
                     np.concatenate([e2(f("L3_ffn_w_up").transpose(0, 2, 1)), f("L3_ffn_sh_up").T]),
                     np.concatenate([e2(f("L3_ffn_w_down")), f("L3_ffn_sh_down")]))
    a["router0"] = flat2(np.concatenate([f("L0_ffn_router_weight"), f("L0_ffn_w_shared_gate")], 0).T)
    a["router1"] = flat2(np.concatenate([f("L3_ffn_router_w").T, f("L3_ffn_sh_gate_w")], 1))

    for l, n in ((0, "L1"), (1, "L3")):
        g = lambda w: f(f"{n}_xattn_{w}")
        a[f"Wq{l}"] = c(g("Wq").reshape(H, HK, D).transpose(1, 0, 2))
        a[f"Wo{l}"] = c(g("Wo").reshape(D, H, HK).transpose(2, 1, 0))
        a[f"Kv{l}"] = c(g("w_kc_kv").transpose(1, 0, 2))
        a[f"Kr{l}"] = c(g("W_kr").transpose(2, 0, 1))
        a[f"Qr{l}"] = c(g("W_qr").transpose(2, 0, 1))
    a["Kq0"] = c(f("L1_xattn_w_kc_q").transpose(1, 0, 2))
    a["Kq1"] = c(f("L3_xattn_w_kc_q").reshape(H, HK, 2, CH).transpose(3, 2, 0, 1))
    a["w1ffn"] = c(np.stack([two(f("L1_ffn_w_gate").T).reshape(P, 2048), two(f("L1_ffn_w_up").T).reshape(P, 2048),
                             f("L1_ffn_w_down").T.reshape(8, P, D).transpose(1, 0, 2).reshape(P, 2048)], 1))
    a["router2"] = two(f("L2_ffn_router_w").T).reshape(P, KD * E2)
    a["w2d"] = two(f("L2_ffn_down_w").reshape(E2 * IE2, D).T)
    a["w2u"] = c(f("L2_ffn_up_w").transpose(0, 2, 1).reshape(E2 * IE2, D))

    def rope(length, dim):
        inv = (np.float32(1.0) / np.power(np.float32(10000.0), np.arange(0, dim, 2, dtype=np.float32) / np.float32(dim))).astype(np.float32)
        ang = np.arange(length, dtype=np.float32)[:, None] * inv[None]
        return np.repeat(np.sin(ang), 2, -1), np.repeat(np.cos(ang), 2, -1)

    sk, ck = rope(S, C)
    sk = np.concatenate([-sk[:, :C // 2], sk[:, C // 2:]], 1)
    a["ropek"] = c(np.stack([ck, sk]).reshape(2, 2, P, C).transpose(2, 0, 1, 3))
    sq, cq = rope(S, CQ)
    a["cosq"] = c(np.concatenate([cq[:, :CH].T, cq[:, CH:].T], 1))
    a["sinq"] = c(np.concatenate([sq[:, CH:].T, -sq[:, :CH].T], 1))
    return a


def kernel(**inputs):
    import concourse.bacc as bacc
    from concourse.bass_utils import run_bass_kernel_spmd as run

    nc = bacc.Bacc("TRN2", target_bir_lowering=False, num_devices=1)
    arrays, aps = {}, {}
    for name, v in layouts(inputs).items():
        arrays[f"in_{name}"] = v
        aps[name] = nc.dram_tensor(f"in_{name}", v.shape, mybir.dt.from_np(v.dtype), kind="ExternalInput").ap()
    out = nc.dram_tensor("out", (B, S, D), F32, kind="ExternalOutput").ap()
    build(nc, aps, out)
    r = run(nc, [arrays], core_ids=[0])
    return r.results[0]["out"]
```
